# Optimizing a Trainium2 kernel written in Bass

```python
import numpy as np
import jax
import jax.numpy as jnp

def _softmax(x, axis=-1):
    return jax.nn.softmax(x, axis=axis)

def _gelu(x):
    return jax.nn.gelu(x, approximate=True)

def _silu(x):
    return jax.nn.silu(x)

def _sigmoid(x):
    return jax.nn.sigmoid(x)

def _layernorm(x, axis=-1, eps=1e-05):
    m = jnp.mean(x, axis=axis, keepdims=True)
    v = jnp.var(x, axis=axis, keepdims=True)
    return (x - m) / jnp.sqrt(v + eps)

def _scatter_add(tgt, idx, src, axis=0):
    return tgt.at[idx].add(src)

def _segment_sum(src, seg, n):
    return jax.ops.segment_sum(src, seg, n)
kernel_name = 'mk_decoder_postln_d1_seqx_r4_4b4b1f'

def setup_inputs(seed: int=0):
    np.random.seed(seed)
    _w = jnp.asarray

    def _rec_inputs():
        import jax
        import jax.numpy as jnp
        _rk = jax.random.key(seed)
        x = 7.22e-05 + 1 * jax.random.normal(jax.random.fold_in(_rk, 1), (4, 512, 512), jnp.float32)
        _lenS = 512 - jax.random.randint(jax.random.fold_in(_rk, 7), (4,), 0, max(1, 512 // 4) + 1, jnp.int32)
        _lenS2 = 512 - jax.random.randint(jax.random.fold_in(_rk, 8), (4,), 0, max(1, 512 // 4) + 1, jnp.int32)
        _ctx_1024P = jax.random.normal(jax.random.fold_in(_rk, 11), (4, 16, 256), jnp.float32)
        _ctx_1024c = jax.random.dirichlet(jax.random.fold_in(_rk, 511), 0.3 * jnp.ones((16,), jnp.float32), (4, 512))
        _ctx_1024t = jnp.einsum('bsk,bkd->bsd', _ctx_1024c, _ctx_1024P)
        _ctx_1024t = _ctx_1024t * jax.lax.rsqrt(jnp.mean(jnp.square(_ctx_1024t)) + 1e-12) * 0.953939
        ctx_1024 = 2.81802e-05 + 1.00001 * (_ctx_1024t + 0.3 * jax.random.normal(jax.random.fold_in(_rk, 611), (4, 512, 256), jnp.float32))
        return (x, ctx_1024)
    x, ctx_1024 = _rec_inputs()

    def _L0_attn_setup():
        import jax, jax.numpy as jnp
        import numpy as np
        N_HEADS = 32
        WINDOW = 128

        def _sliding_window_attention(x, Wq, Wk, Wv, Wo, n_heads=N_HEADS, window=WINDOW):
            B, T, D = x.shape
            H, dk = (n_heads, D // n_heads)
            bs = window
            assert T % bs == 0
            nb = T // bs

            def heads(y):
                return y.reshape(B, T, H, dk).transpose(0, 2, 1, 3)
            q = heads(x @ Wq.T)
            k = heads(x @ Wk.T)
            v = heads(x @ Wv.T)
            qb = q.reshape(B, H, nb, bs, dk)
            zpad = jnp.zeros((B, H, bs, dk), dtype=x.dtype)
            kp = jnp.concatenate([zpad, k], axis=2).reshape(B, H, nb + 1, bs, dk)
            vp = jnp.concatenate([zpad, v], axis=2).reshape(B, H, nb + 1, bs, dk)
            kw = jnp.concatenate([kp[:, :, :-1], kp[:, :, 1:]], axis=3)
            vw = jnp.concatenate([vp[:, :, :-1], vp[:, :, 1:]], axis=3)
            scale = 1.0 / np.sqrt(dk).astype(np.float32)
            scores = jnp.einsum('bhnrd,bhncd->bhnrc', qb, kw) * scale
            i = jnp.arange(nb)[:, None, None]
            r = jnp.arange(bs)[None, :, None]
            c = jnp.arange(2 * bs)[None, None, :]
            dist = bs + r - c
            key_global = i * bs - bs + c
            valid = (dist >= 0) & (dist <= window) & (key_global >= 0)
            scores = jnp.where(valid[None, None], scores, jnp.finfo(scores.dtype).min)
            probs = jax.nn.softmax(scores, axis=-1)
            out = jnp.einsum('bhnrc,bhncd->bhnrd', probs, vw)
            out = out.reshape(B, H, T, dk).transpose(0, 2, 1, 3).reshape(B, T, D)
            return out @ Wo.T
        key = jax.random.key(seed)
        ks = jax.random.split(key, 5)
        B, T, D = (2, 1024, 512)
        w_std = 0.02
        return {'x': jax.random.normal(ks[0], (B, T, D), dtype=jnp.float32), 'Wq': jax.random.normal(ks[1], (D, D), dtype=jnp.float32) * w_std, 'Wk': jax.random.normal(ks[2], (D, D), dtype=jnp.float32) * w_std, 'Wv': jax.random.normal(ks[3], (D, D), dtype=jnp.float32) * w_std, 'Wo': jax.random.normal(ks[4], (D, D), dtype=jnp.float32) * w_std}
    _L0_attn_all = _L0_attn_setup()
    _L0_attn_in = {k: v for k, v in _L0_attn_all.items() if k in ('Wq', 'Wk', 'Wv', 'Wo')}
    del _L0_attn_all

    def _L0_xattn_setup():
        import jax, jax.numpy as jnp
        import numpy as np
        key = jax.random.key(seed)
        ks = jax.random.split(key, 6)
        B, L, N, C, D = (8, 128, 512, 256, 128)
        return {'teacher_logits': jax.random.normal(ks[0], (B, L, N), dtype=jnp.float32), 'teacher_features': jax.random.normal(ks[1], (B, N, C), dtype=jnp.float32), 'Wq': jax.random.normal(ks[2], (D, C), dtype=jnp.float32) * (1.0 / np.sqrt(C)), 'bq': jnp.zeros((D,), dtype=jnp.float32), 'Wk': jax.random.normal(ks[3], (D, C), dtype=jnp.float32) * (1.0 / np.sqrt(C)), 'bk': jnp.zeros((D,), dtype=jnp.float32)}
    _L0_xattn_all = _L0_xattn_setup()
    _L0_xattn_in = {k: v for k, v in _L0_xattn_all.items() if k in ('Wq', 'bq', 'Wk', 'bk')}
    del _L0_xattn_all

    def _L0_ffn_setup():
        import jax, jax.numpy as jnp
        import numpy as np
        TOP_K = 2
        key = jax.random.key(seed)
        ks = jax.random.split(key, 7)
        B, S, H = (2, 512, 512)
        E, A, NS = (8, 64, 4096)
        x = jax.random.normal(ks[0], (B, S, H), jnp.float32)
        gate_w = jax.random.normal(ks[1], (E, H), jnp.float32) * 0.01
        W = jax.random.normal(ks[2], (H, H), jnp.float32) * 0.02
        atoms = jax.random.normal(ks[3], (A, NS), jnp.float32) * 0.02
        expert_atom_weights = jax.random.normal(ks[4], (E, A), jnp.float32) * 0.1
        importance = jax.random.normal(ks[5], (E, NS), jnp.float32) * 0.1
        mask_idx = jax.random.randint(ks[6], (NS,), 0, H * H, jnp.int32)
        return dict(x=x, gate_w=gate_w, W=W, atoms=atoms, expert_atom_weights=expert_atom_weights, importance=importance, mask_idx=mask_idx)
    _L0_ffn_all = _L0_ffn_setup()
    _L0_ffn_in = {k: v for k, v in _L0_ffn_all.items() if k in ('gate_w', 'W', 'atoms', 'expert_atom_weights', 'importance', 'mask_idx')}
    del _L0_ffn_all
    return {'x': x, 'ctx_1024': ctx_1024, 'L0_attn_Wq': _L0_attn_in['Wq'], 'L0_attn_Wk': _L0_attn_in['Wk'], 'L0_attn_Wv': _L0_attn_in['Wv'], 'L0_attn_Wo': _L0_attn_in['Wo'], 'L0_xattn_Wq': _L0_xattn_in['Wq'], 'L0_xattn_bq': _L0_xattn_in['bq'], 'L0_xattn_Wk': _L0_xattn_in['Wk'], 'L0_xattn_bk': _L0_xattn_in['bk'], 'L0_ffn_gate_w': _L0_ffn_in['gate_w'], 'L0_ffn_W': _L0_ffn_in['W'], 'L0_ffn_atoms': _L0_ffn_in['atoms'], 'L0_ffn_expert_atom_weights': _L0_ffn_in['expert_atom_weights'], 'L0_ffn_importance': _L0_ffn_in['importance'], 'L0_ffn_mask_idx': _L0_ffn_in['mask_idx']}

def reference(x, ctx_1024, L0_attn_Wq, L0_attn_Wk, L0_attn_Wv, L0_attn_Wo, L0_xattn_Wq, L0_xattn_bq, L0_xattn_Wk, L0_xattn_bk, L0_ffn_gate_w, L0_ffn_W, L0_ffn_atoms, L0_ffn_expert_atom_weights, L0_ffn_importance, L0_ffn_mask_idx):
    import jax
    import jax.numpy as jnp

    def _L0_attn_ref(x, Wq, Wk, Wv, Wo):
        import jax, jax.numpy as jnp
        import numpy as np
        N_HEADS = 32
        WINDOW = 128

        def _sliding_window_attention(x, Wq, Wk, Wv, Wo, n_heads=N_HEADS, window=WINDOW):
            B, T, D = x.shape
            H, dk = (n_heads, D // n_heads)
            bs = window
            assert T % bs == 0
            nb = T // bs

            def heads(y):
                return y.reshape(B, T, H, dk).transpose(0, 2, 1, 3)
            q = heads(x @ Wq.T)
            k = heads(x @ Wk.T)
            v = heads(x @ Wv.T)
            qb = q.reshape(B, H, nb, bs, dk)
            zpad = jnp.zeros((B, H, bs, dk), dtype=x.dtype)
            kp = jnp.concatenate([zpad, k], axis=2).reshape(B, H, nb + 1, bs, dk)
            vp = jnp.concatenate([zpad, v], axis=2).reshape(B, H, nb + 1, bs, dk)
            kw = jnp.concatenate([kp[:, :, :-1], kp[:, :, 1:]], axis=3)
            vw = jnp.concatenate([vp[:, :, :-1], vp[:, :, 1:]], axis=3)
            scale = 1.0 / np.sqrt(dk).astype(np.float32)
            scores = jnp.einsum('bhnrd,bhncd->bhnrc', qb, kw) * scale
            i = jnp.arange(nb)[:, None, None]
            r = jnp.arange(bs)[None, :, None]
            c = jnp.arange(2 * bs)[None, None, :]
            dist = bs + r - c
            key_global = i * bs - bs + c
            valid = (dist >= 0) & (dist <= window) & (key_global >= 0)
            scores = jnp.where(valid[None, None], scores, jnp.finfo(scores.dtype).min)
            probs = jax.nn.softmax(scores, axis=-1)
            out = jnp.einsum('bhnrc,bhncd->bhnrd', probs, vw)
            out = out.reshape(B, H, T, dk).transpose(0, 2, 1, 3).reshape(B, T, D)
            return out @ Wo.T
        return _sliding_window_attention(x, Wq, Wk, Wv, Wo)

    def _L0_xattn_ref(teacher_logits, teacher_features, Wq, bq, Wk, bk):
        import jax, jax.numpy as jnp
        import numpy as np
        query = jnp.einsum('bnc,dc->bnd', teacher_features, Wq) + bq
        key = jnp.einsum('bnc,dc->bnd', teacher_features, Wk) + bk
        energy = jnp.einsum('bnd,bmd->bnm', query, key)
        attention = jax.nn.softmax(energy, axis=-1)
        x_m = jnp.einsum('bln,bmn->blm', teacher_logits, attention)
        return x_m

    def _L0_ffn_ref(x, gate_w, W, atoms, expert_atom_weights, importance, mask_idx):
        import jax, jax.numpy as jnp
        import numpy as np
        TOP_K = 2
        B, S, H = x.shape
        xt = x.reshape(-1, H)
        logits = jnp.clip(xt @ gate_w.T, -50.0, 50.0)
        top_w, top_idx = jax.lax.top_k(logits, TOP_K)
        rw = jax.nn.softmax(top_w, axis=-1)
        deltas = jax.nn.softmax(expert_atom_weights, axis=-1) @ atoms
        weighted = deltas * jax.nn.sigmoid(importance)
        rows = mask_idx // H
        cols = mask_idx % H
        vals = jnp.einsum('tk,tks->ts', rw, weighted[top_idx])
        xg = xt[:, cols]
        contrib = jax.ops.segment_sum((xg * vals).T, rows, num_segments=H)
        out = xt @ W.T + contrib.T
        return out.reshape(B, S, H)
    x = _layernorm(x + _L0_attn_ref(x, L0_attn_Wq, L0_attn_Wk, L0_attn_Wv, L0_attn_Wo), axis=-1)
    x = _layernorm(x + _L0_xattn_ref(x, ctx_1024, L0_xattn_Wq, L0_xattn_bq, L0_xattn_Wk, L0_xattn_bk), axis=-1)
    x = _layernorm(x + _L0_ffn_ref(x, L0_ffn_gate_w, L0_ffn_W, L0_ffn_atoms, L0_ffn_expert_atom_weights, L0_ffn_importance, L0_ffn_mask_idx), axis=-1)
    return x

_drawn_inputs = setup_inputs


def setup_inputs(seed=0):
    import zlib

    import numpy as np

    out = dict(_drawn_inputs(seed))
    spreads = {'L0_xattn_bq': (0.0, 0.1), 'L0_xattn_bk': (0.0, 2.0)}
    factors = {'L0_attn_Wq': 8.0,
     'L0_attn_Wk': 8.0,
     'L0_ffn_gate_w': 22.008,
     'L0_ffn_atoms': 8.0,
     'L0_ffn_expert_atom_weights': 8.0,
     'L0_ffn_importance': 43.004}
    for name, (base, spread) in spreads.items():
        noise = np.random.default_rng([zlib.crc32(name.encode()), seed]).standard_normal(out[name].shape)
        drawn = base * np.exp(spread * noise) if base else spread * noise
        out[name] = jnp.asarray(drawn.astype(out[name].dtype))
    for name, factor in factors.items():
        out[name] = (out[name] * factor).astype(out[name].dtype)
    return out
```

```python
from contextlib import ExitStack

import concourse.bass as bass
from concourse import mybir

P = 128
B, T, D = 4, 512, 512
HEADS, DK = 32, 16
KC = D // P
TILES = T // P
ROUNDS = 2 * B
HR = HEADS // 2
FR = HR * DK
GROUPS = HR // 4
COLS = T + T - P
SLOTS = 8
C, DX = 256, 128
CC = C // P
E, ATOMS, NS = 8, 64, 4096
CHUNKS = NS // P
TOK = B * T
TT = TOK // P
J = 2 * TOK // P + E - 1
ZERO_COLS, ZERO_REP = 512, 16
ZERO_DMAS = D * D * E // (P * ZERO_COLS * ZERO_REP)
NEG = -1e30
EPS = 1e-5

F32 = mybir.dt.float32
F32R = mybir.dt.float32r
BF16 = mybir.dt.bfloat16
I32 = mybir.dt.int32
ALU = mybir.AluOpType
ACT = mybir.ActivationFunctionType
AX = mybir.AxisListType

Q_PART = (0, 0, 0, 1, 1, 2)
K_PART = (0, 1, 2, 0, 1, 0)
NP_ = len(Q_PART)
ROWS = NP_ * DK
MROWS = ROWS + 3


class Common:

    def __init__(self, nc, ctx):
        sb = lambda name, shape, dt: ctx.enter_context(nc.sbuf_tensor(name, shape, dt))
        self.id_f = sb("id_f", [P, P], F32)
        self.zeros = sb("zeros", [P, ZERO_COLS], F32)
        self.before = sb("before", [P, P], F32)
        self.ones = sb("ones", [P, P], F32)
        self.e_value = sb("e_value", [P, CHUNKS, E], F32)
        self.e_index = sb("e_index", [P, CHUNKS], I32)


def entries(nc, c, idx_row, idx_col, atoms, eaw, imp_t):
    with ExitStack() as ctx:
        sb = lambda name, shape, dt: ctx.enter_context(nc.sbuf_tensor(name, shape, dt))
        sem = lambda name: ctx.enter_context(nc.semaphore(name))
        row_i, col_i = sb("row_i", [P, NS], I32), sb("col_i", [P, CHUNKS], I32)
        row_f, col_f = sb("row_f", [P, NS], F32), sb("col_f", [P, CHUNKS], F32)
        same = sb("same", [P, CHUNKS, P], F32)
        earlier = sb("earlier", [P, CHUNKS, P], F32)
        after = sb("after", [P, P], F32)
        atom_sb = sb("atom_sb", [ATOMS, NS], F32)
        imp = sb("imp", [P, CHUNKS * E], F32)
        ew, ew_t = sb("ew", [E, ATOMS], F32), sb("ew_t", [ATOMS, E], F32)
        st = sb("st", [E, 4], F32)
        value = sb("value", [P, CHUNKS * E], F32)
        dup = sb("dup", [P, CHUNKS], F32)
        place_i, high_i = sb("place_i", [P, CHUNKS], I32), sb("high_i", [P, CHUNKS], I32)
        place, spare_i, spare = sb("place", [P, CHUNKS], F32), sb("spare_i", [P, CHUNKS], I32), sb("spare", [P, CHUNKS], F32)
        ps = [ctx.enter_context(nc.psum_tensor(f"ps_n{i}", [P, T], F32)) for i in range(3)]
        idx_in, atoms_in, eaw_in, imp_in = sem("idx_in"), sem("atoms_in"), sem("eaw_in"), sem("imp_in")
        filled, const, ve, ac, te = sem("filled_n"), sem("const_n"), sem("vector_n"), sem("scalar_n"), sem("tensor_n")
        block = ctx.enter_context(nc.Block())

        @block.sync
        def _(sp):
            sp.dma_start(ew[:], eaw).then_inc(eaw_in, 16)
            sp.dma_start(col_i[:], idx_col).then_inc(idx_in, 16)
            sp.dma_start(row_i[:], idx_row.partition_broadcast(P)).then_inc(idx_in, 16)
            sp.dma_start(imp[:], imp_t).then_inc(imp_in, 16)
            sp.dma_start(atom_sb[:], atoms).then_inc(atoms_in, 16)

        @block.gpsimd
        def _(pool):
            pool.memset(c.id_f[:], 0.0).then_inc(filled, 1)
            pool.memset(after[:], 1.0).then_inc(filled, 1)
            pool.memset(c.before[:], 1.0).then_inc(filled, 1)
            pool.memset(c.zeros[:], 0.0).then_inc(const, 1)
            pool.memset(c.ones[:], 1.0).then_inc(const, 1)
            pool.iota(spare_i[:], pattern=[[P, CHUNKS]], base=D * D, channel_multiplier=1).then_inc(const, 1)
            pool.wait_ge(filled, 3)
            pool.affine_select(out=c.id_f[:], in_=c.id_f[:], compare_op=ALU.not_equal, fill=1.0, base=0,
                               pattern=[[-1, P]], channel_multiplier=1).then_inc(const, 1)
            pool.affine_select(out=after[:], in_=after[:], compare_op=ALU.is_ge, fill=0.0, base=-1,
                               pattern=[[-1, P]], channel_multiplier=1).then_inc(const, 1)
            pool.affine_select(out=c.before[:], in_=c.before[:], compare_op=ALU.is_ge, fill=0.0, base=-1,
                               pattern=[[1, P]], channel_multiplier=-1).then_inc(const, 1)

        @block.scalar
        def _(act):
            act.wait_ge(ve, 1)
            act.activation(ew[:], ew[:], ACT.Exp, bias=st[:, 0:1], accum_out=st[:, 1:2]).then_inc(ac, 1)
            act.wait_ge(imp_in, 16)
            act.activation(imp[:], imp[:], ACT.Exp, scale=-1.0).then_inc(ac, 1)

        @block.vector
        def _(dve):
            n = [0]

            def link(ins):
                n[0] += 1
                ins.then_inc(ve, 1)
                dve.wait_ge(ve, n[0])

            dve.wait_ge(eaw_in, 16)
            link(dve.tensor_reduce(st[:, 0:1], ew[:], AX.X, ALU.max, negate=True))
            dve.wait_ge(ac, 1)
            link(dve.reciprocal(st[:, 2:3], st[:, 1:2]))
            link(dve.tensor_scalar(ew[:], ew[:], st[:, 2:3], None, ALU.mult))
            dve.wait_ge(te, 1)
            link(dve.tensor_copy(ew_t[:], ps[0][0:ATOMS, 0:E]))
            dve.wait_ge(ac, 2)
            link(dve.tensor_scalar(imp[:], imp[:], 1.0, None, ALU.add))
            link(dve.reciprocal(imp[:], imp[:]))
            dve.wait_ge(idx_in, 32)
            dve.wait_ge(const, 6)
            link(dve.tensor_copy(row_f[:], row_i[:]))
            link(dve.tensor_copy(col_f[:], col_i[:]))
            link(dve.tensor_tensor(same[:], row_f[:].rearrange("p (c s) -> p c s", s=P),
                                   col_f[:].unsqueeze(2).broadcast_to([P, CHUNKS, P]), ALU.is_equal))
            dve.wait_ge(te, 2)
            link(dve.tensor_tensor(value[:], ps[1][:, 0:CHUNKS * E], imp[:], ALU.mult))
            link(dve.tensor_tensor(earlier[:], same[:], after[:].unsqueeze(1).broadcast_to([P, CHUNKS, P]), ALU.mult))
            link(dve.tensor_reduce(dup[:], earlier[:], AX.X, ALU.max))
            link(dve.tensor_scalar(place_i[:], col_i[:], D - 1, D.bit_length() - 1, ALU.bitwise_and, ALU.logical_shift_left))
            link(dve.tensor_scalar(high_i[:], col_i[:], D.bit_length() - 1, None, ALU.logical_shift_right))
            link(dve.tensor_copy(place[:], place_i[:]))
            link(dve.tensor_copy(col_f[:], high_i[:]))
            link(dve.tensor_tensor(place[:], place[:], col_f[:], ALU.add))
            link(dve.tensor_copy(spare[:], spare_i[:]))
            link(dve.tensor_tensor(spare[:], spare[:], place[:], ALU.subtract))
            link(dve.tensor_tensor(spare[:], spare[:], dup[:], ALU.mult))
            link(dve.tensor_tensor(c.e_index[:], place[:], spare[:], ALU.add))
            dve.wait_ge(te, 3)
            link(dve.tensor_copy(c.e_value[:].rearrange("p c e -> p (c e)"), ps[2][:, 0:CHUNKS * E]))

        @block.tensor
        def _(pe):
            pe.wait_ge(const, 6)
            pe.wait_ge(ve, 3)
            pe.transpose(ps[0][0:ATOMS, 0:E], ew[:], c.id_f[0:E, 0:E]).then_inc(te, 1)
            pe.wait_ge(ve, 4)
            pe.wait_ge(atoms_in, 16)
            for k in range(CHUNKS):
                mm = pe.matmul(ps[1][:, k * E:(k + 1) * E], atom_sb[:, k * P:(k + 1) * P], ew_t[:], start=True, stop=True)
            mm.then_inc(te, 1)
            pe.wait_ge(ve, 10)
            for k in range(CHUNKS):
                mm = pe.matmul(ps[2][:, k * E:(k + 1) * E], same[:, k], value[:, k * E:(k + 1) * E], start=True, stop=True)
            mm.then_inc(te, 1)


def attention_plan():
    s_items = [(0, a) for a in range(HR // 4)] + [(i, a) for i in range(1, TILES) for a in range(HR // 2)]
    plan = [("split_x", 0)]
    plan += [(k, 0, n) for k in ("proj_q", "proj_k") for n in range(2)]
    plan += [("proj_v", 0, n) for n in range(TILES)]
    plan += [("score_max", 0, i, a) for i, a in s_items]
    for r in range(ROUNDS):
        more = r + 1 < ROUNDS
        if more:
            plan += [("proj_q", r + 1, n) for n in range(2)]
        plan.append(("max_t", r))
        if more:
            plan += [("proj_k", r + 1, n) for n in range(2)]
        if r:
            plan.append(("pv", r - 1, GROUPS - 1))
        if more:
            plan += [("proj_v", r + 1, n) for n in range(TILES)]
        if r:
            plan.append(("o_t", r - 1, GROUPS - 1))
        done = 0
        for n in range(HR):
            plan.append(("score_exp", r, n))
            if n == 3 and r % 2 == 0 and more and r // 2 + 1 < B:
                plan.append(("split_x", r // 2 + 1))
            if more and n >= 3:
                until = len(s_items) * (n - 2) // (HR - 3)
                plan += [("score_max", r + 1, *s_items[k]) for k in range(done, until)]
                done = until
            if n >= 5 and n % 4 == 1:
                plan.append(("pv", r, n // 4 - 1))
            if n >= 7 and n % 4 == 3:
                plan.append(("o_t", r, n // 4 - 1))
    plan += [("pv", ROUNDS - 1, GROUPS - 1), ("o_t", ROUNDS - 1, GROUPS - 1)]
    return plan


def attention(nc, c, x_t, wq_t, wk_t, wv_t, parts_dram, o_dram, s_dram):
    plan = attention_plan()
    at = {step: n for n, step in enumerate(plan)}
    general = [s for s in plan if s[0] in ("proj_q", "proj_k", "proj_v", "max_t", "o_t")]
    bank_of = {s: (n % 2, n // 2) for n, s in enumerate(general)}
    s_order = {s: n for n, s in enumerate(s for s in plan if s[0] == "score_max")}

    with ExitStack() as ctx:
        sb = lambda name, shape, dt: ctx.enter_context(nc.sbuf_tensor(name, shape, dt))
        sem = lambda name: ctx.enter_context(nc.semaphore(name))

        x_raw = sb("x_raw", [P, KC, T], F32)
        x_hi = sb("x_hi", [P, KC, T], F32R)
        x_lo = sb("x_lo", [P, KC, T], F32R)
        w_hi = sb("w_hi", [P, 3, KC, D], F32R)
        w_lo = sb("w_lo", [P, 3, KC, D], F32R)
        q_st = sb("q_st", [P, 2, HR, T], BF16)
        k_st = sb("k_st", [P, 2, HR, T], BF16)
        v_sb = sb("v_sb", [P, 2, TILES, HR, DK + 1], F32)
        probs = sb("probs", [P, SLOTS, COLS], F32)
        w_raw = probs[:, 0:7, :].rearrange("p s c -> p (s c)")[:, 0:3 * KC * D].rearrange("p (w k n) -> p w k n", w=3, k=KC)
        parts = sb("parts", [P, 2, 3, T], BF16)
        rest = sb("rest", [P, 2, T], F32)
        o_sb = sb("o_sb", [P, 2, T], F32)
        o_n = sb("o_n", [P, 2, TILES, FR], F32)
        r_den = sb("r_den", [P, 2, TILES, 4], F32)
        n_max = sb("n_max", [P, HR, TILES], F32)
        m_rest = sb("m_rest", [TILES * HR, P], F32)
        m_part = sb("m_part", [TILES * HR, 3, P], BF16)
        mask_w = sb("mask_w", [P, 2, 2, P], BF16)
        mask_c = sb("mask_c", [P, 4, P], BF16)
        mask_e = sb("mask_e", [P, 2, 2, P], BF16)
        id_b = sb("id_b", [P, P], BF16)

        ps_g = [ctx.enter_context(nc.psum_tensor(f"ps_g{i}", [P, T], F32)) for i in range(2)]
        ps_s = [ctx.enter_context(nc.psum_tensor(f"ps_s{i}", [P, T], F32)) for i in range(2)]
        ps_e = [ctx.enter_context(nc.psum_tensor(f"ps_e{i}", [P, T], F32)) for i in range(3)]
        ps_o = ctx.enter_context(nc.psum_tensor("ps_o", [P, T], F32))

        w_loaded = [sem(f"w_loaded{i}") for i in range(3)]
        w_hi_done, w_lo_done = sem("w_hi_done"), sem("w_lo_done")
        x_loaded, x_hi_done, x_lo_done = sem("x_loaded"), sem("x_hi_done"), sem("x_lo_done")
        const_done, fill_done, o_cleared = sem("const_done"), sem("fill_done"), sem("o_cleared")
        g_full = [sem(f"g_full{i}") for i in range(2)]
        g_free = [sem(f"g_free{i}") for i in range(2)]
        part1_done, rest_done, part2_done, part3_done = (sem(f"part{i}_done") for i in range(1, 5))
        part_stored = [sem(f"part_stored{i}") for i in range(2)]
        q_stacked = [sem(f"q_stacked{i}") for i in range(2)]
        k_stacked = [sem(f"k_stacked{i}") for i in range(2)]
        m_stacked = [sem(f"m_stacked{i}") for i in range(2)]
        v_done, s_full, s_max_done = sem("v_done"), sem("s_full"), sem("s_max_done")
        m_step, e_full, exp_done = sem("m_step"), sem("e_full"), sem("exp_done")
        pv_done, o_copied, den_done, norm_done = (
            sem("pv_done"), sem("o_copied"), sem("den_done"), sem("norm_done"))
        o_stored = [sem(f"o_stored{i}") for i in range(2)]
        zeroed, entry_added = sem("zeroed"), sem("entry_added")

        block = ctx.enter_context(nc.Block())

        def part_no(kind, r, n):
            return 4 * r + 2 * (kind == "proj_k") + n

        def wait_full(eng, step):
            bank, nth = bank_of[step]
            eng.wait_ge(g_full[bank], nth + 1)
            return ps_g[bank]

        @block.sync
        def _(sp):
            for i, w in enumerate((wq_t, wk_t, wv_t)):
                if i == 1:
                    sp.dma_start(x_raw[:], x_t[0].rearrange("(k p) t -> p k t", p=P)).then_inc(x_loaded, 16)
                sp.dma_start(w_raw[:, i], w.rearrange("(k p) n -> p k n", p=P)).then_inc(w_loaded[i], 16)
            rows = D * D // ZERO_DMAS
            for n in range(ZERO_DMAS):
                sp.dma_start(s_dram[n * rows:(n + 1) * rows].rearrange("(p a b) e -> p a (b e)", p=P, a=ZERO_REP),
                             c.zeros[:].unsqueeze(1).broadcast_to([P, ZERO_REP, ZERO_COLS])).then_inc(zeroed, 16)
            sp.dma_start(s_dram[D * D:].rearrange("(p b) e -> p (b e)", p=P), c.zeros[:, 0:CHUNKS * E]).then_inc(zeroed, 16)
            for step in plan:
                kind, r = step[:2]
                if kind == "split_x" and r + 1 < B:
                    sp.wait_ge(x_hi_done, r + 1)
                    sp.wait_ge(x_lo_done, r + 1)
                    sp.dma_start(x_raw[:], x_t[r + 1].rearrange("(k p) t -> p k t", p=P)).then_inc(x_loaded, 16)
                if kind in ("proj_q", "proj_k"):
                    no, which = part_no(*step), int(kind == "proj_k")
                    sp.wait_ge(part3_done, no + 1)
                    sp.dma_start(parts_dram[which, r, :, step[2] * P:(step[2] + 1) * P, :].rearrange("a p t -> p a t"),
                                 parts[:, no % 2]).then_inc(part_stored[no % 2], 16)
                    if step[2] == 1:
                        sp.wait_ge(part_stored[0], 16 * (no // 2 + 1))
                        sp.wait_ge(part_stored[1], 16 * (no // 2 + 1))
                        if r >= 2:
                            sp.wait_ge(e_full, 2 * HR * (r - 1))
                        dst, of, done = ((q_st, Q_PART, q_stacked), (k_st, K_PART, k_stacked))[which]
                        for n in range(NP_):
                            sp.dma_start(dst[n * DK:(n + 1) * DK, r % 2],
                                         parts_dram[which, r, of[n]].rearrange("(h d) t -> d h t", d=DK)
                                         ).then_inc(done[r % 2], 16)
                if kind == "max_t":
                    sp.wait_ge(m_step, 4 * (r + 1))
                    if r >= 2:
                        sp.wait_ge(e_full, 2 * HR * (r - 1))
                    for n in range(3):
                        sp.dma_start(q_st[ROWS + n:ROWS + n + 1, r % 2].rearrange("o h (i t) -> o (h i) t", i=TILES),
                                     m_part[:, n]
                                     ).then_inc(m_stacked[r % 2], 16)
                if kind == "o_t" and step[2] == GROUPS - 1:
                    sp.wait_ge(norm_done, GROUPS * (r + 1))
                    sp.dma_start(o_dram[r // 2, :, (r % 2) * FR:(r % 2 + 1) * FR].rearrange("(i p) f -> p i f", p=P),
                                 o_n[:, r % 2]).then_inc(o_stored[r % 2], 16)
            for i in range(2):
                sp.wait_ge(o_stored[i], 16 * ROUNDS // 2)
            sp.wait_ge(entry_added, 16 * CHUNKS)

        @block.gpsimd
        def _(pool):
            pool.memset(mask_w[:], 0.0).then_inc(fill_done, 1)
            pool.memset(mask_c[:], 0.0).then_inc(fill_done, 1)
            pool.memset(mask_e[:], 0.0).then_inc(fill_done, 1)
            pool.memset(v_sb[:, :, :, :, DK:DK + 1], 1.0).then_inc(const_done, 1)
            pool.wait_ge(fill_done, 3)
            pool.affine_select(out=mask_w[:, :, 0], in_=mask_w[:, :, 0], compare_op=ALU.is_ge, fill=NEG, base=0,
                               pattern=[[0, 2], [1, P]], channel_multiplier=-1).then_inc(const_done, 1)
            pool.affine_select(out=mask_w[:, :, 1], in_=mask_w[:, :, 1], compare_op=ALU.is_ge, fill=NEG, base=0,
                               pattern=[[0, 2], [-1, P]], channel_multiplier=1).then_inc(const_done, 1)
            pool.affine_select(out=mask_c[:], in_=mask_c[:], compare_op=ALU.is_ge, fill=NEG, base=0,
                               pattern=[[0, 4], [-1, P]], channel_multiplier=1).then_inc(const_done, 1)
            pool.affine_select(out=mask_e[:, :, 0], in_=mask_e[:, :, 0], compare_op=ALU.is_ge, fill=NEG, base=0,
                               pattern=[[0, 2], [1, P]], channel_multiplier=-1).then_inc(const_done, 1)
            pool.affine_select(out=mask_e[:, :, 1], in_=mask_e[:, :, 1], compare_op=ALU.is_ge, fill=NEG, base=0,
                               pattern=[[0, 2], [-1, P]], channel_multiplier=1).then_inc(const_done, 1)
            pool.tensor_copy(id_b[:], c.id_f[:]).then_inc(const_done, 1)
            pool.wait_ge(const_done, 7)
            pool.memset(k_st[ROWS:P], 1.0).then_inc(const_done, 1)
            pool.wait_ge(const_done, 8)
            pool.wait_ge(zeroed, 16 * (ZERO_DMAS + 1))
            chunk = 0
            for step in plan:
                kind, r = step[:2]
                if kind == "score_exp" and chunk < CHUNKS and step[2] % 2:
                    if chunk:
                        pool.wait_ge(entry_added, 16 * chunk)
                    pool.indirect_dma_start(out=s_dram, out_offset=bass.IndirectOffsetOnAxis(ap=c.e_index[:, chunk:chunk + 1], axis=0),
                                            in_=c.e_value[:, chunk], in_offset=None, compute_op=ALU.add).then_inc(entry_added, 16)
                    chunk += 1
                if kind == "split_x":
                    pool.wait_ge(x_hi_done, r + 1)
                    pool.tensor_tensor(x_lo[:], x_raw[:], x_hi[:].bitcast(F32), ALU.subtract).then_inc(x_lo_done, 1)

        @block.scalar
        def _(act):
            for i in range(3):
                act.wait_ge(w_loaded[i], 16)
                act.activation(w_hi[:, i], w_raw[:, i], ACT.Copy).then_inc(w_hi_done, 1)
            for step in plan:
                kind, r = step[:2]
                if kind == "split_x":
                    act.wait_ge(x_loaded, 16 * (r + 1))
                    if r:
                        bank, nth = bank_of[("proj_v", 2 * r - 1, TILES - 1)]
                        act.wait_ge(g_full[bank], nth + 1)
                    act.activation(x_hi[:], x_raw[:], ACT.Copy).then_inc(x_hi_done, 1)
                if kind in ("proj_q", "proj_k"):
                    no, scale = part_no(*step), DK ** -0.5 if kind == "proj_q" else 1.0
                    ps = wait_full(act, step)
                    if no >= 2:
                        act.wait_ge(part_stored[no % 2], 16 * (no // 2))
                    act.activation(parts[:, no % 2, 0], ps[:], ACT.Copy, scale=scale).then_inc(part1_done, 1)
                if kind == "proj_v":
                    ps = wait_full(act, step)
                    if r == 0 and step[2] == 0:
                        act.wait_ge(const_done, 8)
                    act.activation(v_sb[:, r % 2, step[2], :, 0:DK], ps[:, 0:FR].rearrange("p (h d) -> p h d", d=DK),
                                   ACT.Copy).then_inc(g_free[bank_of[step][0]], 1)
                if kind == "score_exp":
                    head = HR * r + step[2]
                    if head == 0:
                        act.wait_ge(w_lo_done, 3)
                    if head >= SLOTS:
                        act.wait_ge(pv_done, (head - SLOTS) // 4 + 1)
                    for half, (c0, c1) in enumerate(((0, T), (T, COLS))):
                        e = 2 * head + half
                        act.wait_ge(e_full, e + 1)
                        act.activation(probs[:, head % SLOTS, c0:c1], ps_e[e % 3][:, 0:c1 - c0], ACT.Exp).then_inc(exp_done, 1)
                if kind == "pv":
                    g = GROUPS * r + step[2]
                    act.wait_ge(pv_done, g + 1)
                    if g >= 2:
                        wait_full(act, ("o_t", (g - 2) // GROUPS, (g - 2) % GROUPS))
                    act.activation(o_sb[:, g % 2], ps_o[:], ACT.Copy).then_inc(o_copied, 1)

        @block.vector
        def _(dve):
            dve.memset(ps_o[:], 0.0).then_inc(o_cleared, 1)
            for i in range(3):
                dve.wait_ge(w_hi_done, i + 1)
                dve.tensor_tensor(w_lo[:, i], w_raw[:, i], w_hi[:, i].bitcast(F32), ALU.subtract).then_inc(w_lo_done, 1)
            for step in plan:
                kind, r = step[:2]
                if kind in ("proj_q", "proj_k"):
                    no, scale = part_no(*step), DK ** -0.5 if kind == "proj_q" else 1.0
                    slot = no % 2
                    ps = ps_g[bank_of[step][0]]
                    dve.wait_ge(part1_done, no + 1)
                    dve.scalar_tensor_tensor(out=rest[:, slot], in0=ps[:], scalar=scale, in1=parts[:, slot, 0],
                                             op0=ALU.mult, op1=ALU.subtract).then_inc(g_free[bank_of[step][0]], 1)
                    dve.wait_ge(g_free[bank_of[step][0]], bank_of[step][1] + 1)
                    dve.tensor_copy(parts[:, slot, 1], rest[:, slot]).then_inc(part2_done, 1)
                    dve.wait_ge(part2_done, no + 1)
                    dve.tensor_tensor(parts[:, slot, 2], rest[:, slot], parts[:, slot, 1], ALU.subtract).then_inc(part3_done, 1)
                if kind == "score_max":
                    s, (i, a) = s_order[step], step[2:]
                    per = 4 if i == 0 else 2
                    dve.wait_ge(s_full, s + 1)
                    if s and (i, a) == (0, 0):
                        bank, nth = bank_of[("max_t", r - 1)]
                        dve.wait_ge(g_full[bank], nth + 1)
                    dve.tensor_reduce(n_max[:, per * a:per * (a + 1), i], ps_s[s % 2][:].rearrange("p (h k) -> p h k", h=per),
                                      AX.X, ALU.max, negate=True).then_inc(s_max_done, 1)
                if kind == "max_t":
                    ps, (bank, nth) = wait_full(dve, step), bank_of[step]
                    if r:
                        dve.wait_ge(m_stacked[(r - 1) % 2], 48 * ((r - 1) // 2 + 1))
                    n = TILES * HR
                    dve.tensor_copy(m_part[:, 0], ps[0:n, 0:P]).then_inc(m_step, 1)
                    dve.wait_ge(m_step, 4 * r + 1)
                    dve.tensor_tensor(m_rest[:], ps[0:n, 0:P], m_part[:, 0], ALU.subtract).then_inc(g_free[bank], 1)
                    dve.wait_ge(g_free[bank], nth + 1)
                    dve.tensor_copy(m_part[:, 1], m_rest[:]).then_inc(m_step, 1)
                    dve.wait_ge(m_step, 4 * r + 2)
                    dve.tensor_tensor(m_part[:, 2], m_rest[:], m_part[:, 1], ALU.subtract).then_inc(m_step, 2)
                if kind == "o_t":
                    g = GROUPS * r + step[2]
                    ps, (bank, nth) = wait_full(dve, step), bank_of[step]
                    heads = ps[:].rearrange("p (i h c) -> p i h c", i=TILES, h=4)
                    dve.reciprocal(r_den[:, g % 2], heads[:, :, :, DK]).then_inc(den_done, 1)
                    if r >= 2 and step[2] == 0:
                        dve.wait_ge(o_stored[r % 2], 16 * (r // 2))
                    dve.wait_ge(den_done, g + 1)
                    for i in range(TILES):
                        last = dve.tensor_tensor(
                            o_n[:, r % 2, i, step[2] * 64:(step[2] + 1) * 64].rearrange("p (h d) -> p h d", h=4),
                            heads[:, i, :, 0:DK], r_den[:, g % 2, i].unsqueeze(2).broadcast_to([P, 4, DK]), ALU.mult)
                        if i == TILES - 1:
                            last.then_inc(norm_done, 1)
                    dve.wait_ge(norm_done, g + 1)
                    dve.sem_inc(g_free[bank], 1)

        @block.tensor
        def _(pe):
            def take_bank(step):
                bank, nth = bank_of[step]
                if nth:
                    pe.wait_ge(g_free[bank], nth)
                return ps_g[bank], g_full[bank]

            for step in plan:
                kind, r = step[:2]
                if kind in ("proj_q", "proj_k", "proj_v"):
                    w = ("proj_q", "proj_k", "proj_v").index(kind)
                    pe.wait_ge(w_lo_done, w + 1)
                    pe.wait_ge(x_lo_done, r // 2 + 1)
                    ps, full = take_bank(step)
                    terms = [(a, b, k) for a, b in ((0, 0), (0, 1), (1, 0)) for k in range(KC)]
                    for n, (a, b, k) in enumerate(terms):
                        wt, xt = (w_hi, w_lo)[a], (x_hi, x_lo)[b]
                        f0 = (r % 2) * FR
                        if kind == "proj_v":
                            mm = pe.matmul(ps[:, 0:FR], xt[:, k, step[2] * P:(step[2] + 1) * P], wt[:, w, k, f0:f0 + FR],
                                           start=n == 0, stop=n == len(terms) - 1)
                        else:
                            f0 += step[2] * P
                            mm = pe.matmul(ps[:], wt[:, w, k, f0:f0 + P], xt[:, k], start=n == 0, stop=n == len(terms) - 1)
                    mm.then_inc(full, 1)
                if kind == "score_max":
                    s, (i, a) = s_order[step], step[2:]
                    if s == 0:
                        pe.wait_ge(const_done, 8)
                    if (i, a) == (0, 0):
                        pe.wait_ge(q_stacked[r % 2], 16 * NP_ * (r // 2 + 1))
                        pe.wait_ge(k_stacked[r % 2], 16 * NP_ * (r // 2 + 1))
                    if s >= 2:
                        pe.wait_ge(s_max_done, s - 1)
                    ps, per = ps_s[s % 2], 4 if i == 0 else 2
                    mask = mask_c[:].rearrange("p h k -> p (h k)") if i == 0 else mask_w[:].rearrange("p h w k -> p (h w k)")
                    width = T // per
                    for n in range(per):
                        h = per * a + n
                        mm = pe.matmul(ps[:, n * width:(n + 1) * width], q_st[0:ROWS, r % 2, h, i * P:(i + 1) * P],
                                       k_st[0:ROWS, r % 2, h, (i + 1) * P - width:(i + 1) * P], start=n == 0, stop=False,
                                       skip_group_check=True)
                    mm = pe.matmul(ps[:], id_b[:], mask, start=False, stop=True, skip_group_check=True)
                    mm.then_inc(s_full, 1)
                if kind == "max_t":
                    ps, full = take_bank(step)
                    pe.wait_ge(s_max_done, (r + 1) * len(s_order) // ROUNDS)
                    pe.transpose(ps[0:TILES * HR, 0:P], n_max[:].rearrange("p h i -> p (h i)"), c.id_f[:]).then_inc(full, 1)
                if kind == "score_exp":
                    h = step[2]
                    if h == 0:
                        pe.wait_ge(m_stacked[r % 2], 48 * (r // 2 + 1))
                    for half in range(2):
                        e = 2 * (HR * r + h) + half
                        if e >= 3:
                            pe.wait_ge(exp_done, e - 2)
                        for j in (2 * half, 2 * half + 1):
                            c0, width = 2 * P * (j % 2), min(2 * P, T - j * P)
                            mm = pe.matmul(ps_e[e % 3][:, c0:c0 + width], k_st[0:MROWS, r % 2, h, j * P:(j + 1) * P],
                                           q_st[0:MROWS, r % 2, h, j * P:j * P + width], start=j % 2 == 0, stop=False,
                                           skip_group_check=True)
                        c1 = c0 + width
                        mm = pe.matmul(ps_e[e % 3][:, 0:c1], id_b[:], mask_e[:].rearrange("p a w q -> p (a w q)")[:, 0:c1],
                                       start=False, stop=True, skip_group_check=True)
                        mm.then_inc(e_full, 1)
                if kind == "pv":
                    g = GROUPS * r + step[2]
                    pe.wait_ge(exp_done, 8 * (g + 1))
                    if g == 0:
                        pe.wait_ge(o_cleared, 1)
                    if g:
                        pe.wait_ge(o_copied, g)
                    for j in range(TILES):
                        width = min(2 * P, T - j * P)
                        for n in range(4):
                            h = 4 * step[2] + n
                            mm = pe.matmul(ps_o[32 * n:32 * n + DK + 1, j * P:j * P + width], v_sb[:, r % 2, j, h],
                                           probs[:, (HR * r + h) % SLOTS, 2 * P * j:2 * P * j + width],
                                           start=j == 0, stop=True, skip_group_check=True)
                    mm.then_inc(pv_done, 1)
                if kind == "o_t":
                    g = GROUPS * r + step[2]
                    ps, full = take_bank(step)
                    pe.wait_ge(o_copied, g + 1)
                    for i in range(TILES):
                        mm = pe.transpose(ps[:, i * P:(i + 1) * P], o_sb[:, g % 2, i * P:(i + 1) * P], c.id_f[:])
                    mm.then_inc(full, 1)


def cross_plan():
    def maps(b):
        return [("qx", b), ("kx", b)] + rows("energy", b) + turned("a_t", b)

    def turned(kind, b):
        return [(kind, b, k) for k in range(KC)]

    def rows(kind, b):
        return [(kind, b, i) for i in range(TILES)]

    plan = maps(0) + turned("o_t", 0) + rows("o_proj", 0)
    for b in range(B):
        more = b + 1 < B
        if more:
            plan += maps(b + 1)
        plan += turned("x1_t", b) + rows("mix", b)
        if more:
            plan += turned("o_t", b + 1) + rows("o_proj", b + 1)
        plan += turned("x2_t", b) + [("logit", b)] + rows("x2_w", b) + [("logit_t", b)]
    return plan


def cross(nc, c, x, o_dram, ctx_t, wxq_t, wxk_t, bxq, bxk, wo_t, w_t, gate_t, x2_dram, base, logits):
    plan = cross_plan()
    bank_of = {s: (n % 8, n // 8) for n, s in enumerate(plan)}
    turns = [s[:2] for s in plan if s[0] in ("o_t", "x1_t", "x2_t") and s[2] == 0]
    turn_no = {s: n for n, s in enumerate(turns)}
    lo_no = {s: n for n, s in enumerate(s for s in plan if s[0] in ("qx", "kx"))}
    en_no = {s: n for n, s in enumerate(s for s in plan if s[0] == "energy")}

    with ExitStack() as ctx:
        sb = lambda name, shape, dt: ctx.enter_context(nc.sbuf_tensor(name, shape, dt))
        sem = lambda name: ctx.enter_context(nc.semaphore(name))
        wo_hi, wo_lo = sb("wo_hi", [P, KC, D], F32R), sb("wo_lo", [P, KC, D], F32R)
        wf_hi, wf_lo = sb("wf_hi", [P, KC, D], F32R), sb("wf_lo", [P, KC, D], F32R)
        wx_raw = sb("wx_raw", [P, 2, CC, DX], F32)
        wx_hi, wx_lo = sb("wx_hi", [P, 2, CC, DX], F32R), sb("wx_lo", [P, 2, CC, DX], F32R)
        g_raw = sb("g_raw", [P, KC, P], F32)
        g_hi, g_lo = sb("g_hi", [P, KC, P], F32R), sb("g_lo", [P, KC, P], F32R)
        bias = sb("bias_x", [P, 2], F32)
        x_sb = sb("x_sb", [P, 2, TILES, D], F32)
        on_sb = sb("on_sb", [P, 2, TILES, D], F32)
        t_hi, t_lo = sb("t_hi", [P, 2, KC, T], F32R), sb("t_lo", [P, 2, KC, T], F32R)
        c_raw = sb("c_raw", [P, CC, T], F32)
        c_hi, c_lo = sb("c_hi", [P, CC, T], F32R), sb("c_lo", [P, CC, T], F32R)
        qk_hi, qk_lo = sb("qk_hi", [P, 2, T], F32R), sb("qk_lo", [P, 2, T], F32R)
        e_sb = sb("e_sb", [P, TILES, T], F32)
        a_hi, a_lo = sb("a_hi", [P, 2, TILES, T], F32R), sb("a_lo", [P, 2, TILES, T], F32R)
        n_mx = sb("n_mx", [P, TILES], F32)
        a_sum, a_inv = sb("a_sum", [P, TILES], F32), sb("a_inv", [P, TILES], F32)
        stats = sb("stats", [P, TILES, 6], F32)
        mv = sb("mv", [P, 2, TILES, 2], F32)
        var_e, rstd, m_half = sb("var_e", [P, 2, TILES], F32), sb("rstd", [P, 2, TILES], F32), sb("m_half", [P, TILES], F32)
        lg_sb = sb("lg_sb", [P, T], F32)
        ps = [ctx.enter_context(nc.psum_tensor(f"ps_c{i}", [P, T], F32)) for i in range(8)]

        wo_in, wf_in, wx_in, g_in = sem("wo_in"), sem("wf_in"), sem("wx_in"), sem("g_in")
        w_hi_done, w_lo_done, half_done = sem("cw_hi_done"), sem("cw_lo_done"), sem("half_done")
        full = [sem(f"c_full{i}") for i in range(8)]
        free = [sem(f"c_free{i}") for i in range(8)]
        x_in = [sem(f"x_in{i}") for i in range(2)]
        on_in = [sem(f"on_in{i}") for i in range(2)]
        c_in, c_hi_done, c_lo_done = sem("c_in"), sem("c_hi_done"), sem("c_lo_done")
        qk_hi_done, qk_lo_done = sem("qk_hi_done"), sem("qk_lo_done")
        mx_done, map_done, a_hi_done, a_lo_done, inv_done = (
            sem("mx_done"), sem("map_done"), sem("a_hi_done"), sem("a_lo_done"), sem("inv_done"))
        t_hi_done, t_lo_done = sem("t_hi_done"), sem("t_lo_done")
        stat_done, agg_done, var_done, rstd_done, norm_done = (
            sem("stat_done"), sem("agg_done"), sem("var_done"), sem("rstd_done"), sem("cnorm_done"))
        x2_stored, base_done, lg_done, logit_done = sem("x2_stored"), sem("base_done"), sem("lg_done"), sem("logit_done")
        block = ctx.enter_context(nc.Block())

        norms = [s[:2] for s in plan if s[0] in ("o_proj", "mix") and s[2] == 0]
        norm_no = {s: n for n, s in enumerate(norms)}
        frees, count = {}, [0] * 8
        for step in plan:
            bank = bank_of[step][0]
            count[bank] += step[0] in ("qx", "kx", "energy", "o_proj", "mix", "logit")
            frees[step] = count[bank]

        @block.sync
        def _(sp):
            sp.dma_start(wx_raw[:, 0], wxq_t.rearrange("(k p) n -> p k n", p=P)).then_inc(wx_in, 16)
            sp.dma_start(wx_raw[:, 1], wxk_t.rearrange("(k p) n -> p k n", p=P)).then_inc(wx_in, 16)
            sp.dma_start(bias[:, 0:1], bxq).then_inc(wx_in, 16)
            sp.dma_start(bias[:, 1:2], bxk).then_inc(wx_in, 16)
            sp.dma_start(c_raw[:], ctx_t[0].rearrange("(k p) t -> p k t", p=P)).then_inc(c_in, 16)
            sp.dma_start(on_sb[:, 0], o_dram[0].rearrange("(i p) f -> p i f", p=P)).then_inc(on_in[0], 16)
            sp.dma_start(x_sb[:, 1], wo_t.rearrange("(k p) n -> p k n", p=P)).then_inc(wo_in, 16)
            sp.dma_start(x_sb[:, 0], x[0].rearrange("(i p) f -> p i f", p=P)).then_inc(x_in[0], 16)
            sp.dma_start(on_sb[:, 1], w_t.rearrange("(k p) n -> p k n", p=P)).then_inc(wf_in, 16)
            sp.dma_start(g_raw[:, :, 0:E], gate_t.rearrange("(k p) e -> p k e", p=P)).then_inc(g_in, 16)
            sp.wait_ge(w_lo_done, 4)
            sp.dma_start(on_sb[:, 1], o_dram[1].rearrange("(i p) f -> p i f", p=P)).then_inc(on_in[1], 16)
            sp.dma_start(x_sb[:, 1], x[1].rearrange("(i p) f -> p i f", p=P)).then_inc(x_in[1], 16)
            for step in plan:
                kind, b = step[:2]
                if kind == "kx" and b + 1 < B:
                    sp.wait_ge(c_lo_done, b + 1)
                    sp.dma_start(c_raw[:], ctx_t[b + 1].rearrange("(k p) t -> p k t", p=P)).then_inc(c_in, 16)
                if kind == "mix" and step[2] == TILES - 1:
                    sp.wait_ge(norm_done, TILES * (norm_no[("mix", b)] + 1))
                    sp.dma_start(x2_dram[b * T:(b + 1) * T].rearrange("(i p) f -> p i f", p=P), x_sb[:, b % 2]).then_inc(x2_stored, 16)
                if kind == "o_proj" and step[2] == TILES - 1 and b + 2 < B:
                    sp.wait_ge(t_lo_done, KC * (turn_no[("o_t", b)] + 1))
                    sp.dma_start(on_sb[:, b % 2], o_dram[b + 2].rearrange("(i p) f -> p i f", p=P)).then_inc(on_in[b % 2], 16)
                if kind == "x2_w" and step[2] == TILES - 1 and b + 2 < B:
                    sp.wait_ge(base_done, TILES * (b + 1))
                    sp.wait_ge(x2_stored, 16 * (b + 1))
                    sp.dma_start(x_sb[:, b % 2], x[b + 2].rearrange("(i p) f -> p i f", p=P)).then_inc(x_in[b % 2], 16)
            sp.wait_ge(x2_stored, 16 * B)

        @block.gpsimd
        def _(pool):
            pool.memset(g_raw[:, :, E:P], 0.0).then_inc(half_done, 1)
            pool.memset(m_half[:], -0.5).then_inc(half_done, 1)
            pool.wait_ge(half_done, 2)
            for step in plan:
                kind, b = step[:2]
                if kind == "qx":
                    pool.wait_ge(c_hi_done, b + 1)
                    pool.tensor_tensor(c_lo[:], c_raw[:], c_hi[:].bitcast(F32), ALU.subtract).then_inc(c_lo_done, 1)
                if kind in ("o_proj", "mix") and step[2] == TILES - 1:
                    n = norm_no[step[:2]]
                    pool.wait_ge(agg_done, TILES * (n + 1))
                    pool.tensor_scalar(var_e[:, n % 2], mv[:, n % 2, :, 1], EPS, None, ALU.add).then_inc(var_done, 1)
                    pool.wait_ge(var_done, n + 1)
                    pool.tensor_tensor(rstd[:, n % 2], var_e[:, n % 2], m_half[:], ALU.pow).then_inc(rstd_done, 1)

        @block.scalar
        def _(act):
            def weights(n, src, hi, loaded, count):
                act.wait_ge(loaded, count)
                act.activation(hi, src, ACT.Copy).then_inc(w_hi_done, 1)

            weights(0, wx_raw[:], wx_hi[:], wx_in, 64)
            act.wait_ge(c_in, 16)
            act.activation(c_hi[:], c_raw[:], ACT.Copy).then_inc(c_hi_done, 1)
            weights(1, x_sb[:, 1], wo_hi[:], wo_in, 16)
            weights(2, on_sb[:, 1], wf_hi[:], wf_in, 16)
            act.wait_ge(half_done, 2)
            weights(3, g_raw[:], g_hi[:], g_in, 16)
            for step in plan:
                kind, b = step[:2]
                bank, nth = bank_of[step]
                if kind in ("qx", "kx"):
                    n, w = lo_no[step], int(kind == "kx")
                    act.wait_ge(full[bank], nth + 1)
                    if b and not w:
                        eb, en = bank_of[("energy", b - 1, TILES - 1)]
                        act.wait_ge(full[eb], en + 1)
                    act.activation(qk_hi[:, w], ps[bank][:], ACT.Identity, bias=bias[:, w:w + 1]).then_inc(qk_hi_done, 1)
                    if w and b + 1 < B:
                        act.wait_ge(c_in, 16 * (b + 2))
                        act.activation(c_hi[:], c_raw[:], ACT.Copy).then_inc(c_hi_done, 1)
                if kind == "energy":
                    n, i = en_no[step], step[2]
                    act.wait_ge(mx_done, n + 1)
                    if b and i == 0:
                        tb, tn = bank_of[("a_t", b - 1, KC - 1)]
                        act.wait_ge(full[tb], tn + 1)
                    act.activation(e_sb[:, i], ps[bank][:], ACT.Exp, bias=n_mx[:, i:i + 1],
                                   accum_out=a_sum[:, i:i + 1]).then_inc(free[bank], 1)
                if kind == "a_t":
                    act.wait_ge(full[bank], nth + 1)
                    if b >= 2 and step[2] == 0:
                        mb, mn = bank_of[("mix", b - 2, TILES - 1)]
                        act.wait_ge(full[mb], mn + 1)
                    act.activation(a_hi[:, b % 2, step[2]], ps[bank][:], ACT.Copy).then_inc(a_hi_done, 1)
                if kind in ("o_t", "x1_t", "x2_t"):
                    n, k = turn_no[step[:2]], step[2]
                    act.wait_ge(full[bank], nth + 1)
                    if n >= 2 and k == 0:
                        last = {"o_t": ("o_proj", TILES - 1), "x1_t": ("mix", TILES - 1), "x2_t": ("x2_w", TILES - 1)}
                        name, at = last[turns[n - 2][0]]
                        ub, un = bank_of[(name, turns[n - 2][1], at)]
                        act.wait_ge(full[ub], un + 1)
                    act.activation(t_hi[:, n % 2, k], ps[bank][:], ACT.Copy).then_inc(t_hi_done, 1)
                if kind == "logit":
                    act.wait_ge(full[bank], nth + 1)
                    if b:
                        lb, ln = bank_of[("logit_t", b - 1)]
                        act.wait_ge(full[lb], ln + 1)
                    act.activation(lg_sb[:], ps[bank][:], ACT.Copy).then_inc(free[bank], 1)

        @block.vector
        def _(dve):
            def low(src, hi, lo):
                dve.tensor_tensor(lo, src, hi.bitcast(F32), ALU.subtract).then_inc(w_lo_done, 1)

            def scale_map(step):
                n, i = en_no[step], step[2]
                dve.wait_ge(free[bank_of[step][0]], frees[step])
                dve.reciprocal(a_inv[:, i:i + 1], a_sum[:, i:i + 1]).then_inc(inv_done, 1)
                dve.wait_ge(inv_done, n + 1)
                dve.tensor_scalar(e_sb[:, i], e_sb[:, i], a_inv[:, i:i + 1], None, ALU.mult).then_inc(map_done, 1)

            dve.wait_ge(w_hi_done, 1)
            low(wx_raw[:], wx_hi[:], wx_lo[:])
            dve.wait_ge(w_hi_done, 2)
            low(x_sb[:, 1], wo_hi[:], wo_lo[:])
            dve.wait_ge(w_hi_done, 3)
            low(on_sb[:, 1], wf_hi[:], wf_lo[:])
            dve.wait_ge(w_hi_done, 4)
            low(g_raw[:], g_hi[:], g_lo[:])
            for at, step in enumerate(plan):
                kind, b = step[:2]
                bank, nth = bank_of[step]
                if kind in ("qx", "kx"):
                    n, w = lo_no[step], int(kind == "kx")
                    dve.wait_ge(qk_hi_done, n + 1)
                    dve.scalar_tensor_tensor(out=qk_lo[:, w], in0=ps[bank][:], scalar=bias[:, w:w + 1],
                                             in1=qk_hi[:, w].bitcast(F32), op0=ALU.add, op1=ALU.subtract).then_inc(free[bank], 1)
                if kind == "energy":
                    n, i = en_no[step], step[2]
                    dve.wait_ge(full[bank], nth + 1)
                    dve.tensor_reduce(n_mx[:, i:i + 1], ps[bank][:], AX.X, ALU.max, negate=True).then_inc(mx_done, 1)
                    if i:
                        scale_map(plan[at - 1])
                    if i == TILES - 1:
                        scale_map(step)
                if kind == "a_t":
                    dve.wait_ge(a_hi_done, KC * b + step[2] + 1)
                    dve.tensor_tensor(a_lo[:, b % 2, step[2]], ps[bank][:], a_hi[:, b % 2, step[2]].bitcast(F32),
                                      ALU.subtract).then_inc(a_lo_done, 1)
                if kind in ("o_t", "x1_t", "x2_t"):
                    n, k = turn_no[step[:2]], step[2]
                    dve.wait_ge(t_hi_done, KC * n + k + 1)
                    dve.tensor_tensor(t_lo[:, n % 2, k], ps[bank][:], t_hi[:, n % 2, k].bitcast(F32), ALU.subtract).then_inc(t_lo_done, 1)
                if kind in ("o_proj", "mix"):
                    n, i = norm_no[step[:2]], step[2]
                    tile = x_sb[:, b % 2, i]
                    dve.wait_ge(full[bank], nth + 1)
                    if kind == "o_proj" and i == 0:
                        dve.wait_ge(x_in[b % 2], 16 * (b // 2 + 1))
                    dve.tensor_tensor(tile, ps[bank][:], tile, ALU.add).then_inc(free[bank], 1)
                    dve.wait_ge(free[bank], frees[step])
                    dve.bn_stats(stats[:, i], tile).then_inc(stat_done, 1)
                    dve.wait_ge(stat_done, TILES * n + i + 1)
                    dve.bn_aggr(mv[:, n % 2, i], stats[:, i]).then_inc(agg_done, 1)
                    if i == TILES - 1:
                        dve.wait_ge(rstd_done, n + 1)
                        for m in range(TILES):
                            dve.tensor_scalar(x_sb[:, b % 2, m], x_sb[:, b % 2, m], mv[:, n % 2, m, 0:1], rstd[:, n % 2, m:m + 1],
                                              ALU.subtract, ALU.mult).then_inc(norm_done, 1)
                if kind == "x2_w":
                    dve.wait_ge(full[bank], nth + 1)
                    dve.tensor_tensor(base[:, TILES * b + step[2]], ps[bank][:], x_sb[:, b % 2, step[2]], ALU.add).then_inc(base_done, 1)
                if kind == "logit_t":
                    dve.wait_ge(full[bank], nth + 1)
                    dve.tensor_scalar(logits[:, TILES * b:TILES * (b + 1)], ps[bank][:].rearrange("p (i m) -> p i m", m=P)[:, :, 0:E],
                                      50.0, -50.0, ALU.min, ALU.max).then_inc(logit_done, 1)

        @block.tensor
        def _(pe):
            def freed(step):
                kind, b = step[:2]
                if kind == "a_t":
                    pe.wait_ge(a_lo_done, KC * b + step[2] + 1)
                elif kind in ("o_t", "x1_t", "x2_t"):
                    pe.wait_ge(t_lo_done, KC * turn_no[step[:2]] + step[2] + 1)
                elif kind == "x2_w":
                    pe.wait_ge(base_done, TILES * b + step[2] + 1)
                elif kind == "logit_t":
                    pe.wait_ge(logit_done, b + 1)
                else:
                    bank, nth = bank_of[step]
                    pe.wait_ge(free[bank], frees[step])

            for n, step in enumerate(plan):
                kind, b = step[:2]
                bank, nth = bank_of[step]
                out = ps[bank]
                if n >= 8:
                    freed(plan[n - 8])
                three = ((0, 0), (0, 1), (1, 0))
                if kind in ("qx", "kx"):
                    w = int(kind == "kx")
                    pe.wait_ge(w_lo_done, 1)
                    pe.wait_ge(c_lo_done, b + 1)
                    for m, (s, t, k) in enumerate((s, t, k) for s, t in three for k in range(CC)):
                        mm = pe.matmul(out[:], (wx_hi, wx_lo)[s][:, w, k], (c_hi, c_lo)[t][:, k], start=m == 0, stop=m == 3 * CC - 1)
                if kind == "energy":
                    i = step[2]
                    kb, kn = bank_of[("kx", b)]
                    pe.wait_ge(free[kb], frees[("kx", b)])
                    for m, (s, t) in enumerate(three):
                        mm = pe.matmul(out[:], (qk_hi, qk_lo)[s][:, 0, i * P:(i + 1) * P], (qk_hi, qk_lo)[t][:, 1], start=m == 0, stop=m == 2)
                if kind in ("o_t", "x1_t", "x2_t", "a_t"):
                    k = step[2]
                    if k == 0:
                        if kind == "a_t":
                            pe.wait_ge(map_done, TILES * (b + 1))
                        elif kind == "o_t":
                            pe.wait_ge(on_in[b % 2], 16 * (b // 2 + 1))
                        else:
                            pe.wait_ge(norm_done, TILES * (norm_no[("o_proj" if kind == "x1_t" else "mix", b)] + 1))
                    src = e_sb[:] if kind == "a_t" else (on_sb if kind == "o_t" else x_sb)[:, b % 2]
                    for i in range(TILES):
                        mm = pe.transpose(out[:, i * P:(i + 1) * P], src[:, i, k * P:(k + 1) * P], c.id_f[:])
                if kind in ("o_proj", "mix", "x2_w"):
                    i = step[2]
                    t = turn_no[({"o_proj": "o_t", "mix": "x1_t", "x2_w": "x2_t"}[kind], b)]
                    if i == 0:
                        pe.wait_ge(t_lo_done, KC * (t + 1))
                        pe.wait_ge(w_lo_done, 4)
                        if kind == "mix":
                            pe.wait_ge(a_lo_done, KC * (b + 1))
                    right = {"o_proj": (wo_hi, wo_lo), "x2_w": (wf_hi, wf_lo), "mix": (a_hi, a_lo)}[kind]
                    for m, (s, u, k) in enumerate((s, u, k) for s, u in three for k in range(KC)):
                        rhs = right[u][:, b % 2, k] if kind == "mix" else right[u][:, k]
                        mm = pe.matmul(out[:], (t_hi, t_lo)[s][:, t % 2, k, i * P:(i + 1) * P], rhs, start=m == 0, stop=m == 3 * KC - 1)
                if kind == "logit":
                    t = turn_no[("x2_t", b)]
                    pe.wait_ge(t_lo_done, KC * (t + 1))
                    for m, (s, u, k) in enumerate((s, u, k) for s, u in three for k in range(KC)):
                        mm = pe.matmul(out[:], (g_hi, g_lo)[s][:, k], (t_hi, t_lo)[u][:, t % 2, k], start=m == 0, stop=m == 3 * KC - 1)
                if kind == "logit_t":
                    lb, _ = bank_of[("logit", b)]
                    pe.wait_ge(free[lb], frees[("logit", b)])
                    for i in range(TILES):
                        mm = pe.transpose(out[:, i * P:(i + 1) * P], lg_sb[:, i * P:(i + 1) * P], c.id_f[:])
                mm.then_inc(full[bank], 1)


def experts(nc, c, s_dram, x2_dram, y_dram, base, logits, out):
    with ExitStack() as ctx:
        sb = lambda name, shape, dt: ctx.enter_context(nc.sbuf_tensor(name, shape, dt))
        sem = lambda name: ctx.enter_context(nc.semaphore(name))
        XG, Y, HALF = 4, 3, D // 2
        s_raw = sb("s_raw", [P, HALF * E], F32)
        s_hi, s_lo = sb("s_hi", [P, KC, E, D], F32R), sb("s_lo", [P, KC, E, D], F32R)
        xg = sb("xg", [P, XG, D], F32)
        l_hi, l_lo = sb("l_hi", [P, 2, D], F32R), sb("l_lo", [P, 2, D], F32R)
        y_sb = sb("y_sb", [P, Y, D], F32)
        yg = xg[:, 0:2]
        acc = s_raw[:].rearrange("p (n d) -> p n d", d=D)
        top, top_i = sb("top", [P, TT, 8], F32), sb("top_i", [P, TT, 8], mybir.dt.uint32)
        top_f = sb("top_f", [P, TT, 2], F32)
        i8, i128 = sb("i8", [P, E], F32), sb("i128", [P, P], F32)
        hot = sb("hot", [P, 2, TT, E], F32)
        sel = sb("sel", [P, TT, E], F32)
        keep = sb("keep", [P, E, TT], F32)
        tot, run = sb("tot", [P, E, TT], F32), sb("run", [P, E, TT], F32)
        rank, prod = sb("rank", [P, TT, E], F32), sb("prod", [P, TT, E], F32)
        tiles_i, tiles_f, ends, starts = sb("tiles_i", [P, E], I32), sb("tiles_f", [P, E], F32), sb("ends", [P, E], F32), sb("starts", [P, E], F32)
        slot_f, slot_i = sb("slot_f", [P, 2, TT], F32), sb("slot_i", [P, 2, TT], I32)
        lane_i, lane, tile_i, tile_f = sb("lane_i", [P, 2, TT], I32), sb("lane", [P, 2, TT], F32), sb("tile_i", [P, 2, TT], I32), sb("tile_f", [P, 2, TT], F32)
        past = sb("past", [P, J, E], F32)
        of_tile, of_tile_i = sb("of_tile", [P, J], F32), sb("of_tile_i", [P, J], I32)
        token = sb("token", [P, TT], F32)
        lane_hot = sb("lane_hot", [P, 4, P], F32)
        tile_hot = sb("tile_hot", [P, 4, J], F32)
        pair_token = sb("pair_token", [P, J], I32)
        gap, w_top = sb("gap", [P, TT], F32), sb("w_top", [P, 2, TT], F32)
        stats, mv = sb("stats_f", [P, 2, 6], F32), sb("mv_f", [P, TT, 2], F32)
        var_e, rstd, shift, m_half = sb("var_f", [P, TT], F32), sb("rstd_f", [P, TT], F32), sb("shift", [P, TT], F32), sb("m_half_f", [P, 1], F32)
        ps = [ctx.enter_context(nc.psum_tensor(f"ps_x{i}", [P, T], F32)) for i in range(8)]
        PS_T, PS_Y = ps[0:3], ps[3:6]
        ps_r, ps_k = ps[6], ps[7]

        s_in, s_hi_done, s_lo_done = sem("s_in"), sem("s_hi_done"), sem("s_lo_done")
        const, top_done, route, count_done, list_ready, list_done = (
            sem("x_const"), sem("top_done"), sem("route"), sem("count_done"), sem("list_ready"), sem("list_done"))
        gap_exp, tokens_ready = sem("gap_exp"), sem("tokens_ready")
        x_gathered = [sem(f"x_gathered{i}") for i in range(XG)]
        t_full, l_hi_done, l_lo_done, y_full, y_copied = (
            sem("t_full"), sem("l_hi_done"), sem("l_lo_done"), sem("y_full"), sem("y_copied"))
        y_stored = [sem(f"y_stored{i}") for i in range(Y)]
        y_gathered = [sem(f"y_gathered{i}") for i in range(2)]
        added, stat_done, agg_done, var_done, rstd_done, shift_done, fin_done = (
            sem("added"), sem("fstat_done"), sem("fagg_done"), sem("fvar_done"), sem("frstd_done"), sem("shift_done"), sem("fin_done"))
        out_stored = [sem(f"out_stored{i}") for i in range(4)]
        block = ctx.enter_context(nc.Block())

        @block.sync
        def _(sp):
            for k in range(2 * KC):
                if k:
                    sp.wait_ge(s_hi_done, k)
                    sp.wait_ge(s_lo_done, k)
                rows = s_dram[(k // 2) * P * D:(k // 2 + 1) * P * D].rearrange("(p r) e -> p (r e)", p=P)
                sp.dma_start(s_raw[:], rows[:, (k % 2) * HALF * E:(k % 2 + 1) * HALF * E]).then_inc(s_in, 16)
            for j in range(J):
                sp.wait_ge(y_copied, j + 1)
                sp.dma_start(y_dram[j * P:(j + 1) * P], y_sb[:, j % Y]).then_inc(y_stored[j % Y], 16)
            for i in range(TT):
                sp.wait_ge(fin_done, i + 1)
                sp.dma_start(out[i * P:(i + 1) * P], acc[:, i % 4]).then_inc(out_stored[i % 4], 16)
            for i in range(4):
                sp.wait_ge(out_stored[i], 16 * TT // 4)

        @block.gpsimd
        def _(pool):
            def norm_scale(pool, i):
                pool.wait_ge(var_done, i + 1)
                pool.tensor_tensor(rstd[:, i:i + 1], var_e[:, i:i + 1], m_half[:], ALU.pow).then_inc(rstd_done, 1)

            pool.iota(i8[:], pattern=[[1, E]], base=0, channel_multiplier=0, allow_small_or_imprecise_dtypes=True).then_inc(const, 1)
            pool.iota(i128[:], pattern=[[1, P]], base=0, channel_multiplier=0, allow_small_or_imprecise_dtypes=True).then_inc(const, 1)
            pool.iota(token[:], pattern=[[P, TT]], base=0, channel_multiplier=1, allow_small_or_imprecise_dtypes=True).then_inc(const, 1)
            pool.memset(m_half[:], -0.5).then_inc(const, 1)
            pool.wait_ge(tokens_ready, 1)
            for j in range(J):
                if j >= XG:
                    pool.wait_ge(t_full, j - XG + 1)
                pool.indirect_dma_start(out=xg[:, j % XG], out_offset=None, in_=x2_dram,
                                        in_offset=bass.IndirectOffsetOnAxis(ap=pair_token[:, j:j + 1], axis=0)
                                        ).then_inc(x_gathered[j % XG], 16)
            for i in range(Y):
                pool.wait_ge(y_stored[i], 16 * len(range(i, J, Y)))
            for i in range(TT):
                for n in range(2):
                    if i:
                        pool.wait_ge(added, 2 * (i - 1) + n + 1)
                    pool.indirect_dma_start(out=yg[:, n], out_offset=None, in_=y_dram,
                                            in_offset=bass.IndirectOffsetOnAxis(ap=slot_i[:, n, i:i + 1], axis=0)
                                            ).then_inc(y_gathered[n], 16)
                if i:
                    norm_scale(pool, i - 1)
            norm_scale(pool, TT - 1)

        @block.scalar
        def _(act):
            def copy_y(act, j):
                act.wait_ge(y_full, j + 1)
                if j >= Y:
                    act.wait_ge(y_stored[j % Y], 16 * (j // Y))
                act.activation(y_sb[:, j % Y], PS_Y[j % 3][:], ACT.Copy).then_inc(y_copied, 1)

            for k in range(2 * KC):
                act.wait_ge(s_in, 16 * (k + 1))
                act.activation(s_hi[:, k // 2, :, (k % 2) * HALF:(k % 2 + 1) * HALF], s_raw[:].rearrange("p (r e) -> p e r", e=E), ACT.Copy).then_inc(s_hi_done, 1)
                if k == 0:
                    act.wait_ge(top_done, 1)
                    act.activation(gap[:], gap[:], ACT.Exp).then_inc(gap_exp, 1)
            for j in range(J):
                act.wait_ge(t_full, j + 1)
                if j >= 2:
                    act.wait_ge(y_full, j - 1)
                act.activation(l_hi[:, j % 2], PS_T[j % 3][:], ACT.Copy).then_inc(l_hi_done, 1)
                if j:
                    copy_y(act, j - 1)
            copy_y(act, J - 1)
            for i in range(TT):
                act.wait_ge(shift_done, i + 1)
                act.activation(acc[:, i % 4], acc[:, i % 4], ACT.Identity, scale=rstd[:, i:i + 1], bias=shift[:, i:i + 1]).then_inc(fin_done, 1)

        @block.vector
        def _(dve):
            def norm_shift(dve, i):
                dve.wait_ge(rstd_done, i + 1)
                dve.scalar_tensor_tensor(out=shift[:, i:i + 1], in0=mv[:, i, 0:1], scalar=-1.0, in1=rstd[:, i:i + 1],
                                         op0=ALU.mult, op1=ALU.mult).then_inc(shift_done, 1)

            n = [0]

            def link(ins):
                n[0] += 1
                ins.then_inc(route, 1)
                dve.wait_ge(route, n[0])

            def low_s(k):
                dve.wait_ge(s_hi_done, k + 1)
                part = (slice(None), k // 2, slice(None), slice((k % 2) * HALF, (k % 2 + 1) * HALF))
                dve.tensor_tensor(s_lo[part], s_raw[:].rearrange("p (r e) -> p e r", e=E), s_hi[part].bitcast(F32),
                                  ALU.subtract).then_inc(s_lo_done, 1)

            for i in range(TT):
                link(dve.max(top[:, i], logits[:, i]))
                link(dve.max_index(top_i[:, i], top[:, i], logits[:, i]))
            dve.tensor_tensor(gap[:], top[:, :, 1], top[:, :, 0], ALU.subtract).then_inc(top_done, 1)
            dve.wait_ge(const, 4)
            link(dve.tensor_copy(top_f[:], top_i[:, :, 0:2]))
            for m in range(2):
                link(dve.tensor_tensor(hot[:, m], i8[:].unsqueeze(1).broadcast_to([P, TT, E]),
                                       top_f[:, :, m].unsqueeze(2).broadcast_to([P, TT, E]), ALU.is_equal))
            link(dve.tensor_tensor(sel[:], hot[:, 0], hot[:, 1], ALU.add))
            dve.sem_inc(list_ready, 1)
            link(dve.memset(keep[:], 1.0))
            link(dve.memset(keep[:, :, 0], 0.0))
            dve.wait_ge(count_done, 1)
            totals = ps_r[:, P:2 * P].rearrange("p (i e) -> p e i", e=E)
            link(dve.tensor_copy(tot[:], totals))
            link(dve.tensor_tensor_scan(run[:].rearrange("p e i -> p (e i)"), keep[:].rearrange("p e i -> p (e i)"),
                                        tot[:].rearrange("p e i -> p (e i)"), 0.0, ALU.mult, ALU.add))
            link(dve.tensor_scalar(tiles_f[:], run[:, :, TT - 1], float(P - 1), None, ALU.add))
            link(dve.tensor_copy(tiles_i[:], tiles_f[:]))
            link(dve.tensor_scalar(tiles_i[:], tiles_i[:], P.bit_length() - 1, None, ALU.logical_shift_right))
            link(dve.tensor_copy(tiles_f[:], tiles_i[:]))
            link(dve.tensor_tensor_scan(ends[:], c.ones[:, 0:E], tiles_f[:], 0.0, ALU.mult, ALU.add))
            link(dve.tensor_tensor(starts[:], ends[:], tiles_f[:], ALU.subtract))
            link(dve.tensor_tensor(run[:], run[:], tot[:], ALU.subtract))
            link(dve.scalar_tensor_tensor(out=run[:], in0=starts[:].unsqueeze(2).broadcast_to([P, E, TT]), scalar=float(P),
                                          in1=run[:], op0=ALU.mult, op1=ALU.add))
            link(dve.tensor_tensor(rank[:], ps_r[:, 0:P].rearrange("p (i e) -> p i e", e=E), run[:].rearrange("p e i -> p i e"), ALU.add))
            for m in range(2):
                link(dve.tensor_tensor(prod[:], rank[:], hot[:, m], ALU.mult))
                link(dve.tensor_reduce(slot_f[:, m], prod[:], AX.X, ALU.add))
            link(dve.tensor_copy(slot_i[:], slot_f[:]))
            link(dve.tensor_scalar(lane_i[:], slot_i[:], P - 1, None, ALU.bitwise_and))
            link(dve.tensor_scalar(tile_i[:], slot_i[:], P.bit_length() - 1, None, ALU.logical_shift_right))
            link(dve.tensor_copy(lane[:], lane_i[:]))
            link(dve.tensor_copy(tile_f[:], tile_i[:]))
            link(dve.tensor_tensor(past[:], i128[:, 0:J].unsqueeze(2).broadcast_to([P, J, E]),
                                   ends[:].unsqueeze(1).broadcast_to([P, J, E]), ALU.is_ge))
            link(dve.tensor_reduce(of_tile[:], past[:], AX.X, ALU.add))
            link(dve.tensor_scalar(of_tile[:], of_tile[:], float(E - 1), None, ALU.min))
            link(dve.tensor_copy(of_tile_i[:], of_tile[:]))
            for m in range(2):
                for i in range(TT):
                    u = m * TT + i
                    if u >= 4:
                        dve.wait_ge(list_done, u - 3)
                    dve.tensor_scalar(lane_hot[:, u % 4], i128[:], lane[:, m, i:i + 1], None, ALU.is_equal).then_inc(list_ready, 1)
                    dve.tensor_scalar(tile_hot[:, u % 4], i128[:, 0:J], tile_f[:, m, i:i + 1], token[:, i:i + 1],
                                      ALU.is_equal, ALU.mult).then_inc(list_ready, 1)
            dve.wait_ge(list_done, 2 * TT)
            dve.tensor_copy(pair_token[:], ps_k[:, 0:J]).then_inc(tokens_ready, 1)
            dve.wait_ge(gap_exp, 1)
            link(dve.tensor_scalar(w_top[:, 1], gap[:], 1.0, None, ALU.add))
            link(dve.reciprocal(w_top[:, 0], w_top[:, 1]))
            link(dve.tensor_tensor(w_top[:, 1], w_top[:, 0], gap[:], ALU.mult))
            for k in range(2 * KC):
                low_s(k)
            for j in range(J):
                dve.wait_ge(l_hi_done, j + 1)
                dve.tensor_tensor(l_lo[:, j % 2], PS_T[j % 3][:], l_hi[:, j % 2].bitcast(F32), ALU.subtract).then_inc(l_lo_done, 1)
            for i in range(TT):
                slot = acc[:, i % 4]
                if i >= 4:
                    dve.wait_ge(out_stored[i % 4], 16 * (i // 4))
                for m in range(2):
                    dve.wait_ge(y_gathered[m], 16 * (i + 1))
                    dve.scalar_tensor_tensor(out=slot, in0=yg[:, m], scalar=w_top[:, m, i:i + 1], in1=base[:, i] if m == 0 else slot,
                                             op0=ALU.mult, op1=ALU.add).then_inc(added, 1)
                    dve.wait_ge(added, 2 * i + m + 1)
                dve.bn_stats(stats[:, i % 2], slot).then_inc(stat_done, 1)
                dve.wait_ge(stat_done, i + 1)
                dve.bn_aggr(mv[:, i], stats[:, i % 2]).then_inc(agg_done, 1)
                dve.wait_ge(agg_done, i + 1)
                dve.tensor_scalar(var_e[:, i:i + 1], mv[:, i, 1:2], EPS, None, ALU.add).then_inc(var_done, 1)
                if i:
                    norm_shift(dve, i - 1)
            norm_shift(dve, TT - 1)

        @block.tensor
        def _(pe):
            pe.wait_ge(list_ready, 1)
            flat = sel[:].rearrange("p i e -> p (i e)")
            pe.matmul(ps_r[:, 0:P], c.before[:], flat, start=True, stop=True)
            pe.matmul(ps_r[:, P:2 * P], c.ones[:], flat, start=True, stop=True).then_inc(count_done, 1)
            for u in range(2 * TT):
                pe.wait_ge(list_ready, 2 * u + 3)
                pe.matmul(ps_k[:, 0:J], lane_hot[:, u % 4], tile_hot[:, u % 4], start=u == 0, stop=u == 2 * TT - 1).then_inc(list_done, 1)

            def turn(j):
                pe.wait_ge(x_gathered[j % XG], 16 * (j // XG + 1))
                if j >= 3:
                    pe.wait_ge(l_lo_done, j - 2)
                for k in range(KC):
                    mm = pe.transpose(PS_T[j % 3][:, k * P:(k + 1) * P], xg[:, j % XG, k * P:(k + 1) * P], c.id_f[:])
                mm.then_inc(t_full, 1)

            turn(0)
            pe.wait_ge(s_lo_done, 2 * KC)
            for j in range(J):
                if j + 1 < J:
                    turn(j + 1)
                expert = pe.value_load(of_tile_i[0:1, j:j + 1], min_val=0, max_val=E - 1)
                pe.wait_ge(l_lo_done, j + 1)
                if j >= 3:
                    pe.wait_ge(y_copied, j - 2)
                terms = [(s, u, k) for s, u in ((0, 0), (0, 1), (1, 0)) for k in range(KC)]
                for m, (s, u, k) in enumerate(terms):
                    right = (s_hi, s_lo)[u][:, k, bass.ds(expert, 1), :].rearrange("p o n -> p (o n)")
                    mm = pe.matmul(PS_Y[j % 3][:], (l_hi, l_lo)[s][:, j % 2, k * P:(k + 1) * P], right,
                                   start=m == 0, stop=m == len(terms) - 1)
                mm.then_inc(y_full, 1)


def decoder_layer(nc, a, out):
    dram = lambda name, shape, dt: nc.dram_tensor(name, shape, dt, kind="Internal").ap()
    parts_dram = dram("parts_dram", [2, ROUNDS, 3, FR, T], BF16)
    o_dram = dram("o_dram", [B, T, D], F32)
    s_dram = dram("s_dram", [D * D + NS, E], F32)
    x2_dram = dram("x2_dram", [TOK, D], F32)
    y_dram = dram("y_dram", [J * P, D], F32)
    with ExitStack() as ctx:
        c = Common(nc, ctx)
        entries(nc, c, a["idx_row"], a["idx_col"], a["atoms"], a["expert_atom_weights"], a["importance_t"])
        attention(nc, c, a["x_t"], a["wq_t"], a["wk_t"], a["wv_t"], parts_dram, o_dram, s_dram)
        base = ctx.enter_context(nc.sbuf_tensor("base", [P, TT, D], F32))
        logits = ctx.enter_context(nc.sbuf_tensor("logits", [P, TT, E], F32))
        cross(nc, c, a["x"], o_dram, a["ctx_t"], a["wxq_t"], a["wxk_t"], a["bxq"], a["bxk"], a["wo_t"], a["w_t"],
              a["gate_t"], x2_dram, base, logits)
        experts(nc, c, s_dram, x2_dram, y_dram, base, logits, out)


def kernel(x, ctx_1024, L0_attn_Wq, L0_attn_Wk, L0_attn_Wv, L0_attn_Wo, L0_xattn_Wq, L0_xattn_bq, L0_xattn_Wk,
           L0_xattn_bk, L0_ffn_gate_w, L0_ffn_W, L0_ffn_atoms, L0_ffn_expert_atom_weights, L0_ffn_importance,
           L0_ffn_mask_idx):
    import numpy as np
    import concourse.bacc as bacc
    from concourse.bass_utils import run_bass_kernel_spmd

    lay = np.ascontiguousarray
    n = lambda v: np.asarray(v)
    arrays = {
        "x": lay(n(x)), "x_t": lay(n(x).transpose(0, 2, 1)), "ctx_t": lay(n(ctx_1024).transpose(0, 2, 1)),
        "wq_t": lay(n(L0_attn_Wq).T), "wk_t": lay(n(L0_attn_Wk).T), "wv_t": lay(n(L0_attn_Wv).T), "wo_t": lay(n(L0_attn_Wo).T),
        "wxq_t": lay(n(L0_xattn_Wq).T), "wxk_t": lay(n(L0_xattn_Wk).T),
        "bxq": lay(n(L0_xattn_bq).reshape(DX, 1)), "bxk": lay(n(L0_xattn_bk).reshape(DX, 1)),
        "gate_t": lay(n(L0_ffn_gate_w).T), "w_t": lay(n(L0_ffn_W).T), "atoms": lay(n(L0_ffn_atoms)),
        "expert_atom_weights": lay(n(L0_ffn_expert_atom_weights)),
        "importance_t": lay(n(L0_ffn_importance).reshape(E, CHUNKS, P).transpose(2, 1, 0).reshape(P, CHUNKS * E)),
        "idx_row": lay(n(L0_ffn_mask_idx)), "idx_col": lay(n(L0_ffn_mask_idx).reshape(CHUNKS, P).T),
    }
    nc = bacc.Bacc("TRN2", target_bir_lowering=False, num_devices=1)
    a = {k: nc.dram_tensor(f"in_{k}", v.shape, mybir.dt.from_np(v.dtype), kind="ExternalInput").ap() for k, v in arrays.items()}
    out = nc.dram_tensor("out", [TOK, D], F32, kind="ExternalOutput").ap()
    decoder_layer(nc, a, out)
    r = run_bass_kernel_spmd(nc, [{f"in_{k}": v for k, v in arrays.items()}], core_ids=[0])
    return r.results[0]["out"].reshape(B, T, D)
```

```python
from contextlib import ExitStack

import concourse.bass as bass
from concourse import mybir

P = 128
B, T, D = 4, 512, 512
HEADS, DK = 32, 16
KC = D // P
TILES = T // P
PER_BATCH = 4
ROUNDS = PER_BATCH * B
HR = HEADS // PER_BATCH
STACKS = 4
FR = HR * DK
GROUPS = HR // 4
BLOCKS = 2 * TILES - 1
COLS = T + T - P
SLOTS = 8
C, DX = 256, 128
CC = C // P
E, ATOMS, NS = 8, 64, 4096
CHUNKS = NS // P
EG = 4
TOK = B * T
TT = TOK // P
J = 2 * TOK // P + E - 1
ZERO_COLS, ZERO_REP = 256, 4
ZERO_DMAS = D * D * E // (P * ZERO_COLS * ZERO_REP)
NEG = -1e30
EPS = 1e-5

F32 = mybir.dt.float32
F32R = mybir.dt.float32r
BF16 = mybir.dt.bfloat16
I32 = mybir.dt.int32
ALU = mybir.AluOpType
ACT = mybir.ActivationFunctionType
AX = mybir.AxisListType

Q_PART = (0, 0, 0, 1, 1, 2)
K_PART = (0, 1, 2, 0, 1, 0)
NP_ = len(Q_PART)
ROWS = NP_ * DK
MROWS = ROWS + 3


class Common:

    def __init__(self, nc, ctx):
        sb = lambda name, shape, dt: ctx.enter_context(nc.sbuf_tensor(name, shape, dt))
        self.id_f = sb("id_f", [P, P], F32)
        self.zeros = sb("zeros", [P, ZERO_COLS], F32)


def attention_plan():
    at = []
    for r in range(ROUNDS):
        t = HR * r
        at += [(t + n, "score_exp", r, n) for n in range(HR)]
        s_items = [(0, a) for a in range(HR // 4)] + [(i, a) for i in range(1, TILES) for a in range(HR // 2)]
        at += [(t - HR - 4.2 + HR * k / len(s_items), "score_max", r, *s) for k, s in enumerate(s_items)]
        at.append((t - 3.9, "max_t", r))
        at += [(t - 22.2, "proj_q", r), (t - 20.7, "proj_k", r)]
        if r % 2 == 0:
            at += [(t - 14.3 + n, "proj_v", r, n) for n in range(TILES)]
        if r % PER_BATCH == 0:
            at.append((t - 26.6, "split_x", r // PER_BATCH))
        for g in range(GROUPS):
            at += [(t + 4 * g + 5.6, "pv", r, g), (t + 4 * g + 7.3, "o_t", r, g)]
    at += [(1.6 + 1.6 * n, "zero", n) for n in range(ZERO_DMAS + 1)]
    at += [(19.1, "entry_in", 0), (21.1, "entry_w", 0)]
    for g in range(CHUNKS // EG):
        at += [(24.3 + 5 * g, "entry_v", g), (26.7 + 5 * g, "entry_s", g)]
        at += [(31.3 + 5 * g + n, "scatter", EG * g + n) for n in range(EG)]
    at.sort(key=lambda s: s[0])
    return [s[1:] for s in at], [s[0] for s in at]


def later(plan, times, kinds, others, by):
    out = []
    for at, step in enumerate(plan):
        time = times[at]
        if step[0] in kinds:
            sharing = [times[n] for n in range(at + 1, len(plan)) if plan[n][0] in kinds + others][:2]
            time = min([time + by] + [t - 0.01 for t in sharing[1:]])
        out.append((time, at, step))
    return [step for *_, step in sorted(out)]


def attention(nc, c, x_t, wq_t, wk_t, wv_t, parts_dram, o_dram, idx_row, idx_col, atoms, eaw, imp_t, s_dram):
    plan, times = attention_plan()
    general = [s for s in plan if s[0] in ("proj_q", "proj_k", "proj_v", "max_t", "o_t", "entry_w", "entry_v", "entry_s")]
    bank_of = {s: (n % 2, n // 2) for n, s in enumerate(general)}
    s_order = {s: n for n, s in enumerate(s for s in plan if s[0] == "score_max")}
    vector_plan = later(plan, times, ("proj_q", "proj_k", "o_t", "entry_v", "entry_s", "split_x"), ("proj_v", "max_t", "entry_w"), 0.9)
    p_order = {s: n for n, s in enumerate(s for s in plan if s[0] in ("proj_q", "proj_k"))}

    with ExitStack() as ctx:
        sb = lambda name, shape, dt: ctx.enter_context(nc.sbuf_tensor(name, shape, dt))
        sem = lambda name: ctx.enter_context(nc.semaphore(name))

        x_raw = sb("x_raw", [P, KC, T], F32)
        x_hi = sb("x_hi", [P, KC, T], F32R)
        x_lo = sb("x_lo", [P, KC, T], F32R)
        w_hi = sb("w_hi", [P, 3, KC, D], F32R)
        w_lo = sb("w_lo", [P, 3, KC, D], F32R)
        q_st = sb("q_st", [P, STACKS, HR, T], BF16)
        k_st = sb("k_st", [P, STACKS, HR, T], BF16)
        v_sb = sb("v_sb", [P, 2, TILES, 2 * HR, DK + 1], F32)
        probs = sb("probs", [P, SLOTS, COLS], F32)
        w_raw = probs[:, 0:7, :].rearrange("p s c -> p (s c)")[:, 0:3 * KC * D].rearrange("p (w k n) -> p w k n", w=3, k=KC)
        parts = sb("parts", [P, 2, 3, T], BF16)
        rest = sb("rest", [P, T], F32)
        o_sb = sb("o_sb", [P, T], F32)
        o_n = sb("o_n", [P, 2, TILES, FR], F32)
        r_den = sb("r_den", [P, 2, TILES, 4], F32)
        n_max = sb("n_max", [P, 2, HR, TILES], F32)
        masked = sb("masked", [P, 2, T], BF16)
        m_rest = sb("m_rest", [TILES * HR, P], F32)
        m_part = sb("m_part", [TILES * HR, 3, P], BF16)
        mask = sb("mask", [P, 2, P], BF16)

        mask_e = sb("mask_e", [P, 2, P], BF16)
        id_b = sb("id_b", [P, P], BF16)
        ones_b = sb("ones_b", [3, P], BF16)

        row_i = sb("row_i", [P, EG * P], I32)
        col_i, col_f = sb("col_i", [P, CHUNKS], I32), sb("col_f", [P, CHUNKS], F32)
        same = sb("same", [P, EG, P], F32)
        after = sb("after", [P, P], BF16)
        earlier = sb("earlier", [P, P], BF16)
        atom_sb = sb("atom_sb", [ATOMS, EG * P], F32)
        imp = sb("imp", [P, CHUNKS, E], F32)
        ew, ew_t = sb("ew", [E, ATOMS], F32), sb("ew_t", [ATOMS, E], F32)
        st = sb("st", [E, 4], F32)
        value = sb("value", [P, EG, E], F32)
        e_value = sb("e_value", [P, CHUNKS, E], F32)
        e_index = sb("e_index", [P, CHUNKS], I32)
        dup = sb("dup", [P, CHUNKS], F32)
        place_i, high_i = sb("place_i", [P, CHUNKS], I32), sb("high_i", [P, CHUNKS], I32)
        place, spare_i, spare = sb("place", [P, CHUNKS], F32), sb("spare_i", [P, CHUNKS], I32), sb("spare", [P, CHUNKS], F32)

        ps_g = [ctx.enter_context(nc.psum_tensor(f"ps_g{i}", [P, T], F32)) for i in range(2)]
        ps_s = [ctx.enter_context(nc.psum_tensor(f"ps_s{i}", [P, T], F32)) for i in range(2)]
        ps_e = [ctx.enter_context(nc.psum_tensor(f"ps_e{i}", [P, T], F32)) for i in range(3)]
        ps_o = ctx.enter_context(nc.psum_tensor("ps_o", [P, T], F32))

        w_loaded = [sem(f"w_loaded{i}") for i in range(3)]
        w_hi_done, w_lo_done = sem("w_hi_done"), sem("w_lo_done")
        x_loaded, x_hi_done = sem("x_loaded"), sem("x_hi_done")
        x_lo_done, x_lo_pool = sem("x_lo_done"), sem("x_lo_pool")
        const_done, ones_done, fill_done, o_cleared = sem("const_done"), sem("ones_done"), sem("fill_done"), sem("o_cleared")
        g_full = [sem(f"g_full{i}") for i in range(2)]
        g_free = [sem(f"g_free{i}") for i in range(2)]
        part1_done, rest_done, part2_done, part3_done = sem("part1_done"), sem("rest_done"), sem("part2_done"), sem("part3_done")
        part_stored = [sem(f"part_stored{i}") for i in range(2)]
        q_stacked = [sem(f"q_stacked{i}") for i in range(STACKS)]
        k_stacked = [sem(f"k_stacked{i}") for i in range(STACKS)]
        m_stacked = [sem(f"m_stacked{i}") for i in range(2)]
        s_full, s_max_done = sem("s_full"), sem("s_max_done")
        m_step, e_full, exp_done = sem("m_step"), sem("e_full"), sem("exp_done")
        pv_done, o_copied, den_done, norm_done = (
            sem("pv_done"), sem("o_copied"), sem("den_done"), sem("norm_done"))
        o_stored = [sem(f"o_stored{i}") for i in range(2)]
        eaw_in, imp_in, col_in, row_in, atoms_in = sem("eaw_in"), sem("imp_in"), sem("col_in"), sem("row_in"), sem("atoms_in")
        eaw_max, eaw_exp, imp_exp, soft_done = sem("eaw_max"), sem("eaw_exp"), sem("imp_exp"), sem("soft_done")
        entry_link, same_done, dup_done, entry_ready = sem("entry_link"), sem("same_done"), sem("dup_done"), sem("entry_ready")
        zeroed, entry_added = sem("zeroed"), sem("entry_added")

        block = ctx.enter_context(nc.Block())

        def wait_full(eng, step):
            bank, nth = bank_of[step]
            eng.wait_ge(g_full[bank], nth + 1)
            return ps_g[bank]

        def wait_free(eng, step):
            bank, nth = bank_of[step]
            eng.wait_ge(g_free[bank], nth + 1)

        @block.sync
        def _(sp):
            def load_stacks(r):
                if r >= STACKS:
                    sp.wait_ge(e_full, 2 * HR * (r - STACKS + 1))
                for i in range(2):
                    sp.wait_ge(part_stored[i], 16 * (r + 1))
                for src, repeat, first in ((0, 3, 0), (1, 2, 3), (2, 1, 5)):
                    rows = slice(first * DK, (first + repeat) * DK)
                    sp.dma_start(k_st[rows, r % STACKS], parts_dram[1, r, 0:repeat].rearrange("a (d h) t -> (a d) h t", d=DK)
                                 ).then_inc(k_stacked[r % STACKS], 16)
                    sp.dma_start(q_st[rows, r % STACKS], parts_dram[0, r, src].rearrange("(d h) t -> d h t", d=DK).unsqueeze(0)
                                 .broadcast_to([repeat, DK, HR, T])).then_inc(q_stacked[r % STACKS], 16)

            def load_entries(g):
                if g:
                    sp.wait_ge(same_done, g)
                sp.dma_start(row_i[:], idx_row[g * EG * P:(g + 1) * EG * P].partition_broadcast(P)).then_inc(row_in, 16)
                if g:
                    wait_full(sp, ("entry_v", g - 1))
                sp.dma_start(atom_sb[:], atoms[:, g * EG * P:(g + 1) * EG * P]).then_inc(atoms_in, 16)

            for i, w in enumerate((wq_t, wk_t, wv_t)):
                sp.dma_start(w_raw[:, i], w.rearrange("(k p) n -> p k n", p=P)).then_inc(w_loaded[i], 16)
                if i == 0:
                    sp.dma_start(x_raw[:], x_t[0].rearrange("(k p) t -> p k t", p=P)).then_inc(x_loaded, 16)
            sp.wait_ge(fill_done, 5)
            sp.dma_start(k_st[ROWS:MROWS].rearrange("o s h t -> o (s h t)").rearrange("o (n t) -> o n t", t=P),
                         ones_b[:].unsqueeze(1).broadcast_to([3, STACKS * HR * T // P, P])).then_inc(ones_done, 16)
            sp.dma_start(ew[:], eaw).then_inc(eaw_in, 16)
            sp.dma_start(imp[:].rearrange("p c e -> p (c e)"), imp_t).then_inc(imp_in, 16)
            sp.dma_start(col_i[:], idx_col).then_inc(col_in, 16)
            load_entries(0)
            for step in plan:
                kind, r = step[:2]
                if kind == "split_x" and r + 1 < B:
                    sp.wait_ge(x_hi_done, r + 1)
                    sp.wait_ge(x_lo_done, r + 1)
                    sp.wait_ge(x_lo_pool, r + 1)
                    sp.dma_start(x_raw[:], x_t[r + 1].rearrange("(k p) t -> p k t", p=P)).then_inc(x_loaded, 16)
                if kind in ("proj_q", "proj_k"):
                    no, which = p_order[step], int(kind == "proj_k")
                    sp.wait_ge(part3_done, no + 1)
                    sp.dma_start(parts_dram[which, r].rearrange("a p t -> p a t"), parts[:, no % 2]).then_inc(part_stored[no % 2], 16)
                    if which:
                        load_stacks(r)
                if kind == "max_t":
                    sp.wait_ge(m_step, 4 * (r + 1))
                    sp.wait_ge(q_stacked[r % STACKS], 16 * 3 * (r // STACKS + 1))
                    for n in range(3):
                        sp.dma_start(q_st[ROWS + n:ROWS + n + 1, r % STACKS].rearrange("o h (i t) -> o (h i) t", i=TILES),
                                     m_part[:, n]
                                     ).then_inc(m_stacked[r % 2], 16)
                if kind == "zero":
                    rows = D * D // ZERO_DMAS
                    if r < ZERO_DMAS:
                        sp.dma_start(s_dram[r * rows:(r + 1) * rows].rearrange("(p a b) e -> p a (b e)", p=P, a=ZERO_REP),
                                     c.zeros[:].unsqueeze(1).broadcast_to([P, ZERO_REP, ZERO_COLS])).then_inc(zeroed, 16)
                    else:
                        sp.dma_start(s_dram[D * D:].rearrange("(p b) e -> p (b e)", p=P), c.zeros[:, 0:CHUNKS * E]).then_inc(zeroed, 16)
                if kind == "entry_v" and r + 1 < CHUNKS // EG:
                    load_entries(r + 1)
                if kind == "o_t" and step[2] == GROUPS - 1:
                    sp.wait_ge(norm_done, GROUPS * (r + 1))
                    sp.dma_start(o_dram[r // PER_BATCH, :, (r % PER_BATCH) * FR:(r % PER_BATCH + 1) * FR].rearrange("(i p) f -> p i f", p=P),
                                 o_n[:, r % 2]).then_inc(o_stored[r % 2], 16)
            for i in range(2):
                sp.wait_ge(o_stored[i], 16 * ROUNDS // 2)
            sp.wait_ge(entry_added, 16 * CHUNKS)

        @block.gpsimd
        def _(pool):
            pool.memset(c.id_f[:], 0.0).then_inc(fill_done, 1)
            pool.memset(mask[:], 0.0).then_inc(fill_done, 1)
            pool.memset(after[:], 1.0).then_inc(fill_done, 1)
            pool.memset(mask_e[:], 0.0).then_inc(fill_done, 1)
            pool.memset(ones_b[:], 1.0).then_inc(fill_done, 1)
            pool.wait_ge(fill_done, 5)
            pool.affine_select(out=c.id_f[:], in_=c.id_f[:], compare_op=ALU.not_equal, fill=1.0, base=0,
                               pattern=[[-1, P]], channel_multiplier=1).then_inc(const_done, 1)
            pool.affine_select(out=mask[:, 0], in_=mask[:, 0], compare_op=ALU.is_ge, fill=NEG, base=0,
                               pattern=[[1, P]], channel_multiplier=-1).then_inc(const_done, 1)
            pool.affine_select(out=mask[:, 1], in_=mask[:, 1], compare_op=ALU.is_ge, fill=NEG, base=0,
                               pattern=[[-1, P]], channel_multiplier=1).then_inc(const_done, 1)
            pool.affine_select(out=mask_e[:, 0], in_=mask_e[:, 0], compare_op=ALU.is_ge, fill=NEG, base=0,
                               pattern=[[1, P]], channel_multiplier=-1).then_inc(const_done, 1)
            pool.affine_select(out=mask_e[:, 1], in_=mask_e[:, 1], compare_op=ALU.is_ge, fill=NEG, base=0,
                               pattern=[[-1, P]], channel_multiplier=1).then_inc(const_done, 1)
            pool.affine_select(out=after[:], in_=after[:], compare_op=ALU.is_ge, fill=0.0, base=-1,
                               pattern=[[-1, P]], channel_multiplier=1).then_inc(const_done, 1)
            pool.wait_ge(const_done, 6)
            pool.memset(c.zeros[:], 0.0).then_inc(const_done, 1)
            pool.iota(spare_i[:], pattern=[[P, CHUNKS]], base=D * D, channel_multiplier=1).then_inc(const_done, 1)
            pool.memset(v_sb[:, :, :, :, DK:DK + 1], 1.0).then_inc(const_done, 1)
            pool.tensor_copy(id_b[:], c.id_f[:]).then_inc(const_done, 1)
            for step in plan:
                kind, r = step[:2]
                if kind == "scatter":
                    if r == 0:
                        pool.wait_ge(zeroed, 16 * (ZERO_DMAS + 1))
                    else:
                        pool.wait_ge(entry_added, 16 * r)
                    pool.wait_ge(entry_ready, r // EG + 1)
                    pool.indirect_dma_start(out=s_dram, out_offset=bass.IndirectOffsetOnAxis(ap=e_index[:, r:r + 1], axis=0),
                                            in_=e_value[:, r], in_offset=None, compute_op=ALU.add).then_inc(entry_added, 16)
                if kind == "split_x":
                    pool.wait_ge(x_hi_done, r + 1)
                    pool.tensor_tensor(x_lo[:, KC - 1], x_raw[:, KC - 1], x_hi[:, KC - 1].bitcast(F32), ALU.subtract).then_inc(x_lo_pool, 1)

        @block.scalar
        def _(act):
            for i in range(3):
                act.wait_ge(w_loaded[i], 16)
                act.activation(w_hi[:, i], w_raw[:, i], ACT.Copy).then_inc(w_hi_done, 1)
                if i == 0:
                    act.wait_ge(x_loaded, 16)
                    act.activation(x_hi[:], x_raw[:], ACT.Copy).then_inc(x_hi_done, 1)
            for step in plan:
                kind, r = step[:2]
                if kind == "split_x" and r:
                    act.wait_ge(x_loaded, 16 * (r + 1))
                    wait_full(act, ("proj_v", PER_BATCH * r - 2, TILES - 1))
                    act.activation(x_hi[:], x_raw[:], ACT.Copy).then_inc(x_hi_done, 1)
                if kind in ("proj_q", "proj_k"):
                    no, scale = p_order[step], DK ** -0.5 if kind == "proj_q" else 1.0
                    ps = wait_full(act, step)
                    if no >= 2:
                        act.wait_ge(part_stored[no % 2], 16 * (no // 2))
                    act.activation(parts[:, no % 2, 0], ps[:], ACT.Copy, scale=scale).then_inc(part1_done, 1)
                if kind == "proj_v":
                    ps = wait_full(act, step)
                    if r == 0 and step[2] == 0:
                        act.wait_ge(const_done, 10)
                    act.activation(v_sb[:, r // 2 % 2, step[2], :, 0:DK], ps[:, 0:2 * FR].rearrange("p (h d) -> p h d", d=DK),
                                   ACT.Copy).then_inc(g_free[bank_of[step][0]], 1)
                if kind == "entry_in":
                    act.wait_ge(eaw_max, 1)
                    act.activation(ew[:], ew[:], ACT.Exp, bias=st[:, 0:1], accum_out=st[:, 1:2]).then_inc(eaw_exp, 1)
                    act.wait_ge(imp_in, 16)
                    act.activation(imp[:], imp[:], ACT.Exp, scale=-1.0).then_inc(imp_exp, 1)
                if kind == "score_exp":
                    head = HR * r + step[2]
                    if head == 0:
                        act.wait_ge(w_lo_done, 3)
                    if head >= SLOTS:
                        act.wait_ge(pv_done, (head - SLOTS) // 4 + 1)
                    for half, (c0, c1) in enumerate(((0, T), (T, COLS))):
                        e = 2 * head + half
                        act.wait_ge(e_full, e + 1)
                        act.activation(probs[:, head % SLOTS, c0:c1], ps_e[e % 3][:, 0:c1 - c0], ACT.Exp).then_inc(exp_done, 1)
                if kind == "pv":
                    g = GROUPS * r + step[2]
                    act.wait_ge(pv_done, g + 1)
                    if g >= 1:
                        wait_full(act, ("o_t", (g - 1) // GROUPS, (g - 1) % GROUPS))
                    act.activation(o_sb[:], ps_o[:], ACT.Copy).then_inc(o_copied, 1)

        @block.vector
        def _(dve):
            links = [0]

            def link(ins):
                links[0] += 1
                ins.then_inc(entry_link, 1)
                dve.wait_ge(entry_link, links[0])

            dve.memset(ps_o[:], 0.0).then_inc(o_cleared, 1)
            for i in range(3):
                dve.wait_ge(w_hi_done, i + 1)
                dve.tensor_tensor(w_lo[:, i], w_raw[:, i], w_hi[:, i].bitcast(F32), ALU.subtract).then_inc(w_lo_done, 1)
                if i == 0:
                    dve.wait_ge(x_hi_done, 1)
                    dve.tensor_tensor(x_lo[:, :-1], x_raw[:, :-1], x_hi[:, :-1].bitcast(F32), ALU.subtract).then_inc(x_lo_done, 1)
            for step in vector_plan:
                kind, r = step[:2]
                if kind == "split_x" and r:
                    dve.wait_ge(x_hi_done, r + 1)
                    dve.tensor_tensor(x_lo[:, :-1], x_raw[:, :-1], x_hi[:, :-1].bitcast(F32), ALU.subtract).then_inc(x_lo_done, 1)
                if kind in ("proj_q", "proj_k"):
                    no, scale = p_order[step], DK ** -0.5 if kind == "proj_q" else 1.0
                    slot = no % 2
                    ps = ps_g[bank_of[step][0]]
                    dve.wait_ge(part1_done, no + 1)
                    if no:
                        dve.wait_ge(part3_done, no)
                    dve.scalar_tensor_tensor(out=rest[:], in0=ps[:], scalar=scale, in1=parts[:, slot, 0],
                                             op0=ALU.mult, op1=ALU.subtract).then_inc(g_free[bank_of[step][0]], 1)
                    wait_free(dve, step)
                    dve.tensor_copy(parts[:, slot, 1], rest[:]).then_inc(part2_done, 1)
                    dve.wait_ge(part2_done, no + 1)
                    dve.tensor_tensor(parts[:, slot, 2], rest[:], parts[:, slot, 1], ALU.subtract).then_inc(part3_done, 1)
                if kind == "score_max":
                    s, (i, a) = s_order[step], step[2:]
                    per = 4 if i == 0 else 2
                    width = T // per
                    if s == 0:
                        dve.wait_ge(const_done, 10)
                    dve.wait_ge(s_full, s + 1)
                    if r >= 2 and (i, a) == (0, 0):
                        wait_full(dve, ("max_t", r - 2))
                    if s >= 2:
                        dve.wait_ge(s_max_done, s - 1)
                    for n in range(per):
                        h = per * a + n
                        last = dve.tensor_tensor_reduce(
                            out=masked[:, s % 2, n * width:(n + 1) * width], in0=ps_s[s % 2][:, n * width:(n + 1) * width],
                            in1=mask[:].rearrange("p w k -> p (w k)")[:, 2 * P - width:], scale=-1.0, scalar=-NEG,
                            op0=ALU.add, op1=ALU.min, accum_out=n_max[:, r % 2, h, i:i + 1])
                    last.then_inc(s_max_done, 1)
                if kind == "max_t":
                    ps, (bank, nth) = wait_full(dve, step), bank_of[step]
                    if r:
                        dve.wait_ge(m_stacked[(r - 1) % 2], 48 * ((r - 1) // 2 + 1))
                    n = TILES * HR
                    dve.tensor_copy(m_part[:, 0], ps[0:n, 0:P]).then_inc(m_step, 1)
                    dve.wait_ge(m_step, 4 * r + 1)
                    dve.tensor_tensor(m_rest[:], ps[0:n, 0:P], m_part[:, 0], ALU.subtract).then_inc(g_free[bank], 1)
                    wait_free(dve, step)
                    dve.tensor_copy(m_part[:, 1], m_rest[:]).then_inc(m_step, 1)
                    dve.wait_ge(m_step, 4 * r + 2)
                    dve.tensor_tensor(m_part[:, 2], m_rest[:], m_part[:, 1], ALU.subtract).then_inc(m_step, 2)
                if kind == "entry_in":
                    dve.wait_ge(eaw_in, 16)
                    dve.tensor_reduce(st[:, 0:1], ew[:], AX.X, ALU.max, negate=True).then_inc(eaw_max, 1)
                if kind == "entry_w":
                    dve.wait_ge(eaw_exp, 1)
                    link(dve.reciprocal(st[:, 2:3], st[:, 1:2]))
                    dve.tensor_scalar(ew[:], ew[:], st[:, 2:3], None, ALU.mult).then_inc(soft_done, 1)
                    dve.wait_ge(imp_exp, 1)
                    link(dve.tensor_scalar(imp[:], imp[:], 1.0, None, ALU.add))
                    link(dve.reciprocal(imp[:], imp[:]))
                    dve.wait_ge(col_in, 16)
                    link(dve.tensor_copy(col_f[:], col_i[:]))
                    link(dve.tensor_scalar(place_i[:], col_i[:], D - 1, D.bit_length() - 1, ALU.bitwise_and, ALU.logical_shift_left))
                    link(dve.tensor_scalar(high_i[:], col_i[:], D.bit_length() - 1, None, ALU.logical_shift_right))
                    link(dve.tensor_copy(place[:], high_i[:]))
                    link(dve.tensor_copy(spare[:], place_i[:]))
                    link(dve.tensor_tensor(place[:], place[:], spare[:], ALU.add))
                    link(dve.tensor_copy(spare[:], spare_i[:]))
                    link(dve.tensor_tensor(spare[:], spare[:], place[:], ALU.subtract))
                    ps = wait_full(dve, step)
                    dve.tensor_copy(ew_t[:], ps[0:ATOMS, 0:E]).then_inc(g_free[bank_of[step][0]], 1)
                if kind == "entry_v":
                    dve.wait_ge(row_in, 16 * (r + 1))
                    if r:
                        wait_full(dve, ("entry_s", r - 1))
                    dve.tensor_tensor(same[:], row_i[:].rearrange("p (c s) -> p c s", s=P),
                                      col_f[:, EG * r:EG * (r + 1)].unsqueeze(2).broadcast_to([P, EG, P]), ALU.is_equal).then_inc(same_done, 1)
                    ps = wait_full(dve, step)
                    dve.tensor_tensor(value[:].rearrange("p c e -> p (c e)"), ps[:, 0:EG * E],
                                      imp[:, EG * r:EG * (r + 1)].rearrange("p c e -> p (c e)"), ALU.mult).then_inc(g_free[bank_of[step][0]], 1)
                    dve.wait_ge(same_done, r + 1)
                    for n in range(EG):
                        if EG * r + n:
                            dve.wait_ge(dup_done, EG * r + n)
                        dve.tensor_tensor_reduce(out=earlier[:], in0=same[:, n], in1=after[:], scale=1.0, scalar=0.0, op0=ALU.mult,
                                                 op1=ALU.max, accum_out=dup[:, EG * r + n:EG * r + n + 1]).then_inc(dup_done, 1)
                if kind == "entry_s":
                    own = slice(EG * r, EG * (r + 1))
                    ps = wait_full(dve, step)
                    dve.tensor_copy(e_value[:, own].rearrange("p c e -> p (c e)"), ps[:, 0:EG * E]).then_inc(g_free[bank_of[step][0]], 1)
                    dve.wait_ge(dup_done, EG * (r + 1))
                    link(dve.tensor_tensor(dup[:, own], dup[:, own], spare[:, own], ALU.mult))
                    wait_free(dve, step)
                    dve.tensor_tensor(e_index[:, own], dup[:, own], place[:, own], ALU.add).then_inc(entry_ready, 1)
                if kind == "o_t":
                    g = GROUPS * r + step[2]
                    ps, (bank, nth) = wait_full(dve, step), bank_of[step]
                    heads = ps[:].rearrange("p (i h c) -> p i h c", i=TILES, h=4)
                    dve.reciprocal(r_den[:, g % 2], heads[:, :, :, DK]).then_inc(den_done, 1)
                    if r >= 2 and step[2] == 0:
                        dve.wait_ge(o_stored[r % 2], 16 * (r // 2))
                    dve.wait_ge(den_done, g + 1)
                    for i in range(TILES):
                        last = dve.tensor_tensor(
                            o_n[:, r % 2, i, step[2] * 64:(step[2] + 1) * 64].rearrange("p (h d) -> p h d", h=4),
                            heads[:, i, :, 0:DK], r_den[:, g % 2, i].unsqueeze(2).broadcast_to([P, 4, DK]), ALU.mult)
                        if i == TILES - 1:
                            last.then_inc(norm_done, 1)
                    dve.wait_ge(norm_done, g + 1)
                    dve.sem_inc(g_free[bank], 1)

        @block.tensor
        def _(pe):
            def take_bank(step):
                bank, nth = bank_of[step]
                if nth:
                    pe.wait_ge(g_free[bank], nth)
                return ps_g[bank], g_full[bank]

            pe.wait_ge(const_done, 10)
            for step in plan:
                kind, r = step[:2]
                if kind in ("proj_q", "proj_k", "proj_v"):
                    w = ("proj_q", "proj_k", "proj_v").index(kind)
                    pe.wait_ge(w_lo_done, w + 1)
                    pe.wait_ge(x_lo_done, r // PER_BATCH + 1)
                    pe.wait_ge(x_lo_pool, r // PER_BATCH + 1)
                    ps, full = take_bank(step)
                    terms = [(a, b, k) for a, b in ((0, 0), (0, 1), (1, 0)) for k in range(KC)]
                    for n, (a, b, k) in enumerate(terms):
                        wt, xt = (w_hi, w_lo)[a], (x_hi, x_lo)[b]
                        f0 = (r % PER_BATCH) * FR
                        if kind == "proj_v":
                            mm = pe.matmul(ps[:, 0:2 * FR], xt[:, k, step[2] * P:(step[2] + 1) * P], wt[:, w, k, f0:f0 + 2 * FR],
                                           start=n == 0, stop=n == len(terms) - 1)
                        else:
                            mm = pe.matmul(ps[:], wt[:, w, k, f0:f0 + P], xt[:, k], start=n == 0, stop=n == len(terms) - 1)
                    mm.then_inc(full, 1)
                if kind == "score_max":
                    s, (i, a) = s_order[step], step[2:]
                    if (i, a) == (0, 0):
                        pe.wait_ge(q_stacked[r % STACKS], 16 * 3 * (r // STACKS + 1))
                        pe.wait_ge(k_stacked[r % STACKS], 16 * 3 * (r // STACKS + 1))
                    if s >= 2:
                        pe.wait_ge(s_max_done, s - 1)
                    ps, per = ps_s[s % 2], 4 if i == 0 else 2
                    width = T // per
                    for n in range(per):
                        h = per * a + n
                        mm = pe.matmul(ps[:, n * width:(n + 1) * width], q_st[0:ROWS, r % STACKS, h, i * P:(i + 1) * P],
                                       k_st[0:ROWS, r % STACKS, h, (i + 1) * P - width:(i + 1) * P], start=True, stop=True)
                    mm.then_inc(s_full, 1)
                if kind == "max_t":
                    ps, full = take_bank(step)
                    pe.wait_ge(s_max_done, (r + 1) * len(s_order) // ROUNDS)
                    pe.transpose(ps[0:TILES * HR, 0:P], n_max[:, r % 2].rearrange("p h i -> p (h i)"), c.id_f[:]).then_inc(full, 1)
                if kind == "score_exp":
                    h = step[2]
                    if r == 0 and h == 0:
                        pe.wait_ge(ones_done, 16)
                    if h == 0:
                        pe.wait_ge(m_stacked[r % 2], 48 * (r // 2 + 1))
                    for half in range(2):
                        e = 2 * (HR * r + h) + half
                        if e >= 3:
                            pe.wait_ge(exp_done, e - 2)
                        for j in (2 * half, 2 * half + 1):
                            c0, width = 2 * P * (j % 2), min(2 * P, T - j * P)
                            mm = pe.matmul(ps_e[e % 3][:, c0:c0 + width], k_st[0:MROWS, r % STACKS, h, j * P:(j + 1) * P],
                                           q_st[0:MROWS, r % STACKS, h, j * P:j * P + width], start=j % 2 == 0, stop=False,
                                           skip_group_check=True)
                        c1 = c0 + width
                        right = mask_e[:].rearrange("p w q -> p (w q)")
                        if c1 == T:
                            right = right.unsqueeze(1).broadcast_to([P, 2, 2 * P])
                            mm = pe.matmul(ps_e[e % 3][:].rearrange("p (a w) -> p a w", a=2), id_b[:], right, start=False, stop=True, skip_group_check=True)
                        else:
                            for a0, width in ((0, 2 * P), (2 * P, P)):
                                mm = pe.matmul(ps_e[e % 3][:, a0:a0 + width], id_b[:], right[:, 0:width], start=False,
                                               stop=True, skip_group_check=True)
                        mm.then_inc(e_full, 1)
                if kind == "entry_w":
                    ps, full = take_bank(step)
                    pe.wait_ge(soft_done, 1)
                    pe.transpose(ps[0:ATOMS, 0:E], ew[:], c.id_f[0:E, 0:E]).then_inc(full, 1)
                if kind == "entry_v":
                    ps, full = take_bank(step)
                    pe.wait_ge(atoms_in, 16 * (r + 1))
                    if r == 0:
                        wait_free(pe, ("entry_w", 0))
                    for n in range(EG):
                        mm = pe.matmul(ps[:, n * E:(n + 1) * E], atom_sb[:, n * P:(n + 1) * P], ew_t[:], start=True, stop=True)
                    mm.then_inc(full, 1)
                if kind == "entry_s":
                    ps, full = take_bank(step)
                    pe.wait_ge(same_done, r + 1)
                    wait_free(pe, ("entry_v", r))
                    for n in range(EG):
                        mm = pe.matmul(ps[:, n * E:(n + 1) * E], same[:, n], value[:, n], start=True, stop=True)
                    mm.then_inc(full, 1)
                if kind == "pv":
                    g = GROUPS * r + step[2]
                    pe.wait_ge(exp_done, 8 * (g + 1))
                    if g == 0:
                        pe.wait_ge(o_cleared, 1)
                    if g:
                        pe.wait_ge(o_copied, g)
                    for j in range(TILES):
                        width = min(2 * P, T - j * P)
                        for n in range(4):
                            h = 4 * step[2] + n
                            mm = pe.matmul(ps_o[32 * n:32 * n + DK + 1, j * P:j * P + width], v_sb[:, r // 2 % 2, j, r % 2 * HR + h],
                                           probs[:, (HR * r + h) % SLOTS, 2 * P * j:2 * P * j + width],
                                           start=j == 0, stop=True, skip_group_check=True)
                    mm.then_inc(pv_done, 1)
                if kind == "o_t":
                    g = GROUPS * r + step[2]
                    ps, full = take_bank(step)
                    pe.wait_ge(o_copied, g + 1)
                    for i in range(TILES):
                        mm = pe.transpose(ps[:, i * P:(i + 1) * P], o_sb[:, i * P:(i + 1) * P], c.id_f[:])
                    mm.then_inc(full, 1)


def cross_plan():
    def maps(b):
        return [("qx", b), ("kx", b)] + rows("energy", b) + turned("a_t", b)

    def turned(kind, b):
        return [(kind, b, k) for k in range(KC)]

    def rows(kind, b):
        return [(kind, b, i) for i in range(TILES)]

    plan = maps(0) + turned("o_t", 0) + rows("o_proj", 0)
    for b in range(B):
        more = b + 1 < B
        if more:
            plan += maps(b + 1)
        plan += turned("x1_t", b) + rows("mix", b)
        if more:
            plan += turned("o_t", b + 1) + rows("o_proj", b + 1)
        plan += turned("x2_t", b) + [("logit", b)] + rows("x2_w", b) + [("logit_t", b)]
    return plan


def cross(nc, c, x, o_dram, ctx_t, wxq_t, wxk_t, bxq, bxk, wo_t, w_t, gate_t, x2_dram, base, logits):
    plan = cross_plan()
    bank_of = {s: (n % 8, n // 8) for n, s in enumerate(plan)}
    turns = [s[:2] for s in plan if s[0] in ("o_t", "x1_t", "x2_t") and s[2] == 0]
    turn_no = {s: n for n, s in enumerate(turns)}
    lo_no = {s: n for n, s in enumerate(s for s in plan if s[0] in ("qx", "kx"))}
    en_no = {s: n for n, s in enumerate(s for s in plan if s[0] == "energy")}

    with ExitStack() as ctx:
        sb = lambda name, shape, dt: ctx.enter_context(nc.sbuf_tensor(name, shape, dt))
        sem = lambda name: ctx.enter_context(nc.semaphore(name))
        wo_hi, wo_lo = sb("wo_hi", [P, KC, D], F32R), sb("wo_lo", [P, KC, D], F32R)
        wf_hi, wf_lo = sb("wf_hi", [P, KC, D], F32R), sb("wf_lo", [P, KC, D], F32R)
        wx_raw = sb("wx_raw", [P, 2, CC, DX], F32)
        wx_hi, wx_lo = sb("wx_hi", [P, 2, CC, DX], F32R), sb("wx_lo", [P, 2, CC, DX], F32R)
        g_raw = sb("g_raw", [P, KC, P], F32)
        g_hi, g_lo = sb("g_hi", [P, KC, P], F32R), sb("g_lo", [P, KC, P], F32R)
        bias = sb("bias_x", [P, 2], F32)
        x_sb = sb("x_sb", [P, 2, TILES, D], F32)
        on_sb = sb("on_sb", [P, 2, TILES, D], F32)
        t_hi, t_lo = sb("t_hi", [P, 2, KC, T], F32R), sb("t_lo", [P, 2, KC, T], F32R)
        c_raw = sb("c_raw", [P, CC, T], F32)
        c_hi, c_lo = sb("c_hi", [P, CC, T], F32R), sb("c_lo", [P, CC, T], F32R)
        qk_hi, qk_lo = sb("qk_hi", [P, 2, T], F32R), sb("qk_lo", [P, 2, T], F32R)
        e_sb = sb("e_sb", [P, TILES, T], F32)
        a_hi, a_lo = sb("a_hi", [P, 2, TILES, T], F32R), sb("a_lo", [P, 2, TILES, T], F32R)
        n_mx = sb("n_mx", [P, TILES], F32)
        a_sum, a_inv = sb("a_sum", [P, TILES], F32), sb("a_inv", [P, TILES], F32)
        stats = sb("stats", [P, TILES, 6], F32)
        mv = sb("mv", [P, 2, TILES, 2], F32)
        var_e, rstd, m_half = sb("var_e", [P, 2, TILES], F32), sb("rstd", [P, 2, TILES], F32), sb("m_half", [P, TILES], F32)
        lg_sb = sb("lg_sb", [P, T], F32)
        ps = [ctx.enter_context(nc.psum_tensor(f"ps_c{i}", [P, T], F32)) for i in range(8)]

        wo_in, wf_in, wx_in, g_in = sem("wo_in"), sem("wf_in"), sem("wx_in"), sem("g_in")
        w_hi_done, w_lo_done, half_done = sem("cw_hi_done"), sem("cw_lo_done"), sem("half_done")
        full = [sem(f"c_full{i}") for i in range(8)]
        free = [sem(f"c_free{i}") for i in range(8)]
        x_in = [sem(f"x_in{i}") for i in range(2)]
        on_in = [sem(f"on_in{i}") for i in range(2)]
        c_in, c_hi_done, c_lo_done = sem("c_in"), sem("c_hi_done"), sem("c_lo_done")
        qk_hi_done, qk_lo_done = sem("qk_hi_done"), sem("qk_lo_done")
        mx_done, map_done, a_hi_done, a_lo_done, inv_done = (
            sem("mx_done"), sem("map_done"), sem("a_hi_done"), sem("a_lo_done"), sem("inv_done"))
        t_hi_done, t_lo_done = sem("t_hi_done"), sem("t_lo_done")
        stat_done, agg_done, var_done, rstd_done, norm_done = (
            sem("stat_done"), sem("agg_done"), sem("var_done"), sem("rstd_done"), sem("cnorm_done"))
        x2_stored, base_done, lg_done, logit_done = sem("x2_stored"), sem("base_done"), sem("lg_done"), sem("logit_done")
        block = ctx.enter_context(nc.Block())

        norms = [s[:2] for s in plan if s[0] in ("o_proj", "mix") and s[2] == 0]
        norm_no = {s: n for n, s in enumerate(norms)}
        frees, count = {}, [0] * 8
        for step in plan:
            bank = bank_of[step][0]
            count[bank] += step[0] in ("qx", "kx", "energy", "o_proj", "mix", "logit")
            frees[step] = count[bank]

        @block.sync
        def _(sp):
            sp.dma_start(wx_raw[:, 0], wxq_t.rearrange("(k p) n -> p k n", p=P)).then_inc(wx_in, 16)
            sp.dma_start(wx_raw[:, 1], wxk_t.rearrange("(k p) n -> p k n", p=P)).then_inc(wx_in, 16)
            sp.dma_start(bias[:, 0:1], bxq).then_inc(wx_in, 16)
            sp.dma_start(bias[:, 1:2], bxk).then_inc(wx_in, 16)
            sp.dma_start(c_raw[:], ctx_t[0].rearrange("(k p) t -> p k t", p=P)).then_inc(c_in, 16)
            sp.dma_start(on_sb[:, 0], o_dram[0].rearrange("(i p) f -> p i f", p=P)).then_inc(on_in[0], 16)
            sp.dma_start(x_sb[:, 1], wo_t.rearrange("(k p) n -> p k n", p=P)).then_inc(wo_in, 16)
            sp.dma_start(x_sb[:, 0], x[0].rearrange("(i p) f -> p i f", p=P)).then_inc(x_in[0], 16)
            sp.dma_start(on_sb[:, 1], w_t.rearrange("(k p) n -> p k n", p=P)).then_inc(wf_in, 16)
            sp.dma_start(g_raw[:, :, 0:E], gate_t.rearrange("(k p) e -> p k e", p=P)).then_inc(g_in, 16)
            sp.wait_ge(w_lo_done, 4)
            sp.dma_start(on_sb[:, 1], o_dram[1].rearrange("(i p) f -> p i f", p=P)).then_inc(on_in[1], 16)
            sp.dma_start(x_sb[:, 1], x[1].rearrange("(i p) f -> p i f", p=P)).then_inc(x_in[1], 16)
            for step in plan:
                kind, b = step[:2]
                if kind == "kx" and b + 1 < B:
                    sp.wait_ge(c_lo_done, b + 1)
                    sp.dma_start(c_raw[:], ctx_t[b + 1].rearrange("(k p) t -> p k t", p=P)).then_inc(c_in, 16)
                if kind == "mix" and step[2] == TILES - 1:
                    sp.wait_ge(norm_done, TILES * (norm_no[("mix", b)] + 1))
                    sp.dma_start(x2_dram[b * T:(b + 1) * T].rearrange("(i p) f -> p i f", p=P), x_sb[:, b % 2]).then_inc(x2_stored, 16)
                if kind == "o_proj" and step[2] == TILES - 1 and b + 2 < B:
                    sp.wait_ge(t_lo_done, KC * (turn_no[("o_t", b)] + 1))
                    sp.dma_start(on_sb[:, b % 2], o_dram[b + 2].rearrange("(i p) f -> p i f", p=P)).then_inc(on_in[b % 2], 16)
                if kind == "x2_w" and step[2] == TILES - 1 and b + 2 < B:
                    sp.wait_ge(base_done, TILES * (b + 1))
                    sp.wait_ge(x2_stored, 16 * (b + 1))
                    sp.dma_start(x_sb[:, b % 2], x[b + 2].rearrange("(i p) f -> p i f", p=P)).then_inc(x_in[b % 2], 16)
            sp.wait_ge(x2_stored, 16 * B)

        @block.gpsimd
        def _(pool):
            pool.memset(g_raw[:, :, E:P], 0.0).then_inc(half_done, 1)
            pool.memset(m_half[:], -0.5).then_inc(half_done, 1)
            pool.wait_ge(half_done, 2)
            for step in plan:
                kind, b = step[:2]
                if kind == "qx":
                    pool.wait_ge(c_hi_done, b + 1)
                    pool.tensor_tensor(c_lo[:], c_raw[:], c_hi[:].bitcast(F32), ALU.subtract).then_inc(c_lo_done, 1)
                if kind in ("o_proj", "mix") and step[2] == TILES - 1:
                    n = norm_no[step[:2]]
                    pool.wait_ge(agg_done, TILES * (n + 1))
                    pool.tensor_scalar(var_e[:, n % 2], mv[:, n % 2, :, 1], EPS, None, ALU.add).then_inc(var_done, 1)
                    pool.wait_ge(var_done, n + 1)
                    pool.tensor_tensor(rstd[:, n % 2], var_e[:, n % 2], m_half[:], ALU.pow).then_inc(rstd_done, 1)

        @block.scalar
        def _(act):
            def weights(n, src, hi, loaded, count):
                act.wait_ge(loaded, count)
                act.activation(hi, src, ACT.Copy).then_inc(w_hi_done, 1)

            weights(0, wx_raw[:], wx_hi[:], wx_in, 64)
            act.wait_ge(c_in, 16)
            act.activation(c_hi[:], c_raw[:], ACT.Copy).then_inc(c_hi_done, 1)
            weights(1, x_sb[:, 1], wo_hi[:], wo_in, 16)
            weights(2, on_sb[:, 1], wf_hi[:], wf_in, 16)
            act.wait_ge(half_done, 2)
            weights(3, g_raw[:], g_hi[:], g_in, 16)
            for step in plan:
                kind, b = step[:2]
                bank, nth = bank_of[step]
                if kind in ("qx", "kx"):
                    n, w = lo_no[step], int(kind == "kx")
                    act.wait_ge(full[bank], nth + 1)
                    if b and not w:
                        eb, en = bank_of[("energy", b - 1, TILES - 1)]
                        act.wait_ge(full[eb], en + 1)
                    act.activation(qk_hi[:, w], ps[bank][:], ACT.Identity, bias=bias[:, w:w + 1]).then_inc(qk_hi_done, 1)
                    if w and b + 1 < B:
                        act.wait_ge(c_in, 16 * (b + 2))
                        act.activation(c_hi[:], c_raw[:], ACT.Copy).then_inc(c_hi_done, 1)
                if kind == "energy":
                    n, i = en_no[step], step[2]
                    act.wait_ge(mx_done, n + 1)
                    if b and i == 0:
                        tb, tn = bank_of[("a_t", b - 1, KC - 1)]
                        act.wait_ge(full[tb], tn + 1)
                    act.activation(e_sb[:, i], ps[bank][:], ACT.Exp, bias=n_mx[:, i:i + 1],
                                   accum_out=a_sum[:, i:i + 1]).then_inc(free[bank], 1)
                if kind == "a_t":
                    act.wait_ge(full[bank], nth + 1)
                    if b >= 2 and step[2] == 0:
                        mb, mn = bank_of[("mix", b - 2, TILES - 1)]
                        act.wait_ge(full[mb], mn + 1)
                    act.activation(a_hi[:, b % 2, step[2]], ps[bank][:], ACT.Copy).then_inc(a_hi_done, 1)
                if kind in ("o_t", "x1_t", "x2_t"):
                    n, k = turn_no[step[:2]], step[2]
                    act.wait_ge(full[bank], nth + 1)
                    if n >= 2 and k == 0:
                        last = {"o_t": ("o_proj", TILES - 1), "x1_t": ("mix", TILES - 1), "x2_t": ("x2_w", TILES - 1)}
                        name, at = last[turns[n - 2][0]]
                        ub, un = bank_of[(name, turns[n - 2][1], at)]
                        act.wait_ge(full[ub], un + 1)
                    act.activation(t_hi[:, n % 2, k], ps[bank][:], ACT.Copy).then_inc(t_hi_done, 1)
                if kind == "logit":
                    act.wait_ge(full[bank], nth + 1)
                    if b:
                        lb, ln = bank_of[("logit_t", b - 1)]
                        act.wait_ge(full[lb], ln + 1)
                    act.activation(lg_sb[:], ps[bank][:], ACT.Copy).then_inc(free[bank], 1)

        @block.vector
        def _(dve):
            def low(src, hi, lo):
                dve.tensor_tensor(lo, src, hi.bitcast(F32), ALU.subtract).then_inc(w_lo_done, 1)

            def scale_map(step):
                n, i = en_no[step], step[2]
                dve.wait_ge(free[bank_of[step][0]], frees[step])
                dve.reciprocal(a_inv[:, i:i + 1], a_sum[:, i:i + 1]).then_inc(inv_done, 1)
                dve.wait_ge(inv_done, n + 1)
                dve.tensor_scalar(e_sb[:, i], e_sb[:, i], a_inv[:, i:i + 1], None, ALU.mult).then_inc(map_done, 1)

            dve.wait_ge(w_hi_done, 1)
            low(wx_raw[:], wx_hi[:], wx_lo[:])
            dve.wait_ge(w_hi_done, 2)
            low(x_sb[:, 1], wo_hi[:], wo_lo[:])
            dve.wait_ge(w_hi_done, 3)
            low(on_sb[:, 1], wf_hi[:], wf_lo[:])
            dve.wait_ge(w_hi_done, 4)
            low(g_raw[:], g_hi[:], g_lo[:])
            for at, step in enumerate(plan):
                kind, b = step[:2]
                bank, nth = bank_of[step]
                if kind in ("qx", "kx"):
                    n, w = lo_no[step], int(kind == "kx")
                    dve.wait_ge(qk_hi_done, n + 1)
                    dve.scalar_tensor_tensor(out=qk_lo[:, w], in0=ps[bank][:], scalar=bias[:, w:w + 1],
                                             in1=qk_hi[:, w].bitcast(F32), op0=ALU.add, op1=ALU.subtract).then_inc(free[bank], 1)
                if kind == "energy":
                    n, i = en_no[step], step[2]
                    dve.wait_ge(full[bank], nth + 1)
                    dve.tensor_reduce(n_mx[:, i:i + 1], ps[bank][:], AX.X, ALU.max, negate=True).then_inc(mx_done, 1)
                    if i:
                        scale_map(plan[at - 1])
                    if i == TILES - 1:
                        scale_map(step)
                if kind == "a_t":
                    dve.wait_ge(a_hi_done, KC * b + step[2] + 1)
                    dve.tensor_tensor(a_lo[:, b % 2, step[2]], ps[bank][:], a_hi[:, b % 2, step[2]].bitcast(F32),
                                      ALU.subtract).then_inc(a_lo_done, 1)
                if kind in ("o_t", "x1_t", "x2_t"):
                    n, k = turn_no[step[:2]], step[2]
                    dve.wait_ge(t_hi_done, KC * n + k + 1)
                    dve.tensor_tensor(t_lo[:, n % 2, k], ps[bank][:], t_hi[:, n % 2, k].bitcast(F32), ALU.subtract).then_inc(t_lo_done, 1)
                if kind in ("o_proj", "mix"):
                    n, i = norm_no[step[:2]], step[2]
                    tile = x_sb[:, b % 2, i]
                    dve.wait_ge(full[bank], nth + 1)
                    if kind == "o_proj" and i == 0:
                        dve.wait_ge(x_in[b % 2], 16 * (b // 2 + 1))
                    dve.tensor_tensor(tile, ps[bank][:], tile, ALU.add).then_inc(free[bank], 1)
                    dve.wait_ge(free[bank], frees[step])
                    dve.bn_stats(stats[:, i], tile).then_inc(stat_done, 1)
                    dve.wait_ge(stat_done, TILES * n + i + 1)
                    dve.bn_aggr(mv[:, n % 2, i], stats[:, i]).then_inc(agg_done, 1)
                    if i == TILES - 1:
                        dve.wait_ge(rstd_done, n + 1)
                        for m in range(TILES):
                            dve.tensor_scalar(x_sb[:, b % 2, m], x_sb[:, b % 2, m], mv[:, n % 2, m, 0:1], rstd[:, n % 2, m:m + 1],
                                              ALU.subtract, ALU.mult).then_inc(norm_done, 1)
                if kind == "x2_w":
                    dve.wait_ge(full[bank], nth + 1)
                    dve.tensor_tensor(base[:, TILES * b + step[2]], ps[bank][:], x_sb[:, b % 2, step[2]], ALU.add).then_inc(base_done, 1)
                if kind == "logit_t":
                    dve.wait_ge(full[bank], nth + 1)
                    dve.tensor_scalar(logits[:, TILES * b:TILES * (b + 1)], ps[bank][:].rearrange("p (i m) -> p i m", m=P)[:, :, 0:E],
                                      50.0, -50.0, ALU.min, ALU.max).then_inc(logit_done, 1)

        @block.tensor
        def _(pe):
            def freed(step):
                kind, b = step[:2]
                if kind == "a_t":
                    pe.wait_ge(a_lo_done, KC * b + step[2] + 1)
                elif kind in ("o_t", "x1_t", "x2_t"):
                    pe.wait_ge(t_lo_done, KC * turn_no[step[:2]] + step[2] + 1)
                elif kind == "x2_w":
                    pe.wait_ge(base_done, TILES * b + step[2] + 1)
                elif kind == "logit_t":
                    pe.wait_ge(logit_done, b + 1)
                else:
                    bank, nth = bank_of[step]
                    pe.wait_ge(free[bank], frees[step])

            for n, step in enumerate(plan):
                kind, b = step[:2]
                bank, nth = bank_of[step]
                out = ps[bank]
                if n >= 8:
                    freed(plan[n - 8])
                three = ((0, 0), (0, 1), (1, 0))
                if kind in ("qx", "kx"):
                    w = int(kind == "kx")
                    pe.wait_ge(w_lo_done, 1)
                    pe.wait_ge(c_lo_done, b + 1)
                    for m, (s, t, k) in enumerate((s, t, k) for s, t in three for k in range(CC)):
                        mm = pe.matmul(out[:], (wx_hi, wx_lo)[s][:, w, k], (c_hi, c_lo)[t][:, k], start=m == 0, stop=m == 3 * CC - 1)
                if kind == "energy":
                    i = step[2]
                    kb, kn = bank_of[("kx", b)]
                    pe.wait_ge(free[kb], frees[("kx", b)])
                    for m, (s, t) in enumerate(three):
                        mm = pe.matmul(out[:], (qk_hi, qk_lo)[s][:, 0, i * P:(i + 1) * P], (qk_hi, qk_lo)[t][:, 1], start=m == 0, stop=m == 2)
                if kind in ("o_t", "x1_t", "x2_t", "a_t"):
                    k = step[2]
                    if k == 0:
                        if kind == "a_t":
                            pe.wait_ge(map_done, TILES * (b + 1))
                        elif kind == "o_t":
                            pe.wait_ge(on_in[b % 2], 16 * (b // 2 + 1))
                        else:
                            pe.wait_ge(norm_done, TILES * (norm_no[("o_proj" if kind == "x1_t" else "mix", b)] + 1))
                    src = e_sb[:] if kind == "a_t" else (on_sb if kind == "o_t" else x_sb)[:, b % 2]
                    for i in range(TILES):
                        mm = pe.transpose(out[:, i * P:(i + 1) * P], src[:, i, k * P:(k + 1) * P], c.id_f[:])
                if kind in ("o_proj", "mix", "x2_w"):
                    i = step[2]
                    t = turn_no[({"o_proj": "o_t", "mix": "x1_t", "x2_w": "x2_t"}[kind], b)]
                    if i == 0:
                        pe.wait_ge(t_lo_done, KC * (t + 1))
                        pe.wait_ge(w_lo_done, 4)
                        if kind == "mix":
                            pe.wait_ge(a_lo_done, KC * (b + 1))
                    right = {"o_proj": (wo_hi, wo_lo), "x2_w": (wf_hi, wf_lo), "mix": (a_hi, a_lo)}[kind]
                    for m, (s, u, k) in enumerate((s, u, k) for s, u in three for k in range(KC)):
                        rhs = right[u][:, b % 2, k] if kind == "mix" else right[u][:, k]
                        mm = pe.matmul(out[:], (t_hi, t_lo)[s][:, t % 2, k, i * P:(i + 1) * P], rhs, start=m == 0, stop=m == 3 * KC - 1)
                if kind == "logit":
                    t = turn_no[("x2_t", b)]
                    pe.wait_ge(t_lo_done, KC * (t + 1))
                    for m, (s, u, k) in enumerate((s, u, k) for s, u in three for k in range(KC)):
                        mm = pe.matmul(out[:], (g_hi, g_lo)[s][:, k], (t_hi, t_lo)[u][:, t % 2, k], start=m == 0, stop=m == 3 * KC - 1)
                if kind == "logit_t":
                    lb, _ = bank_of[("logit", b)]
                    pe.wait_ge(free[lb], frees[("logit", b)])
                    for i in range(TILES):
                        mm = pe.transpose(out[:, i * P:(i + 1) * P], lg_sb[:, i * P:(i + 1) * P], c.id_f[:])
                mm.then_inc(full[bank], 1)


def experts(nc, c, s_dram, x2_dram, y_dram, base, logits, out):
    with ExitStack() as ctx:
        sb = lambda name, shape, dt: ctx.enter_context(nc.sbuf_tensor(name, shape, dt))
        sem = lambda name: ctx.enter_context(nc.semaphore(name))
        XG, Y, HALF = 4, 3, D // 2
        s_raw = sb("s_raw", [P, HALF * E], F32)
        s_hi, s_lo = sb("s_hi", [P, KC, E, D], F32R), sb("s_lo", [P, KC, E, D], F32R)
        xg = sb("xg", [P, XG, D], F32)
        l_hi, l_lo = sb("l_hi", [P, 2, D], F32R), sb("l_lo", [P, 2, D], F32R)
        y_sb = sb("y_sb", [P, Y, D], F32)
        yg = xg[:, 0:2]
        acc = s_raw[:].rearrange("p (n d) -> p n d", d=D)
        top, top_i = sb("top", [P, TT, 8], F32), sb("top_i", [P, TT, 8], mybir.dt.uint32)
        top_f = sb("top_f", [P, TT, 2], F32)
        before, ones = sb("before", [P, P], F32), sb("ones", [P, P], F32)
        i8, i128 = sb("i8", [P, E], F32), sb("i128", [P, P], F32)
        hot = sb("hot", [P, 2, TT, E], F32)
        sel = sb("sel", [P, TT, E], F32)
        keep = sb("keep", [P, E, TT], F32)
        tot, run = sb("tot", [P, E, TT], F32), sb("run", [P, E, TT], F32)
        rank, prod = sb("rank", [P, TT, E], F32), sb("prod", [P, TT, E], F32)
        tiles_i, tiles_f, ends, starts = sb("tiles_i", [P, E], I32), sb("tiles_f", [P, E], F32), sb("ends", [P, E], F32), sb("starts", [P, E], F32)
        slot_f, slot_i = sb("slot_f", [P, 2, TT], F32), sb("slot_i", [P, 2, TT], I32)
        lane_i, lane, tile_i, tile_f = sb("lane_i", [P, 2, TT], I32), sb("lane", [P, 2, TT], F32), sb("tile_i", [P, 2, TT], I32), sb("tile_f", [P, 2, TT], F32)
        past = sb("past", [P, J, E], F32)
        of_tile, of_tile_i = sb("of_tile", [P, J], F32), sb("of_tile_i", [P, J], I32)
        token = sb("token", [P, TT], F32)
        lane_hot = sb("lane_hot", [P, 4, P], F32)
        tile_hot = sb("tile_hot", [P, 4, J], F32)
        pair_token = sb("pair_token", [P, J], I32)
        gap, w_top = sb("gap", [P, TT], F32), sb("w_top", [P, 2, TT], F32)
        stats, mv = sb("stats_f", [P, 2, 6], F32), sb("mv_f", [P, TT, 2], F32)
        var_e, rstd, shift, m_half = sb("var_f", [P, TT], F32), sb("rstd_f", [P, TT], F32), sb("shift", [P, TT], F32), sb("m_half_f", [P, 1], F32)
        ps = [ctx.enter_context(nc.psum_tensor(f"ps_x{i}", [P, T], F32)) for i in range(8)]
        PS_T, PS_Y = ps[0:3], ps[3:6]
        ps_r, ps_k = ps[6], ps[7]

        s_in, s_hi_done, s_lo_done = sem("s_in"), sem("s_hi_done"), sem("s_lo_done")
        const, top_done, route, count_done, list_ready, list_done = (
            sem("x_const"), sem("top_done"), sem("route"), sem("count_done"), sem("list_ready"), sem("list_done"))
        gap_exp, tokens_ready = sem("gap_exp"), sem("tokens_ready")
        x_gathered = [sem(f"x_gathered{i}") for i in range(XG)]
        t_full, l_hi_done, l_lo_done, y_full, y_copied = (
            sem("t_full"), sem("l_hi_done"), sem("l_lo_done"), sem("y_full"), sem("y_copied"))
        y_stored = [sem(f"y_stored{i}") for i in range(Y)]
        y_gathered = [sem(f"y_gathered{i}") for i in range(2)]
        added, stat_done, agg_done, var_done, rstd_done, shift_done, fin_done = (
            sem("added"), sem("fstat_done"), sem("fagg_done"), sem("fvar_done"), sem("frstd_done"), sem("shift_done"), sem("fin_done"))
        out_stored = [sem(f"out_stored{i}") for i in range(4)]
        block = ctx.enter_context(nc.Block())

        @block.sync
        def _(sp):
            for k in range(2 * KC):
                if k:
                    sp.wait_ge(s_hi_done, k)
                    sp.wait_ge(s_lo_done, k)
                rows = s_dram[(k // 2) * P * D:(k // 2 + 1) * P * D].rearrange("(p r) e -> p (r e)", p=P)
                sp.dma_start(s_raw[:], rows[:, (k % 2) * HALF * E:(k % 2 + 1) * HALF * E]).then_inc(s_in, 16)
            for j in range(J):
                sp.wait_ge(y_copied, j + 1)
                sp.dma_start(y_dram[j * P:(j + 1) * P], y_sb[:, j % Y]).then_inc(y_stored[j % Y], 16)
            for i in range(TT):
                sp.wait_ge(fin_done, i + 1)
                sp.dma_start(out[i * P:(i + 1) * P], acc[:, i % 4]).then_inc(out_stored[i % 4], 16)
            for i in range(4):
                sp.wait_ge(out_stored[i], 16 * TT // 4)

        @block.gpsimd
        def _(pool):
            def norm_scale(pool, i):
                pool.wait_ge(var_done, i + 1)
                pool.tensor_tensor(rstd[:, i:i + 1], var_e[:, i:i + 1], m_half[:], ALU.pow).then_inc(rstd_done, 1)

            pool.iota(i8[:], pattern=[[1, E]], base=0, channel_multiplier=0, allow_small_or_imprecise_dtypes=True).then_inc(const, 1)
            pool.iota(i128[:], pattern=[[1, P]], base=0, channel_multiplier=0, allow_small_or_imprecise_dtypes=True).then_inc(const, 1)
            pool.iota(token[:], pattern=[[P, TT]], base=0, channel_multiplier=1, allow_small_or_imprecise_dtypes=True).then_inc(const, 1)
            pool.memset(m_half[:], -0.5).then_inc(const, 1)
            pool.memset(ones[:], 1.0).then_inc(const, 1)
            pool.memset(before[:], 1.0).then_inc(const, 1)
            pool.wait_ge(const, 6)
            pool.affine_select(out=before[:], in_=before[:], compare_op=ALU.is_ge, fill=0.0, base=-1,
                               pattern=[[1, P]], channel_multiplier=-1).then_inc(const, 1)
            pool.wait_ge(tokens_ready, 1)
            for j in range(J):
                if j >= XG:
                    pool.wait_ge(t_full, j - XG + 1)
                pool.indirect_dma_start(out=xg[:, j % XG], out_offset=None, in_=x2_dram,
                                        in_offset=bass.IndirectOffsetOnAxis(ap=pair_token[:, j:j + 1], axis=0)
                                        ).then_inc(x_gathered[j % XG], 16)
            for i in range(Y):
                pool.wait_ge(y_stored[i], 16 * len(range(i, J, Y)))
            for i in range(TT):
                for n in range(2):
                    if i:
                        pool.wait_ge(added, 2 * (i - 1) + n + 1)
                    pool.indirect_dma_start(out=yg[:, n], out_offset=None, in_=y_dram,
                                            in_offset=bass.IndirectOffsetOnAxis(ap=slot_i[:, n, i:i + 1], axis=0)
                                            ).then_inc(y_gathered[n], 16)
                if i:
                    norm_scale(pool, i - 1)
            norm_scale(pool, TT - 1)

        @block.scalar
        def _(act):
            def copy_y(act, j):
                act.wait_ge(y_full, j + 1)
                if j >= Y:
                    act.wait_ge(y_stored[j % Y], 16 * (j // Y))
                act.activation(y_sb[:, j % Y], PS_Y[j % 3][:], ACT.Copy).then_inc(y_copied, 1)

            for k in range(2 * KC):
                act.wait_ge(s_in, 16 * (k + 1))
                act.activation(s_hi[:, k // 2, :, (k % 2) * HALF:(k % 2 + 1) * HALF], s_raw[:].rearrange("p (r e) -> p e r", e=E), ACT.Copy).then_inc(s_hi_done, 1)
                if k == 0:
                    act.wait_ge(top_done, 1)
                    act.activation(gap[:], gap[:], ACT.Exp).then_inc(gap_exp, 1)
            for j in range(J):
                act.wait_ge(t_full, j + 1)
                if j >= 2:
                    act.wait_ge(y_full, j - 1)
                act.activation(l_hi[:, j % 2], PS_T[j % 3][:], ACT.Copy).then_inc(l_hi_done, 1)
                if j:
                    copy_y(act, j - 1)
            copy_y(act, J - 1)
            for i in range(TT):
                act.wait_ge(shift_done, i + 1)
                act.activation(acc[:, i % 4], acc[:, i % 4], ACT.Identity, scale=rstd[:, i:i + 1], bias=shift[:, i:i + 1]).then_inc(fin_done, 1)

        @block.vector
        def _(dve):
            def norm_shift(dve, i):
                dve.wait_ge(rstd_done, i + 1)
                dve.scalar_tensor_tensor(out=shift[:, i:i + 1], in0=mv[:, i, 0:1], scalar=-1.0, in1=rstd[:, i:i + 1],
                                         op0=ALU.mult, op1=ALU.mult).then_inc(shift_done, 1)

            n = [0]

            def link(ins):
                n[0] += 1
                ins.then_inc(route, 1)
                dve.wait_ge(route, n[0])

            def low_s(k):
                dve.wait_ge(s_hi_done, k + 1)
                part = (slice(None), k // 2, slice(None), slice((k % 2) * HALF, (k % 2 + 1) * HALF))
                dve.tensor_tensor(s_lo[part], s_raw[:].rearrange("p (r e) -> p e r", e=E), s_hi[part].bitcast(F32),
                                  ALU.subtract).then_inc(s_lo_done, 1)

            for i in range(TT):
                link(dve.max(top[:, i], logits[:, i]))
                link(dve.max_index(top_i[:, i], top[:, i], logits[:, i]))
            dve.tensor_tensor(gap[:], top[:, :, 1], top[:, :, 0], ALU.subtract).then_inc(top_done, 1)
            dve.wait_ge(const, 7)
            link(dve.tensor_copy(top_f[:], top_i[:, :, 0:2]))
            for m in range(2):
                link(dve.tensor_tensor(hot[:, m], i8[:].unsqueeze(1).broadcast_to([P, TT, E]),
                                       top_f[:, :, m].unsqueeze(2).broadcast_to([P, TT, E]), ALU.is_equal))
            link(dve.tensor_tensor(sel[:], hot[:, 0], hot[:, 1], ALU.add))
            dve.sem_inc(list_ready, 1)
            link(dve.memset(keep[:], 1.0))
            link(dve.memset(keep[:, :, 0], 0.0))
            dve.wait_ge(count_done, 1)
            totals = ps_r[:, P:2 * P].rearrange("p (i e) -> p e i", e=E)
            link(dve.tensor_copy(tot[:], totals))
            link(dve.tensor_tensor_scan(run[:].rearrange("p e i -> p (e i)"), keep[:].rearrange("p e i -> p (e i)"),
                                        tot[:].rearrange("p e i -> p (e i)"), 0.0, ALU.mult, ALU.add))
            link(dve.tensor_scalar(tiles_f[:], run[:, :, TT - 1], float(P - 1), None, ALU.add))
            link(dve.tensor_copy(tiles_i[:], tiles_f[:]))
            link(dve.tensor_scalar(tiles_i[:], tiles_i[:], P.bit_length() - 1, None, ALU.logical_shift_right))
            link(dve.tensor_copy(tiles_f[:], tiles_i[:]))
            link(dve.tensor_tensor_scan(ends[:], ones[:, 0:E], tiles_f[:], 0.0, ALU.mult, ALU.add))
            link(dve.tensor_tensor(starts[:], ends[:], tiles_f[:], ALU.subtract))
            link(dve.tensor_tensor(run[:], run[:], tot[:], ALU.subtract))
            link(dve.scalar_tensor_tensor(out=run[:], in0=starts[:].unsqueeze(2).broadcast_to([P, E, TT]), scalar=float(P),
                                          in1=run[:], op0=ALU.mult, op1=ALU.add))
            link(dve.tensor_tensor(rank[:], ps_r[:, 0:P].rearrange("p (i e) -> p i e", e=E), run[:].rearrange("p e i -> p i e"), ALU.add))
            for m in range(2):
                link(dve.tensor_tensor(prod[:], rank[:], hot[:, m], ALU.mult))
                link(dve.tensor_reduce(slot_f[:, m], prod[:], AX.X, ALU.add))
            link(dve.tensor_copy(slot_i[:], slot_f[:]))
            link(dve.tensor_scalar(lane_i[:], slot_i[:], P - 1, None, ALU.bitwise_and))
            link(dve.tensor_scalar(tile_i[:], slot_i[:], P.bit_length() - 1, None, ALU.logical_shift_right))
            link(dve.tensor_copy(lane[:], lane_i[:]))
            link(dve.tensor_copy(tile_f[:], tile_i[:]))
            link(dve.tensor_tensor(past[:], i128[:, 0:J].unsqueeze(2).broadcast_to([P, J, E]),
                                   ends[:].unsqueeze(1).broadcast_to([P, J, E]), ALU.is_ge))
            link(dve.tensor_reduce(of_tile[:], past[:], AX.X, ALU.add))
            link(dve.tensor_scalar(of_tile[:], of_tile[:], float(E - 1), None, ALU.min))
            link(dve.tensor_copy(of_tile_i[:], of_tile[:]))
            for m in range(2):
                for i in range(TT):
                    u = m * TT + i
                    if u >= 4:
                        dve.wait_ge(list_done, u - 3)
                    dve.tensor_scalar(lane_hot[:, u % 4], i128[:], lane[:, m, i:i + 1], None, ALU.is_equal).then_inc(list_ready, 1)
                    dve.tensor_scalar(tile_hot[:, u % 4], i128[:, 0:J], tile_f[:, m, i:i + 1], token[:, i:i + 1],
                                      ALU.is_equal, ALU.mult).then_inc(list_ready, 1)
            dve.wait_ge(list_done, 2 * TT)
            dve.tensor_copy(pair_token[:], ps_k[:, 0:J]).then_inc(tokens_ready, 1)
            dve.wait_ge(gap_exp, 1)
            link(dve.tensor_scalar(w_top[:, 1], gap[:], 1.0, None, ALU.add))
            link(dve.reciprocal(w_top[:, 0], w_top[:, 1]))
            link(dve.tensor_tensor(w_top[:, 1], w_top[:, 0], gap[:], ALU.mult))
            for k in range(2 * KC):
                low_s(k)
            for j in range(J):
                dve.wait_ge(l_hi_done, j + 1)
                dve.tensor_tensor(l_lo[:, j % 2], PS_T[j % 3][:], l_hi[:, j % 2].bitcast(F32), ALU.subtract).then_inc(l_lo_done, 1)
            for i in range(TT):
                slot = acc[:, i % 4]
                if i >= 4:
                    dve.wait_ge(out_stored[i % 4], 16 * (i // 4))
                for m in range(2):
                    dve.wait_ge(y_gathered[m], 16 * (i + 1))
                    dve.scalar_tensor_tensor(out=slot, in0=yg[:, m], scalar=w_top[:, m, i:i + 1], in1=base[:, i] if m == 0 else slot,
                                             op0=ALU.mult, op1=ALU.add).then_inc(added, 1)
                    dve.wait_ge(added, 2 * i + m + 1)
                dve.bn_stats(stats[:, i % 2], slot).then_inc(stat_done, 1)
                dve.wait_ge(stat_done, i + 1)
                dve.bn_aggr(mv[:, i], stats[:, i % 2]).then_inc(agg_done, 1)
                dve.wait_ge(agg_done, i + 1)
                dve.tensor_scalar(var_e[:, i:i + 1], mv[:, i, 1:2], EPS, None, ALU.add).then_inc(var_done, 1)
                if i:
                    norm_shift(dve, i - 1)
            norm_shift(dve, TT - 1)

        @block.tensor
        def _(pe):
            pe.wait_ge(const, 7)
            pe.wait_ge(list_ready, 1)
            flat = sel[:].rearrange("p i e -> p (i e)")
            pe.matmul(ps_r[:, 0:P], before[:], flat, start=True, stop=True)
            pe.matmul(ps_r[:, P:2 * P], ones[:], flat, start=True, stop=True).then_inc(count_done, 1)
            for u in range(2 * TT):
                pe.wait_ge(list_ready, 2 * u + 3)
                pe.matmul(ps_k[:, 0:J], lane_hot[:, u % 4], tile_hot[:, u % 4], start=u == 0, stop=u == 2 * TT - 1).then_inc(list_done, 1)

            def turn(j):
                pe.wait_ge(x_gathered[j % XG], 16 * (j // XG + 1))
                if j >= 3:
                    pe.wait_ge(l_lo_done, j - 2)
                for k in range(KC):
                    mm = pe.transpose(PS_T[j % 3][:, k * P:(k + 1) * P], xg[:, j % XG, k * P:(k + 1) * P], c.id_f[:])
                mm.then_inc(t_full, 1)

            turn(0)
            pe.wait_ge(s_lo_done, 2 * KC)
            for j in range(J):
                if j + 1 < J:
                    turn(j + 1)
                expert = pe.value_load(of_tile_i[0:1, j:j + 1], min_val=0, max_val=E - 1)
                pe.wait_ge(l_lo_done, j + 1)
                if j >= 3:
                    pe.wait_ge(y_copied, j - 2)
                terms = [(s, u, k) for s, u in ((0, 0), (0, 1), (1, 0)) for k in range(KC)]
                for m, (s, u, k) in enumerate(terms):
                    right = (s_hi, s_lo)[u][:, k, bass.ds(expert, 1), :].rearrange("p o n -> p (o n)")
                    mm = pe.matmul(PS_Y[j % 3][:], (l_hi, l_lo)[s][:, j % 2, k * P:(k + 1) * P], right,
                                   start=m == 0, stop=m == len(terms) - 1)
                mm.then_inc(y_full, 1)


def decoder_layer(nc, a, out):
    dram = lambda name, shape, dt: nc.dram_tensor(name, shape, dt, kind="Internal").ap()
    parts_dram = dram("parts_dram", [2, ROUNDS, 3, FR, T], BF16)
    o_dram = dram("o_dram", [B, T, D], F32)
    s_dram = dram("s_dram", [D * D + NS, E], F32)
    x2_dram = dram("x2_dram", [TOK, D], F32)
    y_dram = dram("y_dram", [J * P, D], F32)
    with ExitStack() as ctx:
        c = Common(nc, ctx)
        attention(nc, c, a["x_t"], a["wq_t"], a["wk_t"], a["wv_t"], parts_dram, o_dram,
                  a["idx_row"], a["idx_col"], a["atoms"], a["expert_atom_weights"], a["importance_t"], s_dram)
        base = ctx.enter_context(nc.sbuf_tensor("base", [P, TT, D], F32))
        logits = ctx.enter_context(nc.sbuf_tensor("logits", [P, TT, E], F32))
        cross(nc, c, a["x"], o_dram, a["ctx_t"], a["wxq_t"], a["wxk_t"], a["bxq"], a["bxk"], a["wo_t"], a["w_t"],
              a["gate_t"], x2_dram, base, logits)
        experts(nc, c, s_dram, x2_dram, y_dram, base, logits, out)


def kernel(x, ctx_1024, L0_attn_Wq, L0_attn_Wk, L0_attn_Wv, L0_attn_Wo, L0_xattn_Wq, L0_xattn_bq, L0_xattn_Wk,
           L0_xattn_bk, L0_ffn_gate_w, L0_ffn_W, L0_ffn_atoms, L0_ffn_expert_atom_weights, L0_ffn_importance,
           L0_ffn_mask_idx):
    import numpy as np
    import concourse.bacc as bacc
    from concourse.bass_utils import run_bass_kernel_spmd

    lay = np.ascontiguousarray
    n = lambda v: np.asarray(v)
    by_element = lambda w: lay(n(w).T.reshape(D, PER_BATCH, HR, DK).transpose(0, 1, 3, 2).reshape(D, D))
    arrays = {
        "x": lay(n(x)), "x_t": lay(n(x).transpose(0, 2, 1)), "ctx_t": lay(n(ctx_1024).transpose(0, 2, 1)),
        "wq_t": by_element(L0_attn_Wq), "wk_t": by_element(L0_attn_Wk), "wv_t": lay(n(L0_attn_Wv).T), "wo_t": lay(n(L0_attn_Wo).T),
        "wxq_t": lay(n(L0_xattn_Wq).T), "wxk_t": lay(n(L0_xattn_Wk).T),
        "bxq": lay(n(L0_xattn_bq).reshape(DX, 1)), "bxk": lay(n(L0_xattn_bk).reshape(DX, 1)),
        "gate_t": lay(n(L0_ffn_gate_w).T), "w_t": lay(n(L0_ffn_W).T), "atoms": lay(n(L0_ffn_atoms)),
        "expert_atom_weights": lay(n(L0_ffn_expert_atom_weights)),
        "importance_t": lay(n(L0_ffn_importance).reshape(E, CHUNKS, P).transpose(2, 1, 0).reshape(P, CHUNKS * E)),
        "idx_row": lay(n(L0_ffn_mask_idx)), "idx_col": lay(n(L0_ffn_mask_idx).reshape(CHUNKS, P).T),
    }
    nc = bacc.Bacc("TRN2", target_bir_lowering=False, num_devices=1)
    a = {k: nc.dram_tensor(f"in_{k}", v.shape, mybir.dt.from_np(v.dtype), kind="ExternalInput").ap() for k, v in arrays.items()}
    out = nc.dram_tensor("out", [TOK, D], F32, kind="ExternalOutput").ap()
    decoder_layer(nc, a, out)
    r = run_bass_kernel_spmd(nc, [{f"in_{k}": v for k, v in arrays.items()}], core_ids=[0])
    return r.results[0]["out"].reshape(B, T, D)
```

```python
from contextlib import ExitStack

import concourse.bass as bass
from concourse import mybir

P = 128
B, T, D = 4, 512, 512
HEADS, DK = 32, 16
KC = D // P
TILES = T // P
PER_BATCH = 4
ROUNDS = PER_BATCH * B
HR = HEADS // PER_BATCH
STACKS = 4
FR = HR * DK
GROUPS = HR // 4
BLOCKS = 2 * TILES - 1
COLS = T + T - P
SLOTS = 8
C, DX = 256, 128
CC = C // P
E, ATOMS, NS = 8, 64, 4096
CHUNKS = NS // P
EG = 4
TOK = B * T
TT = TOK // P
J = 2 * TOK // P + E - 1
ZERO_COLS, ZERO_REP = 256, 4
ZERO_DMAS = D * D * E // (P * ZERO_COLS * ZERO_REP)
NEG = -1e30
EPS = 1e-5

F32 = mybir.dt.float32
F32R = mybir.dt.float32r
BF16 = mybir.dt.bfloat16
I32 = mybir.dt.int32
ALU = mybir.AluOpType
ACT = mybir.ActivationFunctionType
AX = mybir.AxisListType

Q_PART = (0, 0, 0, 1, 1, 2)
K_PART = (0, 1, 2, 0, 1, 0)
NP_ = len(Q_PART)
ROWS = NP_ * DK
MROWS = ROWS + 3


class Common:

    def __init__(self, nc, ctx):
        sb = lambda name, shape, dt: ctx.enter_context(nc.sbuf_tensor(name, shape, dt))
        self.id_f = sb("id_f", [P, P], F32)
        self.zeros = sb("zeros", [P, ZERO_COLS], F32)


class Routing:

    def __init__(self, nc, ctx):
        sb = lambda name, shape, dt: ctx.enter_context(nc.sbuf_tensor(name, shape, dt))
        self.before = sb("before", [P, P], F32)
        self.ones = sb("ones", [P, P], F32)
        self.i8, self.i128 = sb("i8", [P, E], F32), sb("i128", [P, P], F32)
        self.token = sb("token", [P, TT], F32)
        self.top, self.top_i = sb("top", [P, TT, 8], F32), sb("top_i", [P, TT, 8], mybir.dt.uint32)


def attention_plan():
    at = []
    for r in range(ROUNDS):
        t = HR * r
        at += [(t + n, "score_exp", r, n) for n in range(HR)]
        s_items = [(0, a) for a in range(HR // 4)] + [(i, a) for i in range(1, TILES) for a in range(HR // 2)]
        at += [(t - HR - 3.6 + HR * k / len(s_items), "score_max", r, *s) for k, s in enumerate(s_items)]
        at.append((t - 3.3, "max_t", r))
        at += [(t - 23.4, "proj_q", r), (t - 21.2, "proj_k", r)]
        if r % 2 == 0:
            at += [(t - 13.8 + n, "proj_v", r, n) for n in range(TILES)]
        if r % PER_BATCH == 0:
            at.append((t - 26.6, "split_x", r // PER_BATCH))
        for g in range(GROUPS):
            at += [(t + 4 * g + 5.6, "pv", r, g), (t + 4 * g + 7.75, "o_t", r, g)]
    at += [(1.6 + 1.6 * n, "zero", n) for n in range(ZERO_DMAS + 1)]
    at += [(19.1, "entry_in", 0), (21.1, "entry_w", 0)]
    for g in range(CHUNKS // EG):
        at += [(24.3 + 5 * g, "entry_v", g), (26.7 + 5 * g, "entry_s", g)]
        at += [(31.3 + 5 * g + n, "scatter", EG * g + n) for n in range(EG)]
    at.sort(key=lambda s: s[0])
    return [s[1:] for s in at], [s[0] for s in at]


def later(plan, times, kinds, others, by):
    out = []
    for at, step in enumerate(plan):
        time = times[at]
        if step[0] in kinds:
            sharing = [times[n] for n in range(at + 1, len(plan)) if plan[n][0] in kinds + others][:2]
            time = min([time + by] + [t - 0.01 for t in sharing[1:]])
        out.append((time, at, step))
    return [step for *_, step in sorted(out)]


def attention(nc, c, x_t, wq_t, wk_t, wv_t, parts_dram, o_dram, idx_row, idx_col, atoms, eaw, imp_t, s_dram):
    plan, times = attention_plan()
    general = [s for s in plan if s[0] in ("proj_q", "proj_k", "proj_v", "max_t", "o_t", "entry_w", "entry_v", "entry_s")]
    bank_of = {s: (n % 2, n // 2) for n, s in enumerate(general)}
    s_order = {s: n for n, s in enumerate(s for s in plan if s[0] == "score_max")}
    vector_plan = later(plan, times, ("proj_q", "proj_k", "o_t", "entry_v", "entry_s", "split_x"), ("proj_v", "max_t", "entry_w"), 0.4)
    p_order = {s: n for n, s in enumerate(s for s in plan if s[0] in ("proj_q", "proj_k"))}

    with ExitStack() as ctx:
        sb = lambda name, shape, dt: ctx.enter_context(nc.sbuf_tensor(name, shape, dt))
        sem = lambda name: ctx.enter_context(nc.semaphore(name))

        x_raw = sb("x_raw", [P, KC, T], F32)
        x_hi = sb("x_hi", [P, KC, T], F32R)
        x_lo = sb("x_lo", [P, KC, T], F32R)
        w_hi = sb("w_hi", [P, 3, KC, D], F32R)
        w_lo = sb("w_lo", [P, 3, KC, D], F32R)
        q_st = sb("q_st", [P, STACKS, HR, T], BF16)
        k_st = sb("k_st", [P, STACKS, HR, T], BF16)
        v_sb = sb("v_sb", [P, 2, TILES, 2 * HR, DK + 1], F32)
        probs = sb("probs", [P, SLOTS, COLS], F32)
        w_raw = probs[:, 0:7, :].rearrange("p s c -> p (s c)")[:, 0:3 * KC * D].rearrange("p (w k n) -> p w k n", w=3, k=KC)
        parts = sb("parts", [P, 2, 3, T], BF16)
        rest = sb("rest", [P, T], F32)
        o_sb = sb("o_sb", [P, T], F32)
        o_n = sb("o_n", [P, 2, TILES, FR], F32)
        r_den = sb("r_den", [P, 2, TILES, 4], F32)
        n_max = sb("n_max", [P, 2, HR, TILES], F32)
        masked = sb("masked", [P, 2, T], BF16)
        m_rest = sb("m_rest", [TILES * HR, P], F32)
        m_part = sb("m_part", [TILES * HR, 3, P], BF16)
        mask = sb("mask", [P, 2, P], BF16)

        mask_e = sb("mask_e", [P, 2, P], BF16)
        id_b = sb("id_b", [P, P], BF16)
        ones_b = sb("ones_b", [3, P], BF16)

        row_i = sb("row_i", [P, EG * P], I32)
        col_i, col_f = sb("col_i", [P, CHUNKS], I32), sb("col_f", [P, CHUNKS], F32)
        same = sb("same", [P, EG, P], F32)
        after = sb("after", [P, P], BF16)
        earlier = sb("earlier", [P, P], BF16)
        atom_sb = sb("atom_sb", [ATOMS, EG * P], F32)
        imp = sb("imp", [P, CHUNKS, E], F32)
        ew, ew_t = sb("ew", [E, ATOMS], F32), sb("ew_t", [ATOMS, E], F32)
        st = sb("st", [E, 4], F32)
        value = sb("value", [P, EG, E], F32)
        e_value = sb("e_value", [P, CHUNKS, E], F32)
        e_index = sb("e_index", [P, CHUNKS], I32)
        dup = sb("dup", [P, CHUNKS], F32)
        place_i, high_i = sb("place_i", [P, CHUNKS], I32), sb("high_i", [P, CHUNKS], I32)
        place, spare_i, spare = sb("place", [P, CHUNKS], F32), sb("spare_i", [P, CHUNKS], I32), sb("spare", [P, CHUNKS], F32)

        ps_g = [ctx.enter_context(nc.psum_tensor(f"ps_g{i}", [P, T], F32)) for i in range(2)]
        ps_s = [ctx.enter_context(nc.psum_tensor(f"ps_s{i}", [P, T], F32)) for i in range(2)]
        ps_e = [ctx.enter_context(nc.psum_tensor(f"ps_e{i}", [P, T], F32)) for i in range(3)]
        ps_o = ctx.enter_context(nc.psum_tensor("ps_o", [P, T], F32))

        w_loaded = [sem(f"w_loaded{i}") for i in range(3)]
        w_hi_done, w_lo_done = sem("w_hi_done"), sem("w_lo_done")
        x_loaded, x_hi_done = sem("x_loaded"), sem("x_hi_done")
        x_lo_done, x_lo_pool = sem("x_lo_done"), sem("x_lo_pool")
        const_done, ones_done, fill_done, o_cleared = sem("const_done"), sem("ones_done"), sem("fill_done"), sem("o_cleared")
        g_full = [sem(f"g_full{i}") for i in range(2)]
        g_free = [sem(f"g_free{i}") for i in range(2)]
        part1_done, rest_done, part2_done, part3_done = sem("part1_done"), sem("rest_done"), sem("part2_done"), sem("part3_done")
        part_stored = [sem(f"part_stored{i}") for i in range(2)]
        q_stacked = [sem(f"q_stacked{i}") for i in range(STACKS)]
        k_stacked = [sem(f"k_stacked{i}") for i in range(STACKS)]
        m_stacked = [sem(f"m_stacked{i}") for i in range(2)]
        s_full, s_max_done = sem("s_full"), sem("s_max_done")
        m_step, e_full, exp_done = sem("m_step"), sem("e_full"), sem("exp_done")
        pv_done, o_copied, den_done, norm_done = (
            sem("pv_done"), sem("o_copied"), sem("den_done"), sem("norm_done"))
        o_stored = [sem(f"o_stored{i}") for i in range(2)]
        eaw_in, imp_in, col_in, row_in, atoms_in = sem("eaw_in"), sem("imp_in"), sem("col_in"), sem("row_in"), sem("atoms_in")
        eaw_max, eaw_exp, imp_exp, soft_done = sem("eaw_max"), sem("eaw_exp"), sem("imp_exp"), sem("soft_done")
        entry_link, same_done, dup_done, entry_ready = sem("entry_link"), sem("same_done"), sem("dup_done"), sem("entry_ready")
        zeroed, entry_added = sem("zeroed"), sem("entry_added")

        block = ctx.enter_context(nc.Block())

        def wait_full(eng, step):
            bank, nth = bank_of[step]
            eng.wait_ge(g_full[bank], nth + 1)
            return ps_g[bank]

        def wait_free(eng, step):
            bank, nth = bank_of[step]
            eng.wait_ge(g_free[bank], nth + 1)

        @block.sync
        def _(sp):
            def load_stacks(r):
                if r >= STACKS:
                    sp.wait_ge(e_full, 2 * HR * (r - STACKS + 1))
                for i in range(2):
                    sp.wait_ge(part_stored[i], 16 * (r + 1))
                for src, repeat, first in ((0, 3, 0), (1, 2, 3), (2, 1, 5)):
                    rows = slice(first * DK, (first + repeat) * DK)
                    sp.dma_start(k_st[rows, r % STACKS], parts_dram[1, r, 0:repeat].rearrange("a (d h) t -> (a d) h t", d=DK)
                                 ).then_inc(k_stacked[r % STACKS], 16)
                    sp.dma_start(q_st[rows, r % STACKS], parts_dram[0, r, src].rearrange("(d h) t -> d h t", d=DK).unsqueeze(0)
                                 .broadcast_to([repeat, DK, HR, T])).then_inc(q_stacked[r % STACKS], 16)

            def load_entries(g):
                if g:
                    sp.wait_ge(same_done, g)
                sp.dma_start(row_i[:], idx_row[g * EG * P:(g + 1) * EG * P].partition_broadcast(P)).then_inc(row_in, 16)
                if g:
                    wait_full(sp, ("entry_v", g - 1))
                sp.dma_start(atom_sb[:], atoms[:, g * EG * P:(g + 1) * EG * P]).then_inc(atoms_in, 16)

            for i, w in enumerate((wq_t, wk_t, wv_t)):
                sp.dma_start(w_raw[:, i], w.rearrange("(k p) n -> p k n", p=P)).then_inc(w_loaded[i], 16)
                if i == 0:
                    sp.dma_start(x_raw[:], x_t[0].rearrange("(k p) t -> p k t", p=P)).then_inc(x_loaded, 16)
            sp.wait_ge(fill_done, 5)
            sp.dma_start(k_st[ROWS:MROWS].rearrange("o s h t -> o (s h t)").rearrange("o (n t) -> o n t", t=P),
                         ones_b[:].unsqueeze(1).broadcast_to([3, STACKS * HR * T // P, P])).then_inc(ones_done, 16)
            sp.dma_start(ew[:], eaw).then_inc(eaw_in, 16)
            sp.dma_start(imp[:].rearrange("p c e -> p (c e)"), imp_t).then_inc(imp_in, 16)
            sp.dma_start(col_i[:], idx_col).then_inc(col_in, 16)
            load_entries(0)
            for step in plan:
                kind, r = step[:2]
                if kind == "split_x" and r + 1 < B:
                    sp.wait_ge(x_hi_done, r + 1)
                    sp.wait_ge(x_lo_done, r + 1)
                    sp.wait_ge(x_lo_pool, r + 1)
                    sp.dma_start(x_raw[:], x_t[r + 1].rearrange("(k p) t -> p k t", p=P)).then_inc(x_loaded, 16)
                if kind in ("proj_q", "proj_k"):
                    no, which = p_order[step], int(kind == "proj_k")
                    sp.wait_ge(part3_done, no + 1)
                    sp.dma_start(parts_dram[which, r].rearrange("a p t -> p a t"), parts[:, no % 2]).then_inc(part_stored[no % 2], 16)
                    if which:
                        load_stacks(r)
                if kind == "max_t":
                    sp.wait_ge(m_step, 4 * (r + 1))
                    sp.wait_ge(q_stacked[r % STACKS], 16 * 3 * (r // STACKS + 1))
                    for n in range(3):
                        sp.dma_start(q_st[ROWS + n:ROWS + n + 1, r % STACKS].rearrange("o h (i t) -> o (h i) t", i=TILES),
                                     m_part[:, n]
                                     ).then_inc(m_stacked[r % 2], 16)
                if kind == "zero":
                    rows = D * D // ZERO_DMAS
                    if r < ZERO_DMAS:
                        sp.dma_start(s_dram[r * rows:(r + 1) * rows].rearrange("(p a b) e -> p a (b e)", p=P, a=ZERO_REP),
                                     c.zeros[:].unsqueeze(1).broadcast_to([P, ZERO_REP, ZERO_COLS])).then_inc(zeroed, 16)
                    else:
                        sp.dma_start(s_dram[D * D:].rearrange("(p b) e -> p (b e)", p=P), c.zeros[:, 0:CHUNKS * E]).then_inc(zeroed, 16)
                if kind == "entry_v" and r + 1 < CHUNKS // EG:
                    load_entries(r + 1)
                if kind == "o_t" and step[2] == GROUPS - 1:
                    sp.wait_ge(norm_done, GROUPS * (r + 1))
                    sp.dma_start(o_dram[r // PER_BATCH, :, (r % PER_BATCH) * FR:(r % PER_BATCH + 1) * FR].rearrange("(i p) f -> p i f", p=P),
                                 o_n[:, r % 2]).then_inc(o_stored[r % 2], 16)
            for i in range(2):
                sp.wait_ge(o_stored[i], 16 * ROUNDS // 2)
            sp.wait_ge(entry_added, 16 * CHUNKS)

        @block.gpsimd
        def _(pool):
            pool.memset(c.id_f[:], 0.0).then_inc(fill_done, 1)
            pool.memset(mask[:], 0.0).then_inc(fill_done, 1)
            pool.memset(after[:], 1.0).then_inc(fill_done, 1)
            pool.memset(mask_e[:], 0.0).then_inc(fill_done, 1)
            pool.memset(ones_b[:], 1.0).then_inc(fill_done, 1)
            pool.wait_ge(fill_done, 5)
            pool.affine_select(out=c.id_f[:], in_=c.id_f[:], compare_op=ALU.not_equal, fill=1.0, base=0,
                               pattern=[[-1, P]], channel_multiplier=1).then_inc(const_done, 1)
            pool.affine_select(out=mask[:, 0], in_=mask[:, 0], compare_op=ALU.is_ge, fill=NEG, base=0,
                               pattern=[[1, P]], channel_multiplier=-1).then_inc(const_done, 1)
            pool.affine_select(out=mask[:, 1], in_=mask[:, 1], compare_op=ALU.is_ge, fill=NEG, base=0,
                               pattern=[[-1, P]], channel_multiplier=1).then_inc(const_done, 1)
            pool.affine_select(out=mask_e[:, 0], in_=mask_e[:, 0], compare_op=ALU.is_ge, fill=NEG, base=0,
                               pattern=[[1, P]], channel_multiplier=-1).then_inc(const_done, 1)
            pool.affine_select(out=mask_e[:, 1], in_=mask_e[:, 1], compare_op=ALU.is_ge, fill=NEG, base=0,
                               pattern=[[-1, P]], channel_multiplier=1).then_inc(const_done, 1)
            pool.affine_select(out=after[:], in_=after[:], compare_op=ALU.is_ge, fill=0.0, base=-1,
                               pattern=[[-1, P]], channel_multiplier=1).then_inc(const_done, 1)
            pool.wait_ge(const_done, 6)
            pool.memset(c.zeros[:], 0.0).then_inc(const_done, 1)
            pool.iota(spare_i[:], pattern=[[P, CHUNKS]], base=D * D, channel_multiplier=1).then_inc(const_done, 1)
            pool.memset(v_sb[:, :, :, :, DK:DK + 1], 1.0).then_inc(const_done, 1)
            pool.tensor_copy(id_b[:], c.id_f[:]).then_inc(const_done, 1)
            for step in plan:
                kind, r = step[:2]
                if kind == "scatter":
                    if r == 0:
                        pool.wait_ge(zeroed, 16 * (ZERO_DMAS + 1))
                    else:
                        pool.wait_ge(entry_added, 16 * r)
                    pool.wait_ge(entry_ready, r // EG + 1)
                    pool.indirect_dma_start(out=s_dram, out_offset=bass.IndirectOffsetOnAxis(ap=e_index[:, r:r + 1], axis=0),
                                            in_=e_value[:, r], in_offset=None, compute_op=ALU.add).then_inc(entry_added, 16)
                if kind == "split_x":
                    pool.wait_ge(x_hi_done, r + 1)
                    pool.tensor_tensor(x_lo[:, KC - 1], x_raw[:, KC - 1], x_hi[:, KC - 1].bitcast(F32), ALU.subtract).then_inc(x_lo_pool, 1)

        @block.scalar
        def _(act):
            for i in range(3):
                act.wait_ge(w_loaded[i], 16)
                act.activation(w_hi[:, i], w_raw[:, i], ACT.Copy).then_inc(w_hi_done, 1)
                if i == 0:
                    act.wait_ge(x_loaded, 16)
                    act.activation(x_hi[:], x_raw[:], ACT.Copy).then_inc(x_hi_done, 1)
            for step in plan:
                kind, r = step[:2]
                if kind == "split_x" and r:
                    act.wait_ge(x_loaded, 16 * (r + 1))
                    wait_full(act, ("proj_v", PER_BATCH * r - 2, TILES - 1))
                    act.activation(x_hi[:], x_raw[:], ACT.Copy).then_inc(x_hi_done, 1)
                if kind in ("proj_q", "proj_k"):
                    no, scale = p_order[step], DK ** -0.5 if kind == "proj_q" else 1.0
                    ps = wait_full(act, step)
                    if no >= 2:
                        act.wait_ge(part_stored[no % 2], 16 * (no // 2))
                    act.activation(parts[:, no % 2, 0], ps[:], ACT.Copy, scale=scale).then_inc(part1_done, 1)
                if kind == "proj_v":
                    ps = wait_full(act, step)
                    if r == 0 and step[2] == 0:
                        act.wait_ge(const_done, 10)
                    act.activation(v_sb[:, r // 2 % 2, step[2], :, 0:DK], ps[:, 0:2 * FR].rearrange("p (h d) -> p h d", d=DK),
                                   ACT.Copy).then_inc(g_free[bank_of[step][0]], 1)
                if kind == "entry_in":
                    act.wait_ge(eaw_max, 1)
                    act.activation(ew[:], ew[:], ACT.Exp, bias=st[:, 0:1], accum_out=st[:, 1:2]).then_inc(eaw_exp, 1)
                    act.wait_ge(imp_in, 16)
                    act.activation(imp[:], imp[:], ACT.Exp, scale=-1.0).then_inc(imp_exp, 1)
                if kind == "score_exp":
                    head = HR * r + step[2]
                    if head == 0:
                        act.wait_ge(w_lo_done, 3)
                    if head >= SLOTS:
                        act.wait_ge(pv_done, (head - SLOTS) // 4 + 1)
                    for half, (c0, c1) in enumerate(((0, T), (T, COLS))):
                        e = 2 * head + half
                        act.wait_ge(e_full, e + 1)
                        act.activation(probs[:, head % SLOTS, c0:c1], ps_e[e % 3][:, 0:c1 - c0], ACT.Exp).then_inc(exp_done, 1)
                if kind == "pv":
                    g = GROUPS * r + step[2]
                    act.wait_ge(pv_done, g + 1)
                    if g >= 1:
                        wait_full(act, ("o_t", (g - 1) // GROUPS, (g - 1) % GROUPS))
                    act.activation(o_sb[:], ps_o[:], ACT.Copy).then_inc(o_copied, 1)

        @block.vector
        def _(dve):
            links = [0]

            def link(ins):
                links[0] += 1
                ins.then_inc(entry_link, 1)
                dve.wait_ge(entry_link, links[0])

            dve.memset(ps_o[:], 0.0).then_inc(o_cleared, 1)
            for i in range(3):
                dve.wait_ge(w_hi_done, i + 1)
                dve.tensor_tensor(w_lo[:, i], w_raw[:, i], w_hi[:, i].bitcast(F32), ALU.subtract).then_inc(w_lo_done, 1)
                if i == 0:
                    dve.wait_ge(x_hi_done, 1)
                    dve.tensor_tensor(x_lo[:, :-1], x_raw[:, :-1], x_hi[:, :-1].bitcast(F32), ALU.subtract).then_inc(x_lo_done, 1)
            for step in vector_plan:
                kind, r = step[:2]
                if kind == "split_x" and r:
                    dve.wait_ge(x_hi_done, r + 1)
                    dve.tensor_tensor(x_lo[:, :-1], x_raw[:, :-1], x_hi[:, :-1].bitcast(F32), ALU.subtract).then_inc(x_lo_done, 1)
                if kind in ("proj_q", "proj_k"):
                    no, scale = p_order[step], DK ** -0.5 if kind == "proj_q" else 1.0
                    slot = no % 2
                    ps = ps_g[bank_of[step][0]]
                    dve.wait_ge(part1_done, no + 1)
                    if no:
                        dve.wait_ge(part3_done, no)
                    dve.scalar_tensor_tensor(out=rest[:], in0=ps[:], scalar=scale, in1=parts[:, slot, 0],
                                             op0=ALU.mult, op1=ALU.subtract).then_inc(g_free[bank_of[step][0]], 1)
                    wait_free(dve, step)
                    dve.tensor_copy(parts[:, slot, 1], rest[:]).then_inc(part2_done, 1)
                    dve.wait_ge(part2_done, no + 1)
                    dve.tensor_tensor(parts[:, slot, 2], rest[:], parts[:, slot, 1], ALU.subtract).then_inc(part3_done, 1)
                if kind == "score_max":
                    s, (i, a) = s_order[step], step[2:]
                    per = 4 if i == 0 else 2
                    width = T // per
                    if s == 0:
                        dve.wait_ge(const_done, 10)
                    dve.wait_ge(s_full, s + 1)
                    if r >= 2 and (i, a) == (0, 0):
                        wait_full(dve, ("max_t", r - 2))
                    if s >= 2:
                        dve.wait_ge(s_max_done, s - 1)
                    for n in range(per):
                        h = per * a + n
                        last = dve.tensor_tensor_reduce(
                            out=masked[:, s % 2, n * width:(n + 1) * width], in0=ps_s[s % 2][:, n * width:(n + 1) * width],
                            in1=mask[:].rearrange("p w k -> p (w k)")[:, 2 * P - width:], scale=-1.0, scalar=-NEG,
                            op0=ALU.add, op1=ALU.min, accum_out=n_max[:, r % 2, h, i:i + 1])
                    last.then_inc(s_max_done, 1)
                if kind == "max_t":
                    ps, (bank, nth) = wait_full(dve, step), bank_of[step]
                    if r:
                        dve.wait_ge(m_stacked[(r - 1) % 2], 48 * ((r - 1) // 2 + 1))
                    n = TILES * HR
                    dve.tensor_copy(m_part[:, 0], ps[0:n, 0:P]).then_inc(m_step, 1)
                    dve.wait_ge(m_step, 4 * r + 1)
                    dve.tensor_tensor(m_rest[:], ps[0:n, 0:P], m_part[:, 0], ALU.subtract).then_inc(g_free[bank], 1)
                    wait_free(dve, step)
                    dve.tensor_copy(m_part[:, 1], m_rest[:]).then_inc(m_step, 1)
                    dve.wait_ge(m_step, 4 * r + 2)
                    dve.tensor_tensor(m_part[:, 2], m_rest[:], m_part[:, 1], ALU.subtract).then_inc(m_step, 2)
                if kind == "entry_in":
                    dve.wait_ge(eaw_in, 16)
                    dve.tensor_reduce(st[:, 0:1], ew[:], AX.X, ALU.max, negate=True).then_inc(eaw_max, 1)
                if kind == "entry_w":
                    dve.wait_ge(eaw_exp, 1)
                    link(dve.reciprocal(st[:, 2:3], st[:, 1:2]))
                    dve.tensor_scalar(ew[:], ew[:], st[:, 2:3], None, ALU.mult).then_inc(soft_done, 1)
                    dve.wait_ge(imp_exp, 1)
                    link(dve.tensor_scalar(imp[:], imp[:], 1.0, None, ALU.add))
                    link(dve.reciprocal(imp[:], imp[:]))
                    dve.wait_ge(col_in, 16)
                    link(dve.tensor_copy(col_f[:], col_i[:]))
                    link(dve.tensor_scalar(place_i[:], col_i[:], D - 1, D.bit_length() - 1, ALU.bitwise_and, ALU.logical_shift_left))
                    link(dve.tensor_scalar(high_i[:], col_i[:], D.bit_length() - 1, None, ALU.logical_shift_right))
                    link(dve.tensor_copy(place[:], high_i[:]))
                    link(dve.tensor_copy(spare[:], place_i[:]))
                    link(dve.tensor_tensor(place[:], place[:], spare[:], ALU.add))
                    link(dve.tensor_copy(spare[:], spare_i[:]))
                    link(dve.tensor_tensor(spare[:], spare[:], place[:], ALU.subtract))
                    ps = wait_full(dve, step)
                    dve.tensor_copy(ew_t[:], ps[0:ATOMS, 0:E]).then_inc(g_free[bank_of[step][0]], 1)
                if kind == "entry_v":
                    dve.wait_ge(row_in, 16 * (r + 1))
                    if r:
                        wait_full(dve, ("entry_s", r - 1))
                    dve.tensor_tensor(same[:], row_i[:].rearrange("p (c s) -> p c s", s=P),
                                      col_f[:, EG * r:EG * (r + 1)].unsqueeze(2).broadcast_to([P, EG, P]), ALU.is_equal).then_inc(same_done, 1)
                    ps = wait_full(dve, step)
                    dve.tensor_tensor(value[:].rearrange("p c e -> p (c e)"), ps[:, 0:EG * E],
                                      imp[:, EG * r:EG * (r + 1)].rearrange("p c e -> p (c e)"), ALU.mult).then_inc(g_free[bank_of[step][0]], 1)
                    dve.wait_ge(same_done, r + 1)
                    for n in range(EG):
                        if EG * r + n:
                            dve.wait_ge(dup_done, EG * r + n)
                        dve.tensor_tensor_reduce(out=earlier[:], in0=same[:, n], in1=after[:], scale=1.0, scalar=0.0, op0=ALU.mult,
                                                 op1=ALU.max, accum_out=dup[:, EG * r + n:EG * r + n + 1]).then_inc(dup_done, 1)
                if kind == "entry_s":
                    own = slice(EG * r, EG * (r + 1))
                    ps = wait_full(dve, step)
                    dve.tensor_copy(e_value[:, own].rearrange("p c e -> p (c e)"), ps[:, 0:EG * E]).then_inc(g_free[bank_of[step][0]], 1)
                    dve.wait_ge(dup_done, EG * (r + 1))
                    link(dve.tensor_tensor(dup[:, own], dup[:, own], spare[:, own], ALU.mult))
                    wait_free(dve, step)
                    dve.tensor_tensor(e_index[:, own], dup[:, own], place[:, own], ALU.add).then_inc(entry_ready, 1)
                if kind == "o_t":
                    g = GROUPS * r + step[2]
                    ps, (bank, nth) = wait_full(dve, step), bank_of[step]
                    heads = ps[:].rearrange("p (i h c) -> p i h c", i=TILES, h=4)
                    dve.reciprocal(r_den[:, g % 2], heads[:, :, :, DK]).then_inc(den_done, 1)
                    if r >= 2 and step[2] == 0:
                        dve.wait_ge(o_stored[r % 2], 16 * (r // 2))
                    dve.wait_ge(den_done, g + 1)
                    for i in range(TILES):
                        last = dve.tensor_tensor(
                            o_n[:, r % 2, i, step[2] * 64:(step[2] + 1) * 64].rearrange("p (h d) -> p h d", h=4),
                            heads[:, i, :, 0:DK], r_den[:, g % 2, i].unsqueeze(2).broadcast_to([P, 4, DK]), ALU.mult)
                        if i == TILES - 1:
                            last.then_inc(norm_done, 1)
                    dve.wait_ge(norm_done, g + 1)
                    dve.sem_inc(g_free[bank], 1)

        @block.tensor
        def _(pe):
            def take_bank(step):
                bank, nth = bank_of[step]
                if nth:
                    pe.wait_ge(g_free[bank], nth)
                return ps_g[bank], g_full[bank]

            pe.wait_ge(const_done, 10)
            for step in plan:
                kind, r = step[:2]
                if kind in ("proj_q", "proj_k", "proj_v"):
                    w = ("proj_q", "proj_k", "proj_v").index(kind)
                    pe.wait_ge(w_lo_done, w + 1)
                    pe.wait_ge(x_hi_done, r // PER_BATCH + 1)
                    ps, full = take_bank(step)
                    terms = [(a, b, k) for a, b in ((0, 0), (1, 0), (0, 1)) for k in range(KC)]
                    for n, (a, b, k) in enumerate(terms):
                        if (b, k) == (1, 0):
                            pe.wait_ge(x_lo_done, r // PER_BATCH + 1)
                            pe.wait_ge(x_lo_pool, r // PER_BATCH + 1)
                        wt, xt = (w_hi, w_lo)[a], (x_hi, x_lo)[b]
                        f0 = (r % PER_BATCH) * FR
                        if kind == "proj_v":
                            mm = pe.matmul(ps[:, 0:2 * FR], xt[:, k, step[2] * P:(step[2] + 1) * P], wt[:, w, k, f0:f0 + 2 * FR],
                                           start=n == 0, stop=n == len(terms) - 1)
                        else:
                            mm = pe.matmul(ps[:], wt[:, w, k, f0:f0 + P], xt[:, k], start=n == 0, stop=n == len(terms) - 1)
                    mm.then_inc(full, 1)
                if kind == "score_max":
                    s, (i, a) = s_order[step], step[2:]
                    if (i, a) == (0, 0):
                        pe.wait_ge(q_stacked[r % STACKS], 16 * 3 * (r // STACKS + 1))
                        pe.wait_ge(k_stacked[r % STACKS], 16 * 3 * (r // STACKS + 1))
                    if s >= 2:
                        pe.wait_ge(s_max_done, s - 1)
                    ps, per = ps_s[s % 2], 4 if i == 0 else 2
                    width = T // per
                    for n in range(per):
                        h = per * a + n
                        mm = pe.matmul(ps[:, n * width:(n + 1) * width], q_st[0:ROWS, r % STACKS, h, i * P:(i + 1) * P],
                                       k_st[0:ROWS, r % STACKS, h, (i + 1) * P - width:(i + 1) * P], start=True, stop=True)
                    mm.then_inc(s_full, 1)
                if kind == "max_t":
                    ps, full = take_bank(step)
                    pe.wait_ge(s_max_done, (r + 1) * len(s_order) // ROUNDS)
                    pe.transpose(ps[0:TILES * HR, 0:P], n_max[:, r % 2].rearrange("p h i -> p (h i)"), c.id_f[:]).then_inc(full, 1)
                if kind == "score_exp":
                    h = step[2]
                    if r == 0 and h == 0:
                        pe.wait_ge(ones_done, 16)
                    if h == 0:
                        pe.wait_ge(m_stacked[r % 2], 48 * (r // 2 + 1))
                    for half in range(2):
                        e = 2 * (HR * r + h) + half
                        if e >= 3:
                            pe.wait_ge(exp_done, e - 2)
                        for j in (2 * half, 2 * half + 1):
                            c0, width = 2 * P * (j % 2), min(2 * P, T - j * P)
                            mm = pe.matmul(ps_e[e % 3][:, c0:c0 + width], k_st[0:MROWS, r % STACKS, h, j * P:(j + 1) * P],
                                           q_st[0:MROWS, r % STACKS, h, j * P:j * P + width], start=j % 2 == 0, stop=False,
                                           skip_group_check=True)
                        c1 = c0 + width
                        right = mask_e[:].rearrange("p w q -> p (w q)")
                        if c1 == T:
                            right = right.unsqueeze(1).broadcast_to([P, 2, 2 * P])
                            mm = pe.matmul(ps_e[e % 3][:].rearrange("p (a w) -> p a w", a=2), id_b[:], right, start=False, stop=True, skip_group_check=True)
                        else:
                            for a0, width in ((0, 2 * P), (2 * P, P)):
                                mm = pe.matmul(ps_e[e % 3][:, a0:a0 + width], id_b[:], right[:, 0:width], start=False,
                                               stop=True, skip_group_check=True)
                        mm.then_inc(e_full, 1)
                if kind == "entry_w":
                    ps, full = take_bank(step)
                    pe.wait_ge(soft_done, 1)
                    pe.transpose(ps[0:ATOMS, 0:E], ew[:], c.id_f[0:E, 0:E]).then_inc(full, 1)
                if kind == "entry_v":
                    ps, full = take_bank(step)
                    pe.wait_ge(atoms_in, 16 * (r + 1))
                    if r == 0:
                        wait_free(pe, ("entry_w", 0))
                    for n in range(EG):
                        mm = pe.matmul(ps[:, n * E:(n + 1) * E], atom_sb[:, n * P:(n + 1) * P], ew_t[:], start=True, stop=True)
                    mm.then_inc(full, 1)
                if kind == "entry_s":
                    ps, full = take_bank(step)
                    pe.wait_ge(same_done, r + 1)
                    wait_free(pe, ("entry_v", r))
                    for n in range(EG):
                        mm = pe.matmul(ps[:, n * E:(n + 1) * E], same[:, n], value[:, n], start=True, stop=True)
                    mm.then_inc(full, 1)
                if kind == "pv":
                    g = GROUPS * r + step[2]
                    pe.wait_ge(exp_done, 8 * (g + 1))
                    if g == 0:
                        pe.wait_ge(o_cleared, 1)
                    if g:
                        pe.wait_ge(o_copied, g)
                    for j in range(TILES):
                        width = min(2 * P, T - j * P)
                        for n in range(4):
                            h = 4 * step[2] + n
                            mm = pe.matmul(ps_o[32 * n:32 * n + DK + 1, j * P:j * P + width], v_sb[:, r // 2 % 2, j, r % 2 * HR + h],
                                           probs[:, (HR * r + h) % SLOTS, 2 * P * j:2 * P * j + width],
                                           start=j == 0, stop=True, skip_group_check=True)
                    mm.then_inc(pv_done, 1)
                if kind == "o_t":
                    g = GROUPS * r + step[2]
                    ps, full = take_bank(step)
                    pe.wait_ge(o_copied, g + 1)
                    for i in range(TILES):
                        mm = pe.transpose(ps[:, i * P:(i + 1) * P], o_sb[:, i * P:(i + 1) * P], c.id_f[:])
                    mm.then_inc(full, 1)


def cross_plan():
    def turned(kind, b):
        return [(kind, b, k) for k in range(KC)]

    def rows(kind, b):
        return [(kind, b, i) for i in range(TILES)]

    def energies(b):
        return [("qx", b), ("kx", b)] + rows("energy", b) if b < B else []

    def last_part(b):
        return rows("x2_w", b) + [("logit_t", b)]

    plan = turned("o_t", 0) + energies(0) + rows("o_proj", 0) + turned("a_t", 0) + energies(1)
    for b in range(B):
        plan += turned("x1_t", b) + rows("mix", b)
        if b == B - 1:
            plan += last_part(b - 1)
        else:
            plan += turned("a_t", b + 1) + turned("o_t", b + 1) + rows("o_proj", b + 1)
        plan += turned("x2_t", b) + [("logit", b)] + energies(b + 2)
        if b != B - 2:
            plan += last_part(b)
    return plan


def cross(nc, c, x, o_dram, ctx_t, wxq_t, wxk_t, bxq, bxk, wo_t, w_t, gate_t, x2_dram, base, logits, g):
    plan = cross_plan()
    bank_of = {s: (n % 8, n // 8) for n, s in enumerate(plan)}
    turns = [s[:2] for s in plan if s[0] in ("o_t", "x1_t", "x2_t") and s[2] == 0]
    turn_no = {s: n for n, s in enumerate(turns)}
    lo_no = {s: n for n, s in enumerate(s for s in plan if s[0] in ("qx", "kx"))}
    en_no = {s: n for n, s in enumerate(s for s in plan if s[0] == "energy")}

    with ExitStack() as ctx:
        sb = lambda name, shape, dt: ctx.enter_context(nc.sbuf_tensor(name, shape, dt))
        sem = lambda name: ctx.enter_context(nc.semaphore(name))
        wo_hi, wo_lo = sb("wo_hi", [P, KC, D], F32R), sb("wo_lo", [P, KC, D], F32R)
        wf_hi, wf_lo = sb("wf_hi", [P, KC, D], F32R), sb("wf_lo", [P, KC, D], F32R)
        wx_raw = sb("wx_raw", [P, 2, CC, DX], F32)
        wx_hi, wx_lo = sb("wx_hi", [P, 2, CC, DX], F32R), sb("wx_lo", [P, 2, CC, DX], F32R)
        g_raw = sb("g_raw", [P, KC, P], F32)
        g_hi, g_lo = sb("g_hi", [P, KC, P], F32R), sb("g_lo", [P, KC, P], F32R)
        bias = sb("bias_x", [P, 2], F32)
        x_sb = sb("x_sb", [P, 2, TILES, D], F32)
        on_sb = sb("on_sb", [P, 2, TILES, D], F32)
        t_hi, t_lo = sb("t_hi", [P, 2, KC, T], F32R), sb("t_lo", [P, 2, KC, T], F32R)
        c_raw = sb("c_raw", [P, CC, T], F32)
        c_hi, c_lo = sb("c_hi", [P, CC, T], F32R), sb("c_lo", [P, CC, T], F32R)
        qk_hi, qk_lo = sb("qk_hi", [P, 2, T], F32R), sb("qk_lo", [P, 2, T], F32R)
        e_sb = sb("e_sb", [P, TILES, T], F32)
        a_hi, a_lo = sb("a_hi", [P, 2, TILES, T], F32R), sb("a_lo", [P, 2, TILES, T], F32R)
        n_mx = sb("n_mx", [P, TILES], F32)
        a_sum, a_inv = sb("a_sum", [P, TILES], F32), sb("a_inv", [P, TILES], F32)
        stats = sb("stats", [P, TILES, 6], F32)
        mv = sb("mv", [P, 2, TILES, 2], F32)
        var_e, rstd, m_half = sb("var_e", [P, 2, TILES], F32), sb("rstd", [P, 2, TILES], F32), sb("m_half", [P, TILES], F32)
        lg_sb = sb("lg_sb", [P, T], F32)
        ps = [ctx.enter_context(nc.psum_tensor(f"ps_c{i}", [P, T], F32)) for i in range(8)]

        wo_in, wf_in, wx_in, g_in = sem("wo_in"), sem("wf_in"), sem("wx_in"), sem("g_in")
        w_hi_done, w_lo_done, half_done = sem("cw_hi_done"), sem("cw_lo_done"), sem("half_done")
        full = [sem(f"c_full{i}") for i in range(8)]
        free = [sem(f"c_free{i}") for i in range(8)]
        x_in = [sem(f"x_in{i}") for i in range(2)]
        on_in = [sem(f"on_in{i}") for i in range(2)]
        c_in, c_hi_done, c_lo_done = sem("c_in"), sem("c_hi_done"), sem("c_lo_done")
        qk_hi_done, qk_lo_done = sem("qk_hi_done"), sem("qk_lo_done")
        mx_done, map_done, a_hi_done, a_lo_done, inv_done = (
            sem("mx_done"), sem("map_done"), sem("a_hi_done"), sem("a_lo_done"), sem("inv_done"))
        t_hi_done, t_lo_done = sem("t_hi_done"), sem("t_lo_done")
        stat_done, agg_done, var_done, rstd_done, norm_done = (
            sem("stat_done"), sem("agg_done"), sem("var_done"), sem("rstd_done"), sem("cnorm_done"))
        routing_done, sorted_done = sem("routing_done"), sem("sorted_done")
        x2_stored, base_done, lg_done, logit_done = sem("x2_stored"), sem("base_done"), sem("lg_done"), sem("logit_done")
        block = ctx.enter_context(nc.Block())

        norms = [s[:2] for s in plan if s[0] in ("o_proj", "mix") and s[2] == 0]
        norm_no = {s: n for n, s in enumerate(norms)}
        frees, count = {}, [0] * 8
        for step in plan:
            bank = bank_of[step][0]
            count[bank] += step[0] in ("qx", "kx", "energy", "o_proj", "mix", "logit")
            frees[step] = count[bank]

        @block.sync
        def _(sp):
            sp.dma_start(on_sb[:, 0], o_dram[0].rearrange("(i p) f -> p i f", p=P)).then_inc(on_in[0], 16)
            sp.dma_start(wx_raw[:, 0], wxq_t.rearrange("(k p) n -> p k n", p=P)).then_inc(wx_in, 16)
            sp.dma_start(wx_raw[:, 1], wxk_t.rearrange("(k p) n -> p k n", p=P)).then_inc(wx_in, 16)
            sp.dma_start(bias[:, 0:1], bxq).then_inc(wx_in, 16)
            sp.dma_start(bias[:, 1:2], bxk).then_inc(wx_in, 16)
            sp.dma_start(c_raw[:], ctx_t[0].rearrange("(k p) t -> p k t", p=P)).then_inc(c_in, 16)
            sp.dma_start(x_sb[:, 1], wo_t.rearrange("(k p) n -> p k n", p=P)).then_inc(wo_in, 16)
            sp.dma_start(x_sb[:, 0], x[0].rearrange("(i p) f -> p i f", p=P)).then_inc(x_in[0], 16)
            sp.dma_start(on_sb[:, 1], w_t.rearrange("(k p) n -> p k n", p=P)).then_inc(wf_in, 16)
            sp.dma_start(g_raw[:, :, 0:E], gate_t.rearrange("(k p) e -> p k e", p=P)).then_inc(g_in, 16)
            for step in plan:
                kind, b = step[:2]
                if step == ("mix", 0, 0):
                    sp.wait_ge(w_lo_done, 4)
                    sp.dma_start(on_sb[:, 1], o_dram[1].rearrange("(i p) f -> p i f", p=P)).then_inc(on_in[1], 16)
                    sp.dma_start(x_sb[:, 1], x[1].rearrange("(i p) f -> p i f", p=P)).then_inc(x_in[1], 16)
                if kind == "kx" and b + 1 < B:
                    sp.wait_ge(c_lo_done, b + 1)
                    sp.dma_start(c_raw[:], ctx_t[b + 1].rearrange("(k p) t -> p k t", p=P)).then_inc(c_in, 16)
                if kind == "mix" and step[2] == TILES - 1:
                    sp.wait_ge(norm_done, TILES * (norm_no[("mix", b)] + 1))
                    sp.dma_start(x2_dram[b * T:(b + 1) * T].rearrange("(i p) f -> p i f", p=P), x_sb[:, b % 2]).then_inc(x2_stored, 16)
                if kind == "o_proj" and step[2] == TILES - 1 and b + 2 < B:
                    sp.wait_ge(t_lo_done, KC * (turn_no[("o_t", b)] + 1))
                    sp.dma_start(on_sb[:, b % 2], o_dram[b + 2].rearrange("(i p) f -> p i f", p=P)).then_inc(on_in[b % 2], 16)
                if kind == "x2_w" and step[2] == TILES - 1 and b + 2 < B:
                    sp.wait_ge(base_done, TILES * (b + 1))
                    sp.wait_ge(x2_stored, 16 * (b + 1))
                    sp.dma_start(x_sb[:, b % 2], x[b + 2].rearrange("(i p) f -> p i f", p=P)).then_inc(x_in[b % 2], 16)
            sp.wait_ge(x2_stored, 16 * B)

        @block.gpsimd
        def _(pool):
            pool.memset(g_raw[:, :, E:P], 0.0).then_inc(half_done, 1)
            pool.memset(m_half[:], -0.5).then_inc(half_done, 1)
            pool.wait_ge(half_done, 2)
            pool.iota(g.i8[:], pattern=[[1, E]], base=0, channel_multiplier=0, allow_small_or_imprecise_dtypes=True).then_inc(routing_done, 1)
            pool.iota(g.i128[:], pattern=[[1, P]], base=0, channel_multiplier=0, allow_small_or_imprecise_dtypes=True).then_inc(routing_done, 1)
            pool.iota(g.token[:], pattern=[[P, TT]], base=0, channel_multiplier=1, allow_small_or_imprecise_dtypes=True).then_inc(routing_done, 1)
            pool.memset(g.ones[:], 1.0).then_inc(routing_done, 1)
            pool.memset(g.before[:], 1.0).then_inc(routing_done, 1)
            pool.wait_ge(routing_done, 5)
            pool.affine_select(out=g.before[:], in_=g.before[:], compare_op=ALU.is_ge, fill=0.0, base=-1,
                               pattern=[[1, P]], channel_multiplier=-1).then_inc(routing_done, 1)
            pool.wait_ge(routing_done, 6)
            for step in plan:
                kind, b = step[:2]
                if kind == "qx":
                    pool.wait_ge(c_hi_done, b + 1)
                    pool.tensor_tensor(c_lo[:], c_raw[:], c_hi[:].bitcast(F32), ALU.subtract).then_inc(c_lo_done, 1)
                if kind in ("o_proj", "mix") and step[2] == TILES - 1:
                    n = norm_no[step[:2]]
                    pool.wait_ge(agg_done, TILES * (n + 1))
                    pool.tensor_scalar(var_e[:, n % 2], mv[:, n % 2, :, 1], EPS, None, ALU.add).then_inc(var_done, 1)
                    pool.wait_ge(var_done, n + 1)
                    pool.tensor_tensor(rstd[:, n % 2], var_e[:, n % 2], m_half[:], ALU.pow).then_inc(rstd_done, 1)

        @block.scalar
        def _(act):
            def weights(n, src, hi, loaded, count):
                act.wait_ge(loaded, count)
                act.activation(hi, src, ACT.Copy).then_inc(w_hi_done, 1)

            weights(0, wx_raw[:], wx_hi[:], wx_in, 64)
            act.wait_ge(c_in, 16)
            act.activation(c_hi[:], c_raw[:], ACT.Copy).then_inc(c_hi_done, 1)
            for step in plan:
                kind, b = step[:2]
                bank, nth = bank_of[step]
                if step == ("mix", 0, 0):
                    weights(2, on_sb[:, 1], wf_hi[:], wf_in, 16)
                    act.wait_ge(half_done, 2)
                    weights(3, g_raw[:], g_hi[:], g_in, 16)
                if kind in ("qx", "kx"):
                    n, w = lo_no[step], int(kind == "kx")
                    act.wait_ge(full[bank], nth + 1)
                    if b and not w:
                        eb, en = bank_of[("energy", b - 1, TILES - 1)]
                        act.wait_ge(full[eb], en + 1)
                    act.activation(qk_hi[:, w], ps[bank][:], ACT.Identity, bias=bias[:, w:w + 1]).then_inc(qk_hi_done, 1)
                    if step == ("kx", 0):
                        weights(1, x_sb[:, 1], wo_hi[:], wo_in, 16)
                    if w and b + 1 < B:
                        act.wait_ge(c_in, 16 * (b + 2))
                        act.activation(c_hi[:], c_raw[:], ACT.Copy).then_inc(c_hi_done, 1)
                if kind == "energy":
                    n, i = en_no[step], step[2]
                    act.wait_ge(mx_done, n + 1)
                    if b and i == 0:
                        tb, tn = bank_of[("a_t", b - 1, KC - 1)]
                        act.wait_ge(full[tb], tn + 1)
                    act.activation(e_sb[:, i], ps[bank][:], ACT.Exp, bias=n_mx[:, i:i + 1],
                                   accum_out=a_sum[:, i:i + 1]).then_inc(free[bank], 1)
                if kind == "a_t":
                    act.wait_ge(full[bank], nth + 1)
                    if b >= 2 and step[2] == 0:
                        mb, mn = bank_of[("mix", b - 2, TILES - 1)]
                        act.wait_ge(full[mb], mn + 1)
                    act.activation(a_hi[:, b % 2, step[2]], ps[bank][:], ACT.Copy).then_inc(a_hi_done, 1)
                if kind in ("o_t", "x1_t", "x2_t"):
                    n, k = turn_no[step[:2]], step[2]
                    act.wait_ge(full[bank], nth + 1)
                    if n >= 2 and k == 0:
                        last = {"o_t": ("o_proj", TILES - 1), "x1_t": ("mix", TILES - 1), "x2_t": ("x2_w", TILES - 1)}
                        name, at = last[turns[n - 2][0]]
                        ub, un = bank_of[(name, turns[n - 2][1], at)]
                        act.wait_ge(full[ub], un + 1)
                    act.activation(t_hi[:, n % 2, k], ps[bank][:], ACT.Copy).then_inc(t_hi_done, 1)
                if kind == "logit":
                    act.wait_ge(full[bank], nth + 1)
                    if b:
                        lb, ln = bank_of[("logit_t", b - 1)]
                        act.wait_ge(full[lb], ln + 1)
                    act.activation(lg_sb[:], ps[bank][:], ACT.Copy).then_inc(free[bank], 1)

        @block.vector
        def _(dve):
            def low(src, hi, lo):
                dve.tensor_tensor(lo, src, hi.bitcast(F32), ALU.subtract).then_inc(w_lo_done, 1)

            def scale_map(step):
                n, i = en_no[step], step[2]
                dve.wait_ge(free[bank_of[step][0]], frees[step])
                dve.reciprocal(a_inv[:, i:i + 1], a_sum[:, i:i + 1]).then_inc(inv_done, 1)
                dve.wait_ge(inv_done, n + 1)
                dve.tensor_scalar(e_sb[:, i], e_sb[:, i], a_inv[:, i:i + 1], None, ALU.mult).then_inc(map_done, 1)

            dve.wait_ge(w_hi_done, 1)
            low(wx_raw[:], wx_hi[:], wx_lo[:])
            turned_of = {(k, b): (of, b) for b in range(B) for k, of in (("x1_t", "o_proj"), ("x2_t", "mix"))}
            due = None
            for at, step in enumerate(plan):
                kind, b = step[:2]
                bank, nth = bank_of[step]
                if step == ("energy", 0, 0):
                    dve.wait_ge(w_hi_done, 2)
                    low(x_sb[:, 1], wo_hi[:], wo_lo[:])
                if step == ("mix", 0, 0):
                    dve.wait_ge(w_hi_done, 3)
                    low(on_sb[:, 1], wf_hi[:], wf_lo[:])
                    dve.wait_ge(w_hi_done, 4)
                    low(g_raw[:], g_hi[:], g_lo[:])
                if kind in ("qx", "kx"):
                    n, w = lo_no[step], int(kind == "kx")
                    dve.wait_ge(qk_hi_done, n + 1)
                    dve.scalar_tensor_tensor(out=qk_lo[:, w], in0=ps[bank][:], scalar=bias[:, w:w + 1],
                                             in1=qk_hi[:, w].bitcast(F32), op0=ALU.add, op1=ALU.subtract).then_inc(free[bank], 1)
                if kind == "energy":
                    n, i = en_no[step], step[2]
                    dve.wait_ge(full[bank], nth + 1)
                    dve.tensor_reduce(n_mx[:, i:i + 1], ps[bank][:], AX.X, ALU.max, negate=True).then_inc(mx_done, 1)
                    if i:
                        scale_map(plan[at - 1])
                    if i == TILES - 1:
                        scale_map(step)
                if kind == "a_t":
                    dve.wait_ge(a_hi_done, KC * b + step[2] + 1)
                    dve.tensor_tensor(a_lo[:, b % 2, step[2]], ps[bank][:], a_hi[:, b % 2, step[2]].bitcast(F32),
                                      ALU.subtract).then_inc(a_lo_done, 1)
                if kind in ("o_t", "x1_t", "x2_t"):
                    n, k = turn_no[step[:2]], step[2]
                    dve.wait_ge(t_hi_done, KC * n + k + 1)
                    dve.tensor_tensor(t_lo[:, n % 2, k], ps[bank][:], t_hi[:, n % 2, k].bitcast(F32), ALU.subtract).then_inc(t_lo_done, 1)
                if kind in ("o_proj", "mix"):
                    n, i = norm_no[step[:2]], step[2]
                    tile = x_sb[:, b % 2, i]
                    dve.wait_ge(full[bank], nth + 1)
                    if kind == "o_proj" and i == 0:
                        dve.wait_ge(x_in[b % 2], 16 * (b // 2 + 1))
                    dve.tensor_tensor(tile, ps[bank][:], tile, ALU.add).then_inc(free[bank], 1)
                    dve.wait_ge(free[bank], frees[step])
                    dve.bn_stats(stats[:, i], tile).then_inc(stat_done, 1)
                    dve.wait_ge(stat_done, TILES * n + i + 1)
                    dve.bn_aggr(mv[:, n % 2, i], stats[:, i]).then_inc(agg_done, 1)
                    if i == TILES - 1:
                        waits = plan[at + 1][0] in ("a_t", "o_t", "x1_t", "x2_t") and turned_of.get(plan[at + 1][:2]) != (kind, b)
                        due = (at + KC if waits else at, n, b)
                if due and due[0] == at:
                    _, n, b = due
                    dve.wait_ge(rstd_done, n + 1)
                    for m in range(TILES):
                        dve.tensor_scalar(x_sb[:, b % 2, m], x_sb[:, b % 2, m], mv[:, n % 2, m, 0:1], rstd[:, n % 2, m:m + 1],
                                          ALU.subtract, ALU.mult).then_inc(norm_done, 1)
                    due = None
                if kind == "x2_w":
                    dve.wait_ge(full[bank], nth + 1)
                    dve.tensor_tensor(base[:, TILES * b + step[2]], ps[bank][:], x_sb[:, b % 2, step[2]], ALU.add).then_inc(base_done, 1)
                if kind == "logit_t":
                    dve.wait_ge(full[bank], nth + 1)
                    dve.tensor_scalar(logits[:, TILES * b:TILES * (b + 1)], ps[bank][:].rearrange("p (i m) -> p i m", m=P)[:, :, 0:E],
                                      50.0, -50.0, ALU.min, ALU.max).then_inc(logit_done, 1)
                    dve.wait_ge(logit_done, b + 1)
                    tiles = range(TILES * b, TILES * (b + 1))
                    for i in tiles:
                        dve.max(g.top[:, i], logits[:, i]).then_inc(sorted_done, 1)
                    for i in tiles:
                        dve.wait_ge(sorted_done, i + 1)
                        dve.max_index(g.top_i[:, i], g.top[:, i], logits[:, i])

        @block.tensor
        def _(pe):
            def freed(step):
                kind, b = step[:2]
                if kind == "a_t":
                    pe.wait_ge(a_lo_done, KC * b + step[2] + 1)
                elif kind in ("o_t", "x1_t", "x2_t"):
                    pe.wait_ge(t_lo_done, KC * turn_no[step[:2]] + step[2] + 1)
                elif kind == "x2_w":
                    pe.wait_ge(base_done, TILES * b + step[2] + 1)
                elif kind == "logit_t":
                    pe.wait_ge(logit_done, b + 1)
                else:
                    bank, nth = bank_of[step]
                    pe.wait_ge(free[bank], frees[step])

            for n, step in enumerate(plan):
                kind, b = step[:2]
                bank, nth = bank_of[step]
                out = ps[bank]
                if n >= 8:
                    freed(plan[n - 8])
                three = ((0, 0), (0, 1), (1, 0))
                if kind in ("qx", "kx"):
                    w = int(kind == "kx")
                    pe.wait_ge(w_lo_done, 1)
                    pe.wait_ge(c_hi_done, b + 1)
                    for m, (s, t, k) in enumerate((s, t, k) for t, s in three for k in range(CC)):
                        if (t, k) == (1, 0):
                            pe.wait_ge(c_lo_done, b + 1)
                        mm = pe.matmul(out[:], (wx_hi, wx_lo)[s][:, w, k], (c_hi, c_lo)[t][:, k], start=m == 0, stop=m == 3 * CC - 1)
                if kind == "energy":
                    i = step[2]
                    kb, kn = bank_of[("kx", b)]
                    pe.wait_ge(free[kb], frees[("kx", b)])
                    for m, (s, t) in enumerate(three):
                        mm = pe.matmul(out[:], (qk_hi, qk_lo)[s][:, 0, i * P:(i + 1) * P], (qk_hi, qk_lo)[t][:, 1], start=m == 0, stop=m == 2)
                if kind in ("o_t", "x1_t", "x2_t", "a_t"):
                    k = step[2]
                    if k == 0:
                        if kind == "a_t":
                            pe.wait_ge(map_done, TILES * (b + 1))
                        elif kind == "o_t":
                            pe.wait_ge(on_in[b % 2], 16 * (b // 2 + 1))
                        else:
                            pe.wait_ge(norm_done, TILES * (norm_no[("o_proj" if kind == "x1_t" else "mix", b)] + 1))
                    src = e_sb[:] if kind == "a_t" else (on_sb if kind == "o_t" else x_sb)[:, b % 2]
                    for i in range(TILES):
                        mm = pe.transpose(out[:, i * P:(i + 1) * P], src[:, i, k * P:(k + 1) * P], c.id_f[:])
                if kind in ("o_proj", "mix", "x2_w"):
                    i = step[2]
                    t = turn_no[({"o_proj": "o_t", "mix": "x1_t", "x2_w": "x2_t"}[kind], b)]
                    if i == 0:
                        pe.wait_ge(t_hi_done, KC * (t + 1))
                        pe.wait_ge(w_lo_done, 4 if kind == "x2_w" else 2)
                        if kind == "mix":
                            pe.wait_ge(a_lo_done, KC * (b + 1))
                    right = {"o_proj": (wo_hi, wo_lo), "x2_w": (wf_hi, wf_lo), "mix": (a_hi, a_lo)}[kind]
                    for m, (s, u, k) in enumerate((s, u, k) for s, u in three for k in range(KC)):
                        rhs = right[u][:, b % 2, k] if kind == "mix" else right[u][:, k]
                        if i == 0 and (s, k) == (1, 0):
                            pe.wait_ge(t_lo_done, KC * (t + 1))
                        mm = pe.matmul(out[:], (t_hi, t_lo)[s][:, t % 2, k, i * P:(i + 1) * P], rhs, start=m == 0, stop=m == 3 * KC - 1)
                if kind == "logit":
                    t = turn_no[("x2_t", b)]
                    pe.wait_ge(t_hi_done, KC * (t + 1))
                    pe.wait_ge(w_lo_done, 4)
                    for m, (s, u, k) in enumerate((s, u, k) for u, s in three for k in range(KC)):
                        if (u, k) == (1, 0):
                            pe.wait_ge(t_lo_done, KC * (t + 1))
                        mm = pe.matmul(out[:], (g_hi, g_lo)[s][:, k], (t_hi, t_lo)[u][:, t % 2, k], start=m == 0, stop=m == 3 * KC - 1)
                if kind == "logit_t":
                    lb, _ = bank_of[("logit", b)]
                    pe.wait_ge(free[lb], frees[("logit", b)])
                    for i in range(TILES):
                        mm = pe.transpose(out[:, i * P:(i + 1) * P], lg_sb[:, i * P:(i + 1) * P], c.id_f[:])
                mm.then_inc(full[bank], 1)


def experts(nc, c, g, s_dram, x2_dram, y_dram, base, logits, out):
    with ExitStack() as ctx:
        sb = lambda name, shape, dt: ctx.enter_context(nc.sbuf_tensor(name, shape, dt))
        sem = lambda name: ctx.enter_context(nc.semaphore(name))
        XG, Y = 4, 4
        RAW = 4
        PIECES = 4
        ROWS_S = D // PIECES
        s_raw = sb("s_raw", [P, RAW, ROWS_S * E], F32)
        POOL_PIECES = range(2, PIECES * KC - 2, 3)
        VECTOR_PIECES = [n for n in range(PIECES * KC) if n not in POOL_PIECES]
        s_hi, s_lo = sb("s_hi", [P, KC, E, D], F32R), sb("s_lo", [P, KC, E, D], F32R)
        xg = sb("xg", [P, XG, D], F32)
        l_hi, l_lo = sb("l_hi", [P, 2, D], F32R), sb("l_lo", [P, 2, D], F32R)
        spare = s_raw[:].rearrange("p n d -> p (n d)").rearrange("p (h n d) -> p h n d", h=2, d=D)
        y_sb = spare[:, 1]
        ACC = 2 * Y
        acc = s_raw[:].rearrange("p n d -> p (n d)").rearrange("p (n d) -> p n d", d=D)
        YG = 4
        yg = s_hi[:, 0].bitcast(F32).rearrange("p (i n) d -> p i n d", n=2)
        top, top_i = g.top, g.top_i
        top_f = sb("top_f", [P, TT, 2], F32)
        hot = sb("hot", [P, 2, TT, E], F32)
        sel = sb("sel", [P, TT, E], F32)
        keep = sb("keep", [P, E, TT], F32)
        tot, run = sb("tot", [P, E, TT], F32), sb("run", [P, E, TT], F32)
        rank, prod = sb("rank", [P, TT, E], F32), sb("prod", [P, TT, E], F32)
        tiles_i, tiles_f, ends, starts = sb("tiles_i", [P, E], I32), sb("tiles_f", [P, E], F32), sb("ends", [P, E], F32), sb("starts", [P, E], F32)
        slot_f, slot_i = sb("slot_f", [P, 2, TT], F32), sb("slot_i", [P, 2, TT], I32)
        lane_i, lane, tile_i, tile_f = sb("lane_i", [P, 2, TT], I32), sb("lane", [P, 2, TT], F32), sb("tile_i", [P, 2, TT], I32), sb("tile_f", [P, 2, TT], F32)
        past = sb("past", [P, J, E], F32)
        of_tile, of_tile_i = sb("of_tile", [P, J], F32), sb("of_tile_i", [P, J], I32)
        LIST = 4
        lane_hot = l_lo[:].rearrange("p u (n q) -> p u n q", q=P)
        tile_is, tile_hot = sb("tile_is", [P, LIST, J + 1], F32), sb("tile_hot", [P, 2, LIST, J + 1], F32R)
        pair_token = sb("pair_token", [P, J], I32)
        gap, w_top = sb("gap", [P, TT], F32), sb("w_top", [P, 2, TT], F32)
        stats, mv = sb("stats_f", [P, 2, 6], F32), sb("mv_f", [P, TT, 2], F32)
        var_e, rstd, shift, m_half = sb("var_f", [P, TT], F32), sb("rstd_f", [P, TT], F32), sb("shift", [P, TT], F32), sb("m_half_f", [P, 2], F32)
        ps = [ctx.enter_context(nc.psum_tensor(f"ps_x{i}", [P, T], F32)) for i in range(8)]
        PS_T, PS_Y = ps[0:3], ps[3:6]
        ps_r, ps_k = ps[6], ps[7]

        s_in = [sem(f"s_in{i}") for i in range(RAW)]
        s_hi_done, s_lo_done, s_lo_pool = sem("s_hi_done"), sem("s_lo_done"), sem("s_lo_pool")
        const, top_done, route, count_done, list_ready, list_done = (
            sem("x_const"), sem("top_done"), sem("route"), sem("count_done"), sem("list_ready"), sem("list_done"))
        gap_exp, tokens_ready = sem("gap_exp"), sem("tokens_ready")
        x_gathered = [sem(f"x_gathered{i}") for i in range(XG)]
        t_full, l_hi_done, l_lo_done, y_full, y_copied = (
            sem("t_full"), sem("l_hi_done"), sem("l_lo_done"), sem("y_full"), sem("y_copied"))
        y_stored = [sem(f"y_stored{i}") for i in range(Y)]
        y_gathered = [sem(f"y_gathered{i}") for i in range(YG)]
        added, stat_done, agg_done, var_done, rstd_done, shift_done, fin_done = (
            sem("added"), sem("fstat_done"), sem("fagg_done"), sem("fvar_done"), sem("frstd_done"), sem("shift_done"), sem("fin_done"))
        out_stored = [sem(f"out_stored{i}") for i in range(ACC)]
        block = ctx.enter_context(nc.Block())

        def piece(matrices, n):
            return matrices[:, n // PIECES, :, (n % PIECES) * ROWS_S:(n % PIECES + 1) * ROWS_S]

        def raw(n):
            return s_raw[:, n % RAW].rearrange("p (r e) -> p e r", e=E)

        def low_s(eng, n, done):
            eng.wait_ge(s_hi_done, n + 1)
            eng.tensor_tensor(piece(s_lo, n), raw(n), piece(s_hi, n).bitcast(F32), ALU.subtract).then_inc(done, 1)

        def wait_low_s(eng, n):
            eng.wait_ge(s_lo_done, len([m for m in VECTOR_PIECES if m <= n]))
            if n >= POOL_PIECES[0]:
                eng.wait_ge(s_lo_pool, len([m for m in POOL_PIECES if m <= n]))

        @block.sync
        def _(sp):
            for n in range(PIECES * KC):
                if n >= RAW:
                    wait_low_s(sp, n - RAW)
                rows = s_dram[(n // PIECES) * P * D:(n // PIECES + 1) * P * D].rearrange("(p q r) e -> p q (r e)", p=P, q=PIECES)
                sp.dma_start(s_raw[:, n % RAW], rows[:, n % PIECES]).then_inc(s_in[n % RAW], 16)
            for j in range(J):
                sp.wait_ge(y_copied, j + 1)
                sp.dma_start(y_dram[j * P:(j + 1) * P], y_sb[:, j % Y]).then_inc(y_stored[j % Y], 16)
            for i in range(TT):
                sp.wait_ge(fin_done, i + 1)
                sp.dma_start(out[i * P:(i + 1) * P], acc[:, i % ACC]).then_inc(out_stored[i % ACC], 16)
            for i in range(ACC):
                sp.wait_ge(out_stored[i], 16 * TT // ACC)

        @block.gpsimd
        def _(pool):
            def norm_scale(pool, i):
                pool.wait_ge(var_done, i + 1)
                pool.tensor_tensor(rstd[:, i - 1:i + 1], var_e[:, i - 1:i + 1], m_half[:], ALU.pow).then_inc(rstd_done, 1)

            pool.memset(m_half[:], -0.5).then_inc(const, 1)
            for n in POOL_PIECES:
                low_s(pool, n, s_lo_pool)
            pool.wait_ge(tokens_ready, 1)
            for j in range(J):
                if j >= XG:
                    pool.wait_ge(t_full, j - XG + 1)
                pool.indirect_dma_start(out=xg[:, j % XG], out_offset=None, in_=x2_dram,
                                        in_offset=bass.IndirectOffsetOnAxis(ap=pair_token[:, j:j + 1], axis=0)
                                        ).then_inc(x_gathered[j % XG], 16)
            for i in range(Y):
                pool.wait_ge(y_stored[i], 16 * len(range(i, J, Y)))
            for i in range(TT):
                for n in range(2):
                    if i >= YG:
                        pool.wait_ge(added, 2 * (i - YG) + n + 1)
                    pool.indirect_dma_start(out=yg[:, i % YG, n], out_offset=None, in_=y_dram,
                                            in_offset=bass.IndirectOffsetOnAxis(ap=slot_i[:, n, i:i + 1], axis=0)
                                            ).then_inc(y_gathered[i % YG], 16)
                if i >= 5 and i % 2:
                    norm_scale(pool, i - 4)
            norm_scale(pool, TT - 3)
            norm_scale(pool, TT - 1)

        @block.scalar
        def _(act):
            def copy_y(act, j):
                act.wait_ge(y_full, j + 1)
                if j >= Y:
                    act.wait_ge(y_stored[j % Y], 16 * (j // Y))
                act.activation(y_sb[:, j % Y], PS_Y[j % 3][:], ACT.Copy).then_inc(y_copied, 1)

            for n in range(PIECES * KC):
                act.wait_ge(s_in[n % RAW], 16 * (n // RAW + 1))
                act.activation(piece(s_hi, n), raw(n), ACT.Copy).then_inc(s_hi_done, 1)
                if n == PIECES * KC - 1:
                    act.wait_ge(top_done, 1)
                    act.activation(gap[:], gap[:], ACT.Exp).then_inc(gap_exp, 1)
            for j in range(J):
                act.wait_ge(t_full, j + 1)
                if j >= 2:
                    act.wait_ge(y_full, j - 1)
                act.activation(l_hi[:, j % 2], PS_T[j % 3][:], ACT.Copy).then_inc(l_hi_done, 1)
                if j:
                    copy_y(act, j - 1)
            copy_y(act, J - 1)
            for i in range(TT):
                act.wait_ge(shift_done, i // 2 + 1)
                act.activation(acc[:, i % ACC], acc[:, i % ACC], ACT.Identity, scale=rstd[:, i:i + 1], bias=shift[:, i:i + 1]).then_inc(fin_done, 1)

        @block.vector
        def _(dve):
            def norm_shift(dve, i):
                dve.wait_ge(rstd_done, i // 2 + 1)
                dve.scalar_tensor_tensor(out=shift[:, i - 1:i + 1], in0=mv[:, i - 1:i + 1, 0], scalar=-1.0, in1=rstd[:, i - 1:i + 1],
                                         op0=ALU.mult, op1=ALU.mult).then_inc(shift_done, 1)

            n = [0]

            def link(ins):
                n[0] += 1
                ins.then_inc(route, 1)
                dve.wait_ge(route, n[0])

            pieces = list(VECTOR_PIECES)

            def split_next():
                if pieces:
                    low_s(dve, pieces.pop(0), s_lo_done)

            dve.tensor_tensor(gap[:], top[:, :, 1], top[:, :, 0], ALU.subtract).then_inc(top_done, 1)
            link(dve.tensor_copy(top_f[:], top_i[:, :, 0:2]))
            for m in range(2):
                link(dve.tensor_tensor(hot[:, m], g.i8[:].unsqueeze(1).broadcast_to([P, TT, E]),
                                       top_f[:, :, m].unsqueeze(2).broadcast_to([P, TT, E]), ALU.is_equal))
            link(dve.tensor_tensor(sel[:], hot[:, 0], hot[:, 1], ALU.add))
            dve.sem_inc(list_ready, 1)
            link(dve.memset(keep[:], 1.0))
            link(dve.memset(keep[:, :, 0], 0.0))
            split_next()
            dve.wait_ge(count_done, 1)
            totals = ps_r[:, P:2 * P].rearrange("p (i e) -> p e i", e=E)
            link(dve.tensor_copy(tot[:], totals))
            link(dve.tensor_tensor_scan(run[:].rearrange("p e i -> p (e i)"), keep[:].rearrange("p e i -> p (e i)"),
                                        tot[:].rearrange("p e i -> p (e i)"), 0.0, ALU.mult, ALU.add))
            link(dve.tensor_scalar(tiles_f[:], run[:, :, TT - 1], float(P - 1), None, ALU.add))
            link(dve.tensor_copy(tiles_i[:], tiles_f[:]))
            link(dve.tensor_scalar(tiles_i[:], tiles_i[:], P.bit_length() - 1, None, ALU.logical_shift_right))
            link(dve.tensor_copy(tiles_f[:], tiles_i[:]))
            link(dve.tensor_tensor_scan(ends[:], g.ones[:, 0:E], tiles_f[:], 0.0, ALU.mult, ALU.add))
            link(dve.tensor_tensor(starts[:], ends[:], tiles_f[:], ALU.subtract))
            split_next()
            link(dve.tensor_tensor(run[:], run[:], tot[:], ALU.subtract))
            link(dve.scalar_tensor_tensor(out=run[:], in0=starts[:].unsqueeze(2).broadcast_to([P, E, TT]), scalar=float(P),
                                          in1=run[:], op0=ALU.mult, op1=ALU.add))
            link(dve.tensor_tensor(rank[:], ps_r[:, 0:P].rearrange("p (i e) -> p i e", e=E), run[:].rearrange("p e i -> p i e"), ALU.add))
            for m in range(2):
                link(dve.tensor_tensor(prod[:], rank[:], hot[:, m], ALU.mult))
                link(dve.tensor_reduce(slot_f[:, m], prod[:], AX.X, ALU.add))
            split_next()
            link(dve.tensor_copy(slot_i[:], slot_f[:]))
            link(dve.tensor_scalar(lane_i[:], slot_i[:], P - 1, None, ALU.bitwise_and))
            link(dve.tensor_scalar(tile_i[:], slot_i[:], P.bit_length() - 1, None, ALU.logical_shift_right))
            link(dve.tensor_copy(lane[:], lane_i[:]))
            link(dve.tensor_copy(tile_f[:], tile_i[:]))
            for u in range(2 * TT // LIST):
                m, own = u // (TT // LIST), slice(u * LIST % TT, u * LIST % TT + LIST)
                if u >= 2:
                    dve.wait_ge(list_done, u - 1)
                dve.tensor_tensor(lane_hot[:, u % 2], g.i128[:].unsqueeze(1).broadcast_to([P, LIST, P]),
                                  lane[:, m, own].unsqueeze(2).broadcast_to([P, LIST, P]), ALU.is_equal).then_inc(list_ready, 1)
                link(dve.tensor_tensor(tile_is[:], g.i128[:, 0:J + 1].unsqueeze(1).broadcast_to([P, LIST, J + 1]),
                                       tile_f[:, m, own].unsqueeze(2).broadcast_to([P, LIST, J + 1]), ALU.is_equal))
                dve.tensor_tensor(tile_hot[:, u % 2], tile_is[:], g.token[:, own].unsqueeze(2).broadcast_to([P, LIST, J + 1]),
                                  ALU.mult).then_inc(list_ready, 1)
                dve.wait_ge(list_ready, 2 * u + 3)
                split_next()
            dve.wait_ge(list_done, 2 * TT // LIST)
            dve.tensor_copy(pair_token[:], ps_k[:, 0:J]).then_inc(tokens_ready, 1)
            link(dve.tensor_tensor(past[:], g.i128[:, 0:J].unsqueeze(2).broadcast_to([P, J, E]),
                                   ends[:].unsqueeze(1).broadcast_to([P, J, E]), ALU.is_ge))
            link(dve.tensor_reduce(of_tile[:], past[:], AX.X, ALU.add))
            link(dve.tensor_scalar(of_tile[:], of_tile[:], float(E - 1), None, ALU.min))
            link(dve.tensor_copy(of_tile_i[:], of_tile[:]))
            while pieces:
                split_next()
            dve.wait_ge(gap_exp, 1)
            link(dve.tensor_scalar(w_top[:, 1], gap[:], 1.0, None, ALU.add))
            link(dve.reciprocal(w_top[:, 0], w_top[:, 1]))
            link(dve.tensor_tensor(w_top[:, 1], w_top[:, 0], gap[:], ALU.mult))
            for j in range(J):
                dve.wait_ge(l_hi_done, j + 1)
                dve.tensor_tensor(l_lo[:, j % 2], PS_T[j % 3][:], l_hi[:, j % 2].bitcast(F32), ALU.subtract).then_inc(l_lo_done, 1)
            def add(i, m):
                slot = acc[:, i % ACC]
                if m == 0:
                    dve.wait_ge(y_gathered[i % YG], 2 * 16 * (i // YG + 1))
                if m:
                    dve.wait_ge(added, 2 * i + 1)
                elif i >= ACC:
                    dve.wait_ge(out_stored[i % ACC], 16 * (i // ACC))
                dve.scalar_tensor_tensor(out=slot, in0=yg[:, i % YG, m], scalar=w_top[:, m, i:i + 1], in1=slot if m else base[:, i],
                                         op0=ALU.mult, op1=ALU.add).then_inc(added, 1)

            for i in range(TT + 1):
                if i < TT:
                    add(i, 0)
                if i:
                    dve.wait_ge(added, 2 * i)
                    dve.bn_stats(stats[:, i % 2], acc[:, (i - 1) % ACC]).then_inc(stat_done, 1)
                if i < TT:
                    add(i, 1)
                if i:
                    dve.wait_ge(stat_done, i)
                    dve.bn_aggr(mv[:, i - 1], stats[:, i % 2]).then_inc(agg_done, 1)
                    dve.wait_ge(agg_done, i)
                    dve.tensor_scalar(var_e[:, i - 1:i], mv[:, i - 1, 1:2], EPS, None, ALU.add).then_inc(var_done, 1)
                if i >= 4 and i % 2 == 0:
                    norm_shift(dve, i - 3)
            norm_shift(dve, TT - 1)

        @block.tensor
        def _(pe):
            pe.wait_ge(list_ready, 1)
            flat = sel[:].rearrange("p i e -> p (i e)")
            pe.matmul(ps_r[:, 0:P], g.before[:], flat, start=True, stop=True)
            pe.matmul(ps_r[:, P:2 * P], g.ones[:], flat, start=True, stop=True).then_inc(count_done, 1)
            for u in range(2 * TT // LIST):
                pe.wait_ge(list_ready, 2 * u + 3)
                for n in range(LIST):
                    mm = pe.matmul(ps_k[:, 0:J + 1], lane_hot[:, u % 2, n], tile_hot[:, u % 2, n], start=u == n == 0,
                                   stop=u * LIST + n == 2 * TT - 1)
                mm.then_inc(list_done, 1)

            def turn(j):
                pe.wait_ge(x_gathered[j % XG], 16 * (j // XG + 1))
                if j >= 3:
                    pe.wait_ge(l_lo_done, j - 2)
                for k in range(KC):
                    mm = pe.transpose(PS_T[j % 3][:, k * P:(k + 1) * P], xg[:, j % XG, k * P:(k + 1) * P], c.id_f[:])
                mm.then_inc(t_full, 1)

            turn(0)
            wait_low_s(pe, PIECES * KC - 1)
            for j in range(J):
                if j + 1 < J:
                    turn(j + 1)
                expert = pe.value_load(of_tile_i[0:1, j:j + 1], min_val=0, max_val=E - 1)
                pe.wait_ge(l_lo_done, j + 1)
                if j >= 3:
                    pe.wait_ge(y_copied, j - 2)
                terms = [(s, u, k) for s, u in ((0, 0), (0, 1), (1, 0)) for k in range(KC)]
                for m, (s, u, k) in enumerate(terms):
                    right = (s_hi, s_lo)[u][:, k, bass.ds(expert, 1), :].rearrange("p o n -> p (o n)")
                    mm = pe.matmul(PS_Y[j % 3][:], (l_hi, l_lo)[s][:, j % 2, k * P:(k + 1) * P], right,
                                   start=m == 0, stop=m == len(terms) - 1)
                mm.then_inc(y_full, 1)


def decoder_layer(nc, a, out):
    dram = lambda name, shape, dt: nc.dram_tensor(name, shape, dt, kind="Internal").ap()
    parts_dram = dram("parts_dram", [2, ROUNDS, 3, FR, T], BF16)
    o_dram = dram("o_dram", [B, T, D], F32)
    s_dram = dram("s_dram", [D * D + NS, E], F32)
    x2_dram = dram("x2_dram", [TOK, D], F32)
    y_dram = dram("y_dram", [J * P, D], F32)
    with ExitStack() as ctx:
        c = Common(nc, ctx)
        attention(nc, c, a["x_t"], a["wq_t"], a["wk_t"], a["wv_t"], parts_dram, o_dram,
                  a["idx_row"], a["idx_col"], a["atoms"], a["expert_atom_weights"], a["importance_t"], s_dram)
        g = Routing(nc, ctx)
        base = ctx.enter_context(nc.sbuf_tensor("base", [P, TT, D], F32))
        logits = ctx.enter_context(nc.sbuf_tensor("logits", [P, TT, E], F32))
        cross(nc, c, a["x"], o_dram, a["ctx_t"], a["wxq_t"], a["wxk_t"], a["bxq"], a["bxk"], a["wo_t"], a["w_t"],
              a["gate_t"], x2_dram, base, logits, g)
        experts(nc, c, g, s_dram, x2_dram, y_dram, base, logits, out)


def kernel(x, ctx_1024, L0_attn_Wq, L0_attn_Wk, L0_attn_Wv, L0_attn_Wo, L0_xattn_Wq, L0_xattn_bq, L0_xattn_Wk,
           L0_xattn_bk, L0_ffn_gate_w, L0_ffn_W, L0_ffn_atoms, L0_ffn_expert_atom_weights, L0_ffn_importance,
           L0_ffn_mask_idx):
    import numpy as np
    import concourse.bacc as bacc
    from concourse.bass_utils import run_bass_kernel_spmd

    lay = np.ascontiguousarray
    n = lambda v: np.asarray(v)
    by_element = lambda w: lay(n(w).T.reshape(D, PER_BATCH, HR, DK).transpose(0, 1, 3, 2).reshape(D, D))
    arrays = {
        "x": lay(n(x)), "x_t": lay(n(x).transpose(0, 2, 1)), "ctx_t": lay(n(ctx_1024).transpose(0, 2, 1)),
        "wq_t": by_element(L0_attn_Wq), "wk_t": by_element(L0_attn_Wk), "wv_t": lay(n(L0_attn_Wv).T), "wo_t": lay(n(L0_attn_Wo).T),
        "wxq_t": lay(n(L0_xattn_Wq).T), "wxk_t": lay(n(L0_xattn_Wk).T),
        "bxq": lay(n(L0_xattn_bq).reshape(DX, 1)), "bxk": lay(n(L0_xattn_bk).reshape(DX, 1)),
        "gate_t": lay(n(L0_ffn_gate_w).T), "w_t": lay(n(L0_ffn_W).T), "atoms": lay(n(L0_ffn_atoms)),
        "expert_atom_weights": lay(n(L0_ffn_expert_atom_weights)),
        "importance_t": lay(n(L0_ffn_importance).reshape(E, CHUNKS, P).transpose(2, 1, 0).reshape(P, CHUNKS * E)),
        "idx_row": lay(n(L0_ffn_mask_idx)), "idx_col": lay(n(L0_ffn_mask_idx).reshape(CHUNKS, P).T),
    }
    nc = bacc.Bacc("TRN2", target_bir_lowering=False, num_devices=1)
    a = {k: nc.dram_tensor(f"in_{k}", v.shape, mybir.dt.from_np(v.dtype), kind="ExternalInput").ap() for k, v in arrays.items()}
    out = nc.dram_tensor("out", [TOK, D], F32, kind="ExternalOutput").ap()
    decoder_layer(nc, a, out)
    r = run_bass_kernel_spmd(nc, [{f"in_{k}": v for k, v in arrays.items()}], core_ids=[0])
    return r.results[0]["out"].reshape(B, T, D)
```
